# Optimizing a Trainium2 kernel written in Bass

```python
import numpy as np
import jax
import jax.numpy as jnp

def _softmax(x, axis=-1):
    return jax.nn.softmax(x, axis=axis)
def _gelu(x):
    return jax.nn.gelu(x, approximate=True)
def _silu(x):
    return jax.nn.silu(x)
def _sigmoid(x):
    return jax.nn.sigmoid(x)
def _layernorm(x, axis=-1, eps=1e-5):
    m = jnp.mean(x, axis=axis, keepdims=True)
    v = jnp.var(x, axis=axis, keepdims=True)
    return (x - m) / jnp.sqrt(v + eps)
def _scatter_add(tgt, idx, src, axis=0):
    return tgt.at[idx].add(src)
def _segment_sum(src, seg, n):
    return jax.ops.segment_sum(src, seg, n)

kernel_name = 'mk_metaformer_d1_conv_nchw256_713bdd'

def setup_inputs(seed: int = 0):
    np.random.seed(seed)
    _w = jnp.asarray
    def _rec_inputs():
        import jax
        import jax.numpy as jnp
        _gk = jax.random.key(seed)
        x = -0.0006537 + 1.001 * jax.random.normal(jax.random.fold_in(_gk, 1), (4, 256, 48, 48), jnp.float32)
        return x
    x = _rec_inputs()
    def _L0_conv_setup():
        import jax, jax.numpy as jnp
        import numpy as np
        from jax import lax
        BN_EPS = 1e-05
        DIL = 2
        PAD = 6
        K = 7

        def _attn_kernel(x, w1, b1, w2, b2, bn_gamma, bn_beta, bn_mean, bn_var):
            k = lax.conv_general_dilated(x, w1, window_strides=(1, 1), padding=[(PAD, PAD), (PAD, PAD)], rhs_dilation=(DIL, DIL), dimension_numbers=('NCHW', 'OIHW', 'NCHW'))
            k = jax.nn.relu(k + b1[None, :, None, None])
            k = lax.conv_general_dilated(k, w2, window_strides=(1, 1), padding='VALID', dimension_numbers=('NCHW', 'OIHW', 'NCHW')) + b2[None, :, None, None]
            inv = bn_gamma * lax.rsqrt(bn_var + BN_EPS)
            k = k * inv[None, :, None, None] + (bn_beta - bn_mean * inv)[None, :, None, None]
            k = jax.nn.relu(k)
            return jax.nn.softmax(k, axis=1)
        key = jax.random.key(seed)
        ks = jax.random.split(key, 8)
        B, C, H, W = (4, 256, 48, 48)
        x = jax.random.normal(ks[0], (B, C, H, W), dtype=jnp.float32)
        w1 = jax.random.normal(ks[1], (128, C, 7, 7), dtype=jnp.float32) * 0.02
        b1 = jax.random.normal(ks[2], (128,), dtype=jnp.float32) * 0.02
        w2 = jax.random.normal(ks[3], (49, 128, 1, 1), dtype=jnp.float32) * 0.05
        b2 = jax.random.normal(ks[4], (49,), dtype=jnp.float32) * 0.02
        bn_gamma = jnp.ones((49,), dtype=jnp.float32)
        bn_beta = jnp.zeros((49,), dtype=jnp.float32)
        bn_mean = jnp.zeros((49,), dtype=jnp.float32)
        bn_var = jnp.ones((49,), dtype=jnp.float32)
        return {'x': x, 'w1': w1, 'b1': b1, 'w2': w2, 'b2': b2, 'bn_gamma': bn_gamma, 'bn_beta': bn_beta, 'bn_mean': bn_mean, 'bn_var': bn_var}
    _L0_conv_all = _L0_conv_setup()
    _L0_conv_in = {k: v for k, v in _L0_conv_all.items() if k in ('w1', 'b1', 'w2', 'b2', 'bn_gamma', 'bn_beta', 'bn_mean', 'bn_var', )}
    del _L0_conv_all

    def _L0_ffn_setup():
        import math
        import jax, jax.numpy as jnp
        import numpy as np
        CAPACITY_FACTOR = 1.25
        TOP_K = 2
        LN_EPS = 1e-05

        def _layer_norm(x, gamma, beta):
            mu = jnp.mean(x, axis=-1, keepdims=True)
            var = jnp.var(x, axis=-1, keepdims=True)
            return (x - mu) * jax.lax.rsqrt(var + LN_EPS) * gamma + beta
        key = jax.random.key(seed)
        ks = jax.random.split(key, 4)
        B, S, D, F, E = (8, 4096, 256, 512, 8)
        x = jax.random.normal(ks[0], (B, S, D), dtype=jnp.float32)
        Wr = jax.random.normal(ks[1], (D, E), dtype=jnp.float32) / np.sqrt(D)
        br = jnp.zeros((E,), jnp.float32)
        W1 = jax.random.normal(ks[2], (E, D, F), dtype=jnp.float32) / np.sqrt(D)
        b1 = jnp.zeros((E, F), jnp.float32)
        W2 = jax.random.normal(ks[3], (E, F, D), dtype=jnp.float32) / np.sqrt(F)
        b2 = jnp.zeros((E, D), jnp.float32)
        gamma = jnp.ones((D,), jnp.float32)
        beta = jnp.zeros((D,), jnp.float32)
        return {'x': x, 'Wr': Wr, 'br': br, 'W1': W1, 'b1': b1, 'W2': W2, 'b2': b2, 'gamma': gamma, 'beta': beta}
    _L0_ffn_all = _L0_ffn_setup()
    _L0_ffn_in = {k: v for k, v in _L0_ffn_all.items() if k in ('Wr', 'br', 'W1', 'b1', 'W2', 'b2', 'gamma', 'beta', )}
    del _L0_ffn_all

    return {
        "x": x,
        "L0_conv_w1": _L0_conv_in["w1"],
        "L0_conv_b1": _L0_conv_in["b1"],
        "L0_conv_w2": _L0_conv_in["w2"],
        "L0_conv_b2": _L0_conv_in["b2"],
        "L0_conv_bn_gamma": _L0_conv_in["bn_gamma"],
        "L0_conv_bn_beta": _L0_conv_in["bn_beta"],
        "L0_conv_bn_mean": _L0_conv_in["bn_mean"],
        "L0_conv_bn_var": _L0_conv_in["bn_var"],
        "L0_ffn_Wr": _L0_ffn_in["Wr"],
        "L0_ffn_br": _L0_ffn_in["br"],
        "L0_ffn_W1": _L0_ffn_in["W1"],
        "L0_ffn_b1": _L0_ffn_in["b1"],
        "L0_ffn_W2": _L0_ffn_in["W2"],
        "L0_ffn_b2": _L0_ffn_in["b2"],
        "L0_ffn_gamma": _L0_ffn_in["gamma"],
        "L0_ffn_beta": _L0_ffn_in["beta"],
    }

def reference(x, L0_conv_w1, L0_conv_b1, L0_conv_w2, L0_conv_b2, L0_conv_bn_gamma, L0_conv_bn_beta, L0_conv_bn_mean, L0_conv_bn_var, L0_ffn_Wr, L0_ffn_br, L0_ffn_W1, L0_ffn_b1, L0_ffn_W2, L0_ffn_b2, L0_ffn_gamma, L0_ffn_beta):
    import jax
    import jax.numpy as jnp
    def _L0_conv_ref(x, w1, b1, w2, b2, bn_gamma, bn_beta, bn_mean, bn_var):
        import jax, jax.numpy as jnp
        import numpy as np
        from jax import lax
        BN_EPS = 1e-05
        DIL = 2
        PAD = 6
        K = 7

        def _attn_kernel(x, w1, b1, w2, b2, bn_gamma, bn_beta, bn_mean, bn_var):
            k = lax.conv_general_dilated(x, w1, window_strides=(1, 1), padding=[(PAD, PAD), (PAD, PAD)], rhs_dilation=(DIL, DIL), dimension_numbers=('NCHW', 'OIHW', 'NCHW'))
            k = jax.nn.relu(k + b1[None, :, None, None])
            k = lax.conv_general_dilated(k, w2, window_strides=(1, 1), padding='VALID', dimension_numbers=('NCHW', 'OIHW', 'NCHW')) + b2[None, :, None, None]
            inv = bn_gamma * lax.rsqrt(bn_var + BN_EPS)
            k = k * inv[None, :, None, None] + (bn_beta - bn_mean * inv)[None, :, None, None]
            k = jax.nn.relu(k)
            return jax.nn.softmax(k, axis=1)
        B, C, H, W = x.shape
        attn = _attn_kernel(x, w1, b1, w2, b2, bn_gamma, bn_beta, bn_mean, bn_var)
        xp = jnp.pad(x, ((0, 0), (0, 0), (PAD, PAD), (PAD, PAD)))
        out = jnp.zeros_like(x)
        for p in range(K * K):
            ki, kj = divmod(p, K)
            oi, oj = (ki * DIL, kj * DIL)
            patch = xp[:, :, oi:oi + H, oj:oj + W]
            out = out + patch * attn[:, p][:, None, :, :]
        return out

    def _L0_ffn_ref(x, Wr, br, W1, b1, W2, b2, gamma, beta):
        import math
        import jax, jax.numpy as jnp
        import numpy as np
        CAPACITY_FACTOR = 1.25
        TOP_K = 2
        LN_EPS = 1e-05

        def _layer_norm(x, gamma, beta):
            mu = jnp.mean(x, axis=-1, keepdims=True)
            var = jnp.var(x, axis=-1, keepdims=True)
            return (x - mu) * jax.lax.rsqrt(var + LN_EPS) * gamma + beta
        B, S, D = x.shape
        E = Wr.shape[1]
        N = B * S
        K = TOP_K
        logits = jnp.mean(x, axis=1) @ Wr + br
        routing_weights = jax.nn.softmax(logits, axis=-1)
        capacity = float(math.ceil(N * CAPACITY_FACTOR / E))
        expected_loads = routing_weights.sum(axis=0) * (N / B)
        scale = jnp.where(expected_loads > capacity, capacity / expected_loads, 1.0)
        routing_weights = jax.nn.softmax(routing_weights * scale, axis=-1)
        rw_tok = jnp.broadcast_to(routing_weights[:, None, :], (B, S, E)).reshape(N, E)
        top_w, top_i = jax.lax.top_k(rw_tok, K)
        top_w = jax.nn.softmax(top_w, axis=-1)
        xf = x.reshape(N, D)
        h = jax.nn.gelu(jnp.einsum('nd,edf->enf', xf, W1) + b1[:, None, :], approximate=False)
        y = jnp.einsum('enf,efd->end', h, W2) + b2[:, None, :]
        w_dense = jnp.zeros((N, E), x.dtype).at[jnp.arange(N)[:, None], top_i].add(top_w)
        out = jnp.einsum('ne,end->nd', w_dense, y).reshape(B, S, D)
        out = _layer_norm(out + x, gamma, beta)
        return out

    def _gn(v, G=32, eps=1e-5):
        B_, C_, H_, W_ = v.shape
        g = v.reshape(B_, G, C_ // G, H_, W_)
        m = jnp.mean(g, axis=(2, 3, 4), keepdims=True)
        s = jnp.var(g, axis=(2, 3, 4), keepdims=True)
        return ((g - m) / jnp.sqrt(s + eps)).reshape(v.shape)

    def _ln_c(v, eps=1e-6):
        m = jnp.mean(v, axis=1, keepdims=True)
        s = jnp.var(v, axis=1, keepdims=True)
        return (v - m) / jnp.sqrt(s + eps)

    def _ln_t(v, eps=1e-5):
        m = jnp.mean(v, axis=-1, keepdims=True)
        s = jnp.var(v, axis=-1, keepdims=True)
        return (v - m) / jnp.sqrt(s + eps)

    def _to_tokens(v):
        B_, C_, H_, W_ = v.shape
        return v.reshape(B_, C_, H_ * W_).transpose(0, 2, 1)
    def _from_tokens(t, like):
        B_, C_, H_, W_ = like.shape
        return t.transpose(0, 2, 1).reshape(B_, C_, H_, W_)

    x = x + _L0_conv_ref(_ln_c(x), L0_conv_w1, L0_conv_b1, L0_conv_w2, L0_conv_b2, L0_conv_bn_gamma, L0_conv_bn_beta, L0_conv_bn_mean, L0_conv_bn_var)
    t = _to_tokens(x)
    t = t + _L0_ffn_ref(_ln_t(t), L0_ffn_Wr, L0_ffn_br, L0_ffn_W1, L0_ffn_b1, L0_ffn_W2, L0_ffn_b2, L0_ffn_gamma, L0_ffn_beta)
    x = _from_tokens(t, x)
    return x


_drawn_inputs = setup_inputs


def setup_inputs(seed=0):
    import zlib

    import numpy as np

    out = dict(_drawn_inputs(seed))
    spreads = {'L0_conv_bn_gamma': (1.0, 0.2),
     'L0_conv_bn_beta': (0.0, 0.564),
     'L0_conv_bn_mean': (0.0, 0.768),
     'L0_conv_bn_var': (1.0, 0.6),
     'L0_ffn_br': (0.0, 0.1),
     'L0_ffn_b1': (0.0, 0.377),
     'L0_ffn_b2': (0.0, 0.1),
     'L0_ffn_gamma': (1.0, 0.2),
     'L0_ffn_beta': (0.0, 0.1)}
    factors = {'L0_conv_b1': 23.538, 'L0_conv_b2': 8.0, 'L0_ffn_Wr': 8.0}
    for name, (base, spread) in spreads.items():
        noise = np.random.default_rng([zlib.crc32(name.encode()), seed]).standard_normal(out[name].shape)
        drawn = base * np.exp(spread * noise) if base else spread * noise
        out[name] = jnp.asarray(drawn.astype(out[name].dtype))
    for name, factor in factors.items():
        out[name] = (out[name] * factor).astype(out[name].dtype)
    return out
```

```python
from contextlib import ExitStack

import concourse.bass as bass
from concourse import mybir
from concourse.bass import ds

ALU = mybir.AluOpType
ACT = mybir.ActivationFunctionType
F32 = mybir.dt.float32
F32R = mybir.dt.float32r
F16 = mybir.dt.float16
U32 = mybir.dt.uint32
I32 = mybir.dt.int32
AX = mybir.AxisListType

P = 128
B, C, HH, WW = 4, 256, 48, 48
KS = 7
TAPS = KS * KS
SIDE = HH // 2
IMGS = B * 4
PIX = SIDE * SIDE
N = IMGS * PIX
SB = N // B
CC = C // P
CMID = 128
TR = 4
TT = TR * SIDE
NT = SIDE // TR
PAIRS = IMGS // 2

POINTS = [1.0, -1.0, 2.0, -2.0, 0.0, -0.5]
NP = len(POINTS) + 1
UNITS = 2 * NP - 1
QT = SIDE // 4
VT = QT + 1
CW = 32
HALF = 2 * SIDE * QT
ATT_SCALE = 1024.0
EPAD = 66

LN_STEPS = 3 * NT + 1
LN_VE = 2 * NT + 1
V_STEPS = 13
V_READ, V_DATA = 2, 12
U_STEPS = 15
U_READ, U_DATA = 13, 14
Y_STEPS = 14
SM_STEPS = 14
BN_STEPS = 5


def point_norm(k):
    if k == NP - 1:
        return 1.0
    d = 1.0
    for j, b in enumerate(POINTS):
        if j != k:
            d *= POINTS[k] - b
    return 1.0 / d


class Steps:

    def __init__(self, eng, sem, run, per, first=0):
        self.eng, self.sem, self.base, self.n = eng, sem, run * per, first

    def did(self, ins):
        self.n += 1
        ins.then_inc(self.sem, 1)

    def settle(self):
        after(self.eng, self.sem, self.base + self.n)

    def at(self, n):
        assert self.n == n, (self.n, n)


def after(eng, sem, value):
    if isinstance(value, int) and value <= 0:
        return
    eng.wait_ge(sem, value)


def carry(nc, spare):
    nc.vector.memset(spare, 0.0)


def is_first(q):
    return isinstance(q, int) and q == 0


def conv_phase(nc, xt, w1p, b1, w2, b2, bn_gamma, bn_beta, bn_mean, bn_var, ident_d, xn_d, attn_d):
    PIECES = CC * KS
    with ExitStack() as ctx:
        def sb(name, shape, dt):
            return ctx.enter_context(nc.sbuf_tensor(name, shape, dt))

        def ps(name, shape):
            return ctx.enter_context(nc.psum_tensor(name, shape, F32))

        def sem(name):
            return ctx.enter_context(nc.semaphore(name))

        U = sb("U", [P, 2, UNITS, PIECES, CMID], F16)
        VR = SIDE + KS - 1
        V = sb("V", [P, 2, 2, NP, CC, 2, VR * VT], F16)
        ch = sb("ch", [P, 2, CC, SIDE, CW], F32)
        xa = sb("xa", [TT, 2, NT, C], F32)
        ydata = sb("ydata", [P, 4 * HALF], F32)
        k1 = sb("k1", [P, 4 * HALF], F32)
        WORK = SIDE * (CW + 28 + 14 + 14 + NP * VT)
        work = sb("work", [P, WORK], F32)
        msb = sb("msb", [P, 2, HALF], F32)
        sd = sb("sd", [P, 4, HALF], F32)
        E = sb("E", [TT, 2, NT * TAPS + EPAD - TAPS], F32)
        spare = sb("spare", [1, 1], F32)
        aTs = sb("aTs", [TAPS, 2, 2, PIX], F16)
        ident = sb("ident", [P, P], F32)
        wst = [ydata, k1]
        st = sb("st", [TT, 2, NT, 6], F32)
        mv = sb("mv", [TT, 2, NT, 2], F32)
        ve = sb("ve", [TT, 2, NT], F32)
        rstd = sb("rstd", [TT, 2, NT], F32)
        mhalf = sb("mhalf", [TT, NT], F32)
        mx = sb("mx", [TT, 2, NT], F32)
        sm = sb("sm", [TT, 2, NT], F32)
        w2s = sb("w2s", [TAPS, CMID], F32)
        w2T = sb("w2T", [CMID, TAPS], F32)
        bnp = sb("bnp", [TAPS, 8], F32)
        brow = sb("brow", [1, NT, TAPS], F32)
        ones = sb("ones", [1, TT], F32)
        b1s = sb("b1s", [CMID, 1], F32)
        mxp = sb("mxp", [P, PIECES], F32)
        sg = sb("sg", [P, 6], F32)
        usc = sb("usc", [P, UNITS], F32)

        pM = ps("pM", [P, 4, 512])
        pX = ps("pX", [P, 2, 512])
        pL = ps("pL", [P, 512])
        pA = ps("pA", [P, 512])

        par_loaded = sem("par_loaded")
        pads_zeroed = sem("pads_zeroed")
        usc_set = sem("usc_set")
        w_seen = sem("w_seen")
        wmax_ready = sem("wmax_ready")
        wmax_all = sem("wmax_all")
        sig_step = sem("sig_step")
        u_step = sem("u_step")
        uhi_ready = sem("uhi_ready")
        bn_step = sem("bn_step")
        bn_rstd = sem("bn_rstd")
        w2_turned = sem("w2_turned")
        w2_ready = sem("w2_ready")
        ln_step = sem("ln_step")
        rstd_ready = sem("rstd_ready")
        xT_ready = sem("xT_ready")
        xT_used = sem("xT_used")
        v_step = sem("v_step")
        vhi_ready = sem("vhi_ready")
        m_ready = sem("m_ready")
        m_copied = sem("m_copied")
        y_step = sem("y_step")
        k1_ready = sem("k1_ready")
        logits_ready = sem("logits_ready")
        sm_step = sem("sm_step")
        exp_ready = sem("exp_ready")
        aT_ready = sem("aT_ready")
        ahi_ready = sem("ahi_ready")
        alo_ready = sem("alo_ready")
        w_loaded = [sem(f"w_loaded{s}") for s in range(2)]
        x_loaded = [sem(f"x_loaded{i}") for i in range(2)]
        xn_stored = [sem(f"xn_stored{i}") for i in range(2)]
        at_stored = [sem(f"at_stored{i}") for i in range(2)]

        def pair_loop(eng, body):
            body(0, 0)
            with eng.Fori(0, PAIRS // 2 - 1) as j:
                body(2 * j + 1, 1)
                body(2 * j + 2, 0)
            body(PAIRS - 1, 1)

        def is_last(q):
            return isinstance(q, int) and q == PAIRS - 1

        def utile(w):
            return w[:, 0:UNITS * CMID].rearrange("p (u n) -> p u n", u=UNITS)

        def vtile(w):
            o = SIDE * (CW + 28 + 14 + 14)
            return w[:, o:o + NP * SIDE * VT].rearrange("p (k n) -> p k n", k=NP)

        block = ctx.enter_context(nc.Block())

        @block.sync
        def _(sp):
            sp.dma_start(w2s[:, :], w2).then_inc(par_loaded, 16)
            for k, v in enumerate((b2, bn_gamma, bn_beta, bn_mean, bn_var)):
                sp.dma_start(bnp[:, k:k + 1], v).then_inc(par_loaded, 16)
            sp.dma_start(b1s[:, :], b1).then_inc(par_loaded, 16)
            sp.dma_start(ident[:, :], ident_d).then_inc(par_loaded, 16)

            for i in range(2):
                sp.sem_inc(at_stored[i], 16)

            def load_x(q, i):
                if not is_first(q):
                    sp.wait_ge(xn_stored[i], 16 * q)
                    sp.wait_ge(xT_ready, 8 * q - 4 + 4 * i)
                src = xt[ds((2 * q + i) * PIX, PIX), :].rearrange("(t p) c -> p t c", p=TT)
                sp.dma_start(xa[:, i, :, :], src).then_inc(x_loaded[i], 16)

            def store_xn(q, i):
                sp.wait_ge(ln_step, (2 * q + i + 1) * LN_STEPS)
                dst = xn_d[ds((2 * q + i) * PIX, PIX), :].rearrange("(t p) c -> p t c", p=TT)
                sp.dma_start(dst, xa[:, i, :, :]).then_inc(xn_stored[i], 16)

            def store_attn(q, i):
                sp.wait_ge(alo_ready, 4 * q + 2 * i + 2)
                sp.dma_start(attn_d[:, :, ds((2 * q + i) * PIX, PIX)],
                             aTs[:, i, :, :]).then_inc(at_stored[i], 16)

            load_x(0, 0)
            load_x(0, 1)
            def load_w(k, s):
                sp.dma_start(wst[s][:, 0:KS * CMID],
                             w1p[ds(k, 1), :, :].rearrange("a p n -> (a p) n")).then_inc(w_loaded[s], 16)

            load_w(0, 0)
            load_w(1, 1)
            with sp.Fori(1, PIECES // 2) as j:
                for s in range(2):
                    sp.wait_ge(w_seen, 2 * j + s - 1)
                    load_w(2 * j + s, s)
            for s in range(2):
                sp.wait_ge(w_seen, PIECES - 1 + s)
                load_w(s, s)
            with sp.Fori(1, PIECES // 2) as j:
                for s in range(2):
                    sp.wait_ge(u_step, (2 * j + s - 2) * U_STEPS + U_READ)
                    load_w(2 * j + s, s)

            def body(q):
                if is_first(q):
                    for i in range(2):
                        store_xn(0, i)
                    for i in range(2):
                        load_x(1, i)
                if not is_last(q):
                    for i in range(2):
                        store_xn(q + 1, i)
                    if not (isinstance(q, int) and q >= PAIRS - 2):
                        for i in range(2):
                            load_x(q + 2, i)
                if not is_first(q):
                    for i in range(2):
                        store_attn(q - 1, i)

            body(0)
            with sp.Fori(1, PAIRS - 2) as q:
                body(q)
            body(PAIRS - 2)
            body(PAIRS - 1)
            for i in range(2):
                store_attn(PAIRS - 1, i)
            for i in range(2):
                sp.wait_ge(xn_stored[i], 16 * PAIRS)
                sp.wait_ge(at_stored[i], 16 * (PAIRS + 1))

        @block.gpsimd
        def _(pool):
            for par in range(2):
                for part in range(2):
                    v = V[:, par, part].rearrange("p k c i n -> p (k c i) n")
                    nc.gpsimd.memset(v[:, :, 0:3 * VT], 0.0).then_inc(pads_zeroed, 1)
                    nc.gpsimd.memset(v[:, :, (VR - 3) * VT:VR * VT], 0.0).then_inc(pads_zeroed, 1)
            c = ch[:, :, :, :, :].rearrange("p i c r w -> p (i c r) w")
            nc.gpsimd.memset(c[:, :, 0:3], 0.0).then_inc(pads_zeroed, 1)
            nc.gpsimd.memset(c[:, :, 3 + SIDE:CW], 0.0).then_inc(pads_zeroed, 1)
            nc.gpsimd.memset(mhalf[:, :], -0.5).then_inc(pads_zeroed, 1)
            nc.gpsimd.memset(ones[:, :], 1.0).then_inc(pads_zeroed, 1)
            nc.gpsimd.memset(E[:, :, NT * TAPS:], 0.0).then_inc(pads_zeroed, 1)
            for s in range(2):
                nc.gpsimd.memset(wst[s][:, KS * CMID:(KS + 1) * CMID], 0.0).then_inc(pads_zeroed, 1)
            for k in range(NP):
                nc.gpsimd.memset(usc[:, 2 * k:min(2 * k + 2, UNITS)], point_norm(k)).then_inc(usc_set, 1)
            pool.wait_ge(pads_zeroed, 15)
            pool.wait_ge(bn_step, 1)
            nc.gpsimd.tensor_tensor(bnp[:, 6:7], bnp[:, 5:6], mhalf[0:TAPS, 0:1], ALU.pow).then_inc(bn_rstd, 1)

            def rsqrt(q, i):
                pool.wait_ge(ln_step, (2 * q + i) * LN_STEPS + LN_VE)
                nc.gpsimd.tensor_tensor(rstd[:, i, :], ve[:, i, :], mhalf[:, :], ALU.pow).then_inc(rstd_ready, 1)

            rsqrt(0, 0)
            rsqrt(0, 1)
            pool.wait_ge(wmax_ready, 1)
            nc.gpsimd.partition_all_reduce(sg[:, 1:2], sg[:, 0:1], P,
                                           bass.bass_isa.ReduceOp.max).then_inc(wmax_all, 1)
            with pool.Fori(1, PAIRS) as q:
                rsqrt(q, 0)
                rsqrt(q, 1)

        @block.scalar
        def _(act):
            act.wait_ge(pads_zeroed, 15)
            act.wait_ge(par_loaded, 16 * 8)
            act.wait_ge(w2_turned, 2)
            nc.scalar.copy(w2T[:, :], pL[:, 0:TAPS]).then_inc(w2_ready, 1)
            nc.scalar.copy(brow[:, :, :], pL[0:1, None, P:P + TAPS].broadcast_to([1, NT, TAPS])
                           ).then_inc(w2_ready, 1)

            def plain(q, i):
                for c in range(CC):
                    for h in range(2):
                        u = 8 * q + 4 * i + 2 * c + h
                        act.wait_ge(xT_ready, u + 1)
                        if not is_first(q):
                            act.wait_ge(v_step, (4 * q - 4 + 2 * i + c) * V_STEPS + V_READ)
                        nc.scalar.copy(
                            ch[:, i, c, h * (SIDE // 2):(h + 1) * (SIDE // 2), 3:3 + SIDE],
                            pX[:, h, 0:3 * TT].rearrange("p (r w) -> p r w", w=SIDE)
                        ).then_inc(xT_used, 1)

            def v_high(q, par, i):
                for c in range(CC):
                    act.wait_ge(v_step, (4 * q + 2 * i + c) * V_STEPS + V_DATA)
                    if not (isinstance(q, int) and q < 2):
                        act.wait_ge(m_ready, NP * (q - 1))
                    nc.scalar.copy(V[:, par, 0, :, c, i, 3 * VT:(3 + SIDE) * VT], vtile(work)
                                   ).then_inc(vhi_ready, 1)

            def copy_m(q, k):
                act.wait_ge(m_ready, NP * q + 2 * k + 1)
                if not is_first(q):
                    act.wait_ge(y_step, (q - 1) * Y_STEPS + 2 * k + 2)
                nc.scalar.copy(msb[:, k, :], pM[:, 2 * k, 0:HALF]).then_inc(m_copied, 1)

            def relu(q):
                act.wait_ge(y_step, (q + 1) * Y_STEPS)
                after(act, logits_ready, 2 * q)
                for r in range(4):
                    ins = nc.scalar.activation(k1[:, :].rearrange("p (n r) -> p r n", r=4)[:, r, :],
                                               ydata[:, r * HALF:(r + 1) * HALF], ACT.Relu,
                                               bias=b1s[:, 0:1], scale=sg[:, 4:5])
                ins.then_inc(k1_ready, 1)

            def exp(q, i):
                act.wait_ge(sm_step, q * SM_STEPS + 3 * i + 3)
                nc.scalar.activation(E[:, i, 0:NT * TAPS], E[:, i, 0:NT * TAPS], ACT.Exp).then_inc(exp_ready, 1)

            def a_high(q, i):
                for h in range(2):
                    act.wait_ge(aT_ready, 4 * q + 2 * i + h + 1)
                    act.wait_ge(at_stored[i], 16 * (q + 1))
                    nc.scalar.copy(aTs[:, i, 0, h * 3 * TT:(h + 1) * 3 * TT],
                                   pA[0:TAPS, 0:3 * TT]).then_inc(ahi_ready, 1)

            plain(0, 0)
            v_high(0, 0, 0)
            plain(0, 1)
            v_high(0, 0, 1)
            with act.Fori(0, PIECES) as k:
                act.wait_ge(u_step, k * U_STEPS + U_DATA)
                nc.scalar.copy(U[:, 0, :, ds(k, 1), :].rearrange("p u a n -> p u (a n)"),
                               utile(work)).then_inc(uhi_ready, 1)

            def body(q, par):
                if not is_last(q):
                    plain(q + 1, 0)
                copy_m(q, 0)
                if not is_last(q):
                    v_high(q + 1, 1 - par, 0)
                    plain(q + 1, 1)
                copy_m(q, 1)
                if not is_first(q):
                    exp(q - 1, 0)
                    exp(q - 1, 1)
                if not is_last(q):
                    v_high(q + 1, 1 - par, 1)
                if not is_first(q):
                    a_high(q - 1, 0)
                    a_high(q - 1, 1)
                relu(q)

            pair_loop(act, body)
            for i in range(2):
                exp(PAIRS - 1, i)
            for i in range(2):
                a_high(PAIRS - 1, i)

        @block.vector
        def _(dve):
            tt, stt = nc.vector.tensor_tensor, nc.vector.scalar_tensor_tensor
            Et = E[:, :, 0:NT * TAPS].rearrange("p i (t k) -> p i t k", k=TAPS)

            def ln(q, i):
                s = Steps(dve, ln_step, 2 * q + i, LN_STEPS)
                dve.wait_ge(x_loaded[i], 16 * (q + 1))
                for t in range(NT):
                    s.did(nc.vector.bn_stats(st[:, i, t, :], xa[:, i, t, :]))
                s.settle()
                carry(nc, spare[0:1, 0:1])
                for t in range(NT):
                    s.did(nc.vector.bn_aggr(mv[:, i, t, :], st[:, i, t, :]))
                s.settle()
                s.did(nc.vector.tensor_scalar(ve[:, i, :], mv[:, i, :, 1], 1e-6, None, ALU.add))
                s.at(LN_VE)
                dve.wait_ge(rstd_ready, 2 * q + i + 1)
                for t in range(NT):
                    s.did(nc.vector.tensor_scalar(xa[:, i, t, :], xa[:, i, t, :], mv[:, i, t, 0:1],
                                                  rstd[:, i, t:t + 1], ALU.subtract, ALU.mult))
                s.at(LN_STEPS)

            def v_transform(q, par, i):
                o = 0
                E1 = work[:, 0:SIDE * CW].rearrange("p (r w) -> p r w", w=CW)
                o += SIDE * CW
                S = work[:, o:o + SIDE * 28].rearrange("p (r w) -> p r w", w=28)
                o += SIDE * 28
                Ux = work[:, o:o + SIDE * 14].rearrange("p (w r t) -> p w r t", r=SIDE, w=2)
                o += SIDE * 14
                Sd = work[:, o:o + SIDE * 14].rearrange("p (r t w) -> p r t w", r=SIDE, w=2)
                T = vtile(work).rearrange("p k (r t) -> p k r t", t=VT)
                S4 = S.rearrange("p r (t w) -> p r t w", w=4)
                E4 = E1.rearrange("p r (t w) -> p r t w", w=4)
                for c in range(CC):
                    r = 4 * q + 2 * i + c
                    s = Steps(dve, v_step, r, V_STEPS)
                    D = ch[:, i, c, :, :]
                    D2 = D.rearrange("p r (t w) -> p r t w", w=2)
                    dve.wait_ge(xT_used, 8 * q + 4 * i + 2 * c + 2)
                    s.did(stt(E1[:, :, 0:30], D[:, :, 0:30], 0.5, D[:, :, 1:31], ALU.mult, ALU.add))
                    s.did(stt(Sd.rearrange("p r t w -> p r (t w)"), D2[:, :, 0:14, 1], -4.0,
                              D2[:, :, 1:15, 1], ALU.mult, ALU.add))
                    s.at(V_READ)
                    s.settle()
                    s.did(stt(S, E1[:, :, 0:28], -4.0, E1[:, :, 2:30], ALU.mult, ALU.add))
                    s.did(tt(Ux[:, 0], E4[:, :, 0:VT, 3], E4[:, :, 0:VT, 1], ALU.subtract))
                    s.did(tt(Ux[:, 1], E4[:, :, 1:VT + 1, 0], E4[:, :, 0:VT, 2], ALU.subtract))
                    s.settle()
                    s.did(tt(T[:, 0], S4[:, :, :, 2], S4[:, :, :, 1], ALU.add))
                    s.did(tt(T[:, 1], S4[:, :, :, 2], S4[:, :, :, 1], ALU.subtract))
                    s.did(stt(T[:, 2], Ux[:, 0], 2.0, Ux[:, 1], ALU.mult, ALU.add))
                    s.did(stt(T[:, 3], Ux[:, 0], -2.0, Ux[:, 1], ALU.mult, ALU.add))
                    s.did(tt(T[:, 4], S4[:, :, :, 2], S4[:, :, :, 0], ALU.subtract))
                    s.did(tt(T[:, 5], Sd[:, :, :, 1], Sd[:, :, :, 0], ALU.subtract))
                    s.did(tt(T[:, 6], S4[:, :, :, 3], S4[:, :, :, 1], ALU.subtract))
                    s.at(V_DATA)
                    s.settle()
                    dve.wait_ge(vhi_ready, r + 1)
                    rows = slice(3 * VT, (3 + SIDE) * VT)
                    s.did(tt(V[:, par, 1, :, c, i, rows], vtile(work), V[:, par, 0, :, c, i, rows],
                             ALU.subtract))
                    s.at(V_STEPS)
                    s.settle()

            y = [ydata[:, r * HALF:(r + 1) * HALF] for r in range(4)]

            def y_points(q, k):
                s = Steps(dve, y_step, q, Y_STEPS, 2 * k)
                dve.wait_ge(m_copied, 2 * q + k + 1)
                dve.wait_ge(m_ready, NP * q + 2 * k + 2)
                m = pM[:, 2 * k + 1, 0:HALF]
                s.did(tt(sd[:, 2 * k, :], msb[:, k, :], m, ALU.add))
                s.did(tt(sd[:, 2 * k + 1, :], msb[:, k, :], m, ALU.subtract))

            def y_mid(q):
                s = Steps(dve, y_step, q, Y_STEPS, 4)
                s.settle()
                after(dve, k1_ready, q)
                s.did(tt(y[0], sd[:, 0, :], sd[:, 2, :], ALU.add))
                s.did(stt(y[1], sd[:, 3, :], 2.0, sd[:, 1, :], ALU.mult, ALU.add))
                s.did(stt(y[2], sd[:, 2, :], 4.0, sd[:, 0, :], ALU.mult, ALU.add))
                s.did(stt(y[3], sd[:, 3, :], 8.0, sd[:, 1, :], ALU.mult, ALU.add))
                s.settle()
                dve.wait_ge(m_ready, NP * q + 5)
                s.did(tt(y[0], pM[:, 0, 0:HALF], y[0], ALU.add))

            def y_end(q):
                s = Steps(dve, y_step, q, Y_STEPS, 9)
                s.settle()
                dve.wait_ge(m_ready, NP * q + 6)
                for r in range(4):
                    s.did(stt(y[r], pM[:, 1, 0:HALF], (-0.5) ** r, y[r], ALU.mult, ALU.add))
                s.settle()
                dve.wait_ge(m_ready, NP * q + 7)
                s.did(tt(y[3], pM[:, 2, 0:HALF], y[3], ALU.add))
                s.at(Y_STEPS)

            def shift_logits(q, i):
                s = Steps(dve, sm_step, q, SM_STEPS, 3 * i)
                L = pL[0:TT, 0:NT * TAPS].rearrange("p (t k) -> p t k", t=NT)
                dve.wait_ge(logits_ready, 2 * q + i + 1)
                s.did(nc.vector.tensor_reduce(mx[:, i, :], L, AX.X, ALU.max))
                s.settle()
                s.did(nc.vector.tensor_scalar(mx[:, i, :], mx[:, i, :], 0.0, None, ALU.max))
                s.settle()
                s.did(stt(Et[:, i], L, 0.0, mx[:, i, :, None].broadcast_to([TT, NT, TAPS]),
                          ALU.max, ALU.subtract))

            def normalise(q, i):
                s = Steps(dve, sm_step, q, SM_STEPS, 6 + 4 * i)
                dve.wait_ge(exp_ready, 2 * q + i + 1)
                s.did(nc.vector.tensor_reduce(sm[:, i, :], Et[:, i], AX.X, ALU.add))
                s.settle()
                s.did(nc.vector.reciprocal(sm[:, i, :], sm[:, i, :]))
                s.settle()
                s.did(nc.vector.tensor_scalar(sm[:, i, :], sm[:, i, :], ATT_SCALE, None, ALU.mult))
                s.settle()
                s.did(tt(Et[:, i], Et[:, i], sm[:, i, :, None].broadcast_to([TT, NT, TAPS]), ALU.mult))

            def a_low(q, i):
                for h in range(2):
                    dve.wait_ge(ahi_ready, 4 * q + 2 * i + h + 1)
                    cols = slice(h * 3 * TT, (h + 1) * 3 * TT)
                    tt(aTs[:, i, 1, cols], pA[0:TAPS, 0:3 * TT], aTs[:, i, 0, cols],
                       ALU.subtract).then_inc(alo_ready, 1)

            dve.wait_ge(par_loaded, 16 * 8)
            s = Steps(dve, bn_step, 0, BN_STEPS)
            s.did(nc.vector.tensor_scalar(bnp[:, 5:6], bnp[:, 4:5], 1e-5, None, ALU.add))
            s.did(tt(bnp[:, 0:1], bnp[:, 0:1], bnp[:, 3:4], ALU.subtract))
            dve.wait_ge(bn_rstd, 1)
            s.did(tt(bnp[:, 7:8], bnp[:, 6:7], bnp[:, 1:2], ALU.mult))
            s.settle()
            s.did(nc.vector.tensor_scalar(w2s[:, :], w2s[:, :], bnp[:, 7:8], None, ALU.mult))
            s.did(stt(bnp[:, 0:1], bnp[:, 0:1], bnp[:, 7:8], bnp[:, 2:3], ALU.mult, ALU.add))
            s.at(BN_STEPS)

            ln(0, 0)
            ln(0, 1)
            dve.wait_ge(pads_zeroed, 15)
            v_transform(0, 0, 0)
            v_transform(0, 0, 1)

            with dve.Fori(0, PIECES // 2) as j:
                for sl in range(2):
                    dve.wait_ge(w_loaded[sl], 16 * (j + 1))
                    nc.vector.tensor_reduce(mxp[:, ds(2 * j + sl, 1)], wst[sl][:, 0:KS * CMID], AX.X, ALU.max,
                                            apply_absolute_value=True).then_inc(w_seen, 1)
            dve.wait_ge(w_seen, PIECES)
            nc.vector.tensor_reduce(sg[:, 0:1], mxp[:, :], AX.X, ALU.max).then_inc(wmax_ready, 1)
            dve.wait_ge(wmax_all, 1)
            s = Steps(dve, sig_step, 0, 5)
            s.did(nc.vector.tensor_scalar(sg[:, 1:2], sg[:, 1:2], 2.0 ** -100, 2.0 ** 100, ALU.max, ALU.min))
            s.settle()
            s.did(nc.vector.tensor_scalar(sg[:, 2:3].bitcast(U32), sg[:, 1:2].bitcast(U32), 0x7F800000, None,
                                          ALU.bitwise_and))
            s.settle()
            s.did(nc.vector.tensor_scalar(sg[:, 4:5], sg[:, 2:3], 2.0 ** -10, None, ALU.mult))
            s.settle()
            s.did(nc.vector.reciprocal(sg[:, 3:4], sg[:, 4:5]))
            s.settle()
            dve.wait_ge(usc_set, NP)
            s.did(nc.vector.tensor_scalar(usc[:, :], usc[:, :], sg[:, 3:4], None, ALU.mult))
            s.settle()

            def u_transform(k, j, sl):
                T = utile(work)
                o = UNITS * CMID
                A4 = work[:, o:o + 8 * CMID].rearrange("p (k g n) -> p k g n", k=4, g=2)
                g = wst[sl][:, 0:8 * CMID].rearrange("p (g j n) -> p j g n", g=2, j=4)

                def pt(i):
                    return T[:, 2 * i:2 * i + 2, :]

                s = Steps(dve, u_step, k, U_STEPS)
                dve.wait_ge(w_loaded[sl], 16 * (j + PIECES // 2 + 1))
                s.did(tt(A4[:, 0], g[:, 0], g[:, 2], ALU.add))
                s.did(tt(A4[:, 1], g[:, 1], g[:, 3], ALU.add))
                s.did(stt(A4[:, 2], g[:, 2], 4.0, g[:, 0], ALU.mult, ALU.add))
                s.did(stt(A4[:, 3], g[:, 3], 4.0, g[:, 1], ALU.mult, ALU.add))
                s.did(stt(pt(5), g[:, 3], -0.5, g[:, 2], ALU.mult, ALU.add))
                s.did(nc.vector.tensor_copy(pt(4), g[:, 0]))
                s.settle()
                s.did(stt(pt(5), pt(5), -0.5, g[:, 1], ALU.mult, ALU.add))
                s.did(tt(pt(0), A4[:, 0], A4[:, 1], ALU.add))
                s.did(tt(pt(1), A4[:, 0], A4[:, 1], ALU.subtract))
                s.did(stt(pt(2), A4[:, 3], 2.0, A4[:, 2], ALU.mult, ALU.add))
                s.did(stt(pt(3), A4[:, 3], -2.0, A4[:, 2], ALU.mult, ALU.add))
                s.settle()
                s.did(nc.vector.tensor_copy(T[:, UNITS - 1, :], g[:, 3, 0, :]))
                s.did(stt(pt(5), pt(5), -0.5, g[:, 0], ALU.mult, ALU.add))
                s.at(U_READ)
                s.settle()
                s.did(tt(T, T, usc[:, :, None].broadcast_to([P, UNITS, CMID]), ALU.mult))
                s.at(U_DATA)
                s.settle()
                dve.wait_ge(uhi_ready, k + 1)
                s.did(tt(U[:, 1, :, ds(k, 1), :].rearrange("p u a n -> p u (a n)"), T,
                         U[:, 0, :, ds(k, 1), :].rearrange("p u a n -> p u (a n)"), ALU.subtract))
                s.settle()
                s.at(U_STEPS)

            with dve.Fori(0, PIECES // 2) as j:
                u_transform(2 * j, j, 0)
                u_transform(2 * j + 1, j, 1)

            def body(q, par):
                if not is_last(q):
                    ln(q + 1, 0)
                    ln(q + 1, 1)
                y_points(q, 0)
                if not is_last(q):
                    v_transform(q + 1, 1 - par, 0)
                if not is_first(q):
                    shift_logits(q - 1, 0)
                y_points(q, 1)
                if not is_first(q):
                    shift_logits(q - 1, 1)
                    normalise(q - 1, 0)
                    normalise(q - 1, 1)
                if not is_last(q):
                    v_transform(q + 1, 1 - par, 1)
                if not is_first(q):
                    a_low(q - 1, 0)
                y_mid(q)
                if not is_first(q):
                    a_low(q - 1, 1)
                y_end(q)

            pair_loop(dve, body)
            for stage in (shift_logits, normalise, a_low):
                for i in range(2):
                    stage(PAIRS - 1, i)

        @block.tensor
        def _(pe):
            pe.wait_ge(par_loaded, 16 * 8)
            pe.wait_ge(bn_step, BN_STEPS)
            nc.tensor.transpose(pL[:, 0:TAPS], w2s[:, :], ident[0:TAPS, 0:TAPS]).then_inc(w2_turned, 1)
            nc.tensor.transpose(pL[0:1, P:P + TAPS], bnp[:, 0:1], ident[0:TAPS, 0:TAPS]).then_inc(w2_turned, 1)

            def turn_x(q, i):
                pe.wait_ge(ln_step, (2 * q + i + 1) * LN_STEPS)
                for c in range(CC):
                    for h in range(2):
                        if not (is_first(q) and i == 0 and c == 0):
                            pe.wait_ge(xT_used, 8 * q + 4 * i + 2 * c + h - 1)
                        for t in range(3):
                            last = nc.tensor.transpose(pX[:, h, t * TT:(t + 1) * TT],
                                                       xa[:, i, 3 * h + t, c * P:(c + 1) * P], ident[0:TT, 0:TT])
                        last.then_inc(xT_ready, 1)

            def conv(q, par, k):
                if k == 0:
                    pe.wait_ge(v_step, (4 * q + 4) * V_STEPS)
                if k < 3:
                    after(pe, y_step, q * Y_STEPS - (5, 1, 0)[k])
                elif k == 4:
                    pe.wait_ge(m_copied, 2 * q + 1)
                elif k == 5:
                    pe.wait_ge(y_step, q * Y_STEPS + 2)
                elif k == 6:
                    pe.wait_ge(m_copied, 2 * q + 2)
                work_list = [(g, ky, c, a, b) for g in range(2) if 2 * k + g < UNITS
                             for ky in range(KS) for c in range(CC) for a, b in ((0, 0), (0, 1), (1, 0))]
                for n, (g, ky, c, a, b) in enumerate(work_list):
                    v = V[:, par, b, k, c].rearrange("p i (r t) -> p i r t", t=VT)
                    last = nc.tensor.matmul(pM[:, k % 4, 0:HALF], U[:, a, 2 * k + g, c * KS + ky, :],
                                            v[:, :, ky:ky + SIDE, g:g + QT],
                                            start=(n == 0), stop=(n == len(work_list) - 1))
                last.then_inc(m_ready, 1)

            def logits(q, i):
                if i == 0:
                    pe.wait_ge(k1_ready, q + 1)
                if i == 1:
                    pe.wait_ge(sm_step, q * SM_STEPS + 3)
                L = pL[0:TT, 0:NT * TAPS]
                nc.tensor.matmul(L, ones[:, :], brow[:, :, :].rearrange("p t k -> p (t k)"),
                                 start=True, stop=False)
                for t in range(NT):
                    last = nc.tensor.matmul(L[:, t * TAPS:(t + 1) * TAPS],
                                            k1[:, (i * NT + t) * TT:(i * NT + t + 1) * TT], w2T[:, :],
                                            start=False, stop=(t == NT - 1))
                last.then_inc(logits_ready, 1)

            def turn_a(q, i, h):
                pe.wait_ge(sm_step, q * SM_STEPS + 10 + 4 * i)
                if i + h > 0:
                    pe.wait_ge(alo_ready, 4 * q + 2 * i + h)
                for t in range(3):
                    last = nc.tensor.transpose(pA[0:EPAD, t * TT:(t + 1) * TT],
                                               E[:, i, (3 * h + t) * TAPS:(3 * h + t) * TAPS + EPAD],
                                               ident[0:TT, 0:TT])
                last.then_inc(aT_ready, 1)

            turn_x(0, 0)
            turn_x(0, 1)
            pe.wait_ge(w2_ready, 2)
            pe.wait_ge(u_step, PIECES * U_STEPS)

            def body(q, par):
                conv(q, par, 0)
                if not is_last(q):
                    turn_x(q + 1, 0)
                if not is_first(q):
                    logits(q - 1, 0)
                conv(q, par, 1)
                if not is_last(q):
                    turn_x(q + 1, 1)
                conv(q, par, 2)
                if not is_first(q):
                    logits(q - 1, 1)
                for n in range(4):
                    conv(q, par, 3 + n)
                    if not is_first(q):
                        turn_a(q - 1, n // 2, n % 2)

            pair_loop(pe, body)
            logits(PAIRS - 1, 0)
            logits(PAIRS - 1, 1)
            for n in range(4):
                turn_a(PAIRS - 1, n // 2, n % 2)


BLK = 3
R = KS // 2
EDGE = [w for w in range(SIDE) if w < R or w >= SIDE - R]
G0 = TT + SIDE * (TR - 1 - R - 1) + (SIDE - 1 - R)
GW = G0 + SIDE * (R - 1) + R + TT + TT
HHS = [(d, h) for d in (-1, 0, 1) for h in range(TR) if (d, h) not in ((-1, TR - 1), (1, 0))]
BT = 4 * NT
SLOT = 8
T_STEPS = 4 + 3 * NT + 1


def spread_table():
    import numpy as np
    g = np.zeros((TAPS, len(EDGE) + 1, GW), np.float16)
    for v, w in enumerate([SIDE // 2] + EDGE):
        for ki in range(KS):
            for kj in range(KS):
                if 0 <= w + kj - R < SIDE:
                    g[ki * KS + kj, v, SIDE * ki + kj + G0] = 1
    return g


def attend_phase(nc, xt, xn_d, attn_d, spread_d, t_d, tn_d, acc):
    with ExitStack() as ctx:
        def sb(name, shape, dt):
            return ctx.enter_context(nc.sbuf_tensor(name, shape, dt))

        def sem(name):
            return ctx.enter_context(nc.semaphore(name))

        G = sb("G", list(spread_d.shape), F16)
        aT = sb("aT", [TAPS, 2, SB], F16)
        A = sb("A", [TT, BLK, 2 * BT, TT], F16)
        xr = sb("xr", [TT, 2, NT, C], F32)
        xn = sb("xn", [TT, 2, NT, C], F32)
        X = sb("X", [TT, 2, NT, 2, C], F16)
        ts_ = sb("ts", [TT, 2, NT, C], F32)
        tn = sb("tn", [TT, 2, NT, C], F32)
        spare = sb("spare2", [1, 1], F32)
        st = sb("st2", [TT, NT, 6], F32)
        mv = sb("mv2", [TT, NT, 2], F32)
        ve = sb("ve2", [TT, NT], F32)
        rstd = sb("rstd2", [TT, NT], F32)
        mhalf = sb("mhalf2", [TT, NT], F32)
        pS = [ctx.enter_context(nc.psum_tensor(f"pS{g}", [P, 3, 512], F32)) for g in range(2)]
        pO = ctx.enter_context(nc.psum_tensor("pO", [P, 2, 512], F32))

        g_loaded = sem("g_loaded")
        at_loaded = sem("at_loaded")
        xr_loaded = [sem(f"xr_loaded{s}") for s in range(2)]
        xn_loaded = [sem(f"xn_loaded{s}") for s in range(2)]
        a_zeroed = sem("a_zeroed")
        spread = sem("spread")
        a_by_act = sem("a_by_act")
        a_by_dve = sem("a_by_dve")
        xhi_ready = sem("xhi_ready")
        o_ready = sem("o_ready")
        t_step = sem("t_step")
        rstd_ready2 = sem("rstd_ready2")
        acc_step = sem("acc_step")
        t_stored = [sem(f"t_stored{s}") for s in range(2)]
        tn_stored = [sem(f"tn_stored{s}") for s in range(2)]
        NU = len(HHS)

        def batch_loop(eng, body):
            body(0)
            with eng.Fori(1, B) as b:
                body(b)

        block = ctx.enter_context(nc.Block())

        @block.sync
        def _(sp):
            sp.dma_start(G[:, :, :], spread_d).then_inc(g_loaded, 16)

            def load(b, m):
                n, s = 4 * b + m, m % 2
                if not (is_first(b) and m < 2):
                    sp.wait_ge(t_step, (n - 2) * T_STEPS + 4)
                rows = ds(n * PIX, PIX)
                sp.dma_start(xn[:, s], xn_d[rows, :].rearrange("(t p) c -> p t c", p=TT)).then_inc(xn_loaded[s], 16)
                sp.dma_start(xr[:, s], xt[rows, :].rearrange("(t p) c -> p t c", p=TT)).then_inc(xr_loaded[s], 16)

            def body(b):
                if not is_first(b):
                    sp.wait_ge(spread, NU * b)
                sp.dma_start(aT[:, :, :], attn_d[:, :, ds(b * SB, SB)]).then_inc(at_loaded, 16)
                for m in range(4):
                    load(b, m)
            batch_loop(sp, body)

        @block.gpsimd
        def _(pool):
            nc.gpsimd.memset(A[:, 0, :, (TR - 1) * SIDE:TR * SIDE], 0.0).then_inc(a_zeroed, 1)
            nc.gpsimd.memset(A[:, 2, :, 0:SIDE], 0.0).then_inc(a_zeroed, 1)
            nc.gpsimd.memset(mhalf[:, :], -0.5).then_inc(a_zeroed, 1)
            pool.wait_ge(a_zeroed, 3)

            def body(b):
                for m in range(4):
                    n, s = 4 * b + m, m % 2
                    pool.wait_ge(t_step, n * T_STEPS + 4 + 2 * NT + 1)
                    nc.gpsimd.tensor_tensor(rstd[:, :], ve[:, :], mhalf[:, :], ALU.pow).then_inc(rstd_ready2, 1)
                    after(pool, acc_step, n)
                    pool.wait_ge(t_step, (n + 1) * T_STEPS)
                    rows = ds(n * PIX, PIX)
                    pool.dma_start(t_d[rows, :].rearrange("(t p) c -> p t c", p=TT), ts_[:, s]).then_inc(t_stored[s], 16)
                    pool.dma_start(tn_d[rows, :].rearrange("(t p) c -> p t c", p=TT), tn[:, s]).then_inc(tn_stored[s], 16)
                    a = acc[:, ds(b, 1)].rearrange("p b t c -> p (b t) c")
                    if m == 0:
                        nc.gpsimd.tensor_copy(a, tn[:, s]).then_inc(acc_step, 1)
                    else:
                        nc.gpsimd.tensor_tensor(a, a, tn[:, s], ALU.add).then_inc(acc_step, 1)
            batch_loop(pool, body)
            for s in range(2):
                pool.wait_ge(t_stored[s], 16 * IMGS // 2)
                pool.wait_ge(tn_stored[s], 16 * IMGS // 2)

        def spread_out(eng, copy, b, parity, done):
            eng.wait_ge(a_zeroed, 3)
            for u in range(parity, NU, 2):
                d, h = HHS[u]
                eng.wait_ge(spread, NU * b + u + 1)
                if u == parity and not is_first(b):
                    eng.wait_ge(o_ready, 12 * b)
                dst = A[:, d + 1, :, h * SIDE:(h + 1) * SIDE].rearrange("p n (k w) -> p k n w", w=SLOT)
                src = pS[parity][0:TT, :, 0:SLOT * 2 * BT].rearrange("p k (w n) -> p k n w", w=SLOT)
                copy(dst, src).then_inc(done, 1)

        @block.scalar
        def _(act):
            def body(b):
                spread_out(act, nc.scalar.copy, b, 0, a_by_act)
                for m in range(4):
                    n, s = 4 * b + m, m % 2
                    act.wait_ge(xn_loaded[s], 16 * (2 * b + m // 2 + 1))
                    if not (is_first(b) and m < 2):
                        act.wait_ge(o_ready, 3 * (n - 1))
                    nc.scalar.copy(X[:, s, :, 0, :], xn[:, s]).then_inc(xhi_ready, 1)
            batch_loop(act, body)

        @block.vector
        def _(dve):
            def body(b):
                spread_out(dve, nc.vector.tensor_copy, b, 1, a_by_dve)
                for m in range(4):
                    n, sl = 4 * b + m, m % 2
                    s = Steps(dve, t_step, n, T_STEPS)
                    dve.wait_ge(xhi_ready, n + 1)
                    s.did(nc.vector.tensor_tensor(X[:, sl, :, 1, :], xn[:, sl], X[:, sl, :, 0, :], ALU.subtract))
                    dve.wait_ge(xr_loaded[sl], 16 * (2 * b + m // 2 + 1))
                    if not (is_first(b) and m < 2):
                        dve.wait_ge(t_stored[sl], 16 * (2 * b + m // 2))
                        dve.wait_ge(tn_stored[sl], 16 * (2 * b + m // 2))
                        dve.wait_ge(acc_step, n - 1)
                    for u in range(3):
                        dve.wait_ge(o_ready, 3 * n + u + 1)
                        s.did(nc.vector.scalar_tensor_tensor(
                            ts_[:, sl, 2 * u:2 * u + 2, :].rearrange("p t c -> p (t c)"),
                            pO[0:TT, (3 * m + u) % 2, :], 1.0 / ATT_SCALE,
                            xr[:, sl, 2 * u:2 * u + 2, :].rearrange("p t c -> p (t c)"), ALU.mult, ALU.add))
                    s.settle()
                    for t in range(NT):
                        s.did(nc.vector.bn_stats(st[:, t, :], ts_[:, sl, t, :]))
                    s.settle()
                    carry(nc, spare[0:1, 0:1])
                    for t in range(NT):
                        s.did(nc.vector.bn_aggr(mv[:, t, :], st[:, t, :]))
                    s.settle()
                    s.did(nc.vector.tensor_scalar(ve[:, :], mv[:, :, 1], 1e-5, None, ALU.add))
                    dve.wait_ge(rstd_ready2, n + 1)
                    for t in range(NT):
                        s.did(nc.vector.tensor_scalar(tn[:, sl, t, :], ts_[:, sl, t, :], mv[:, t, 0:1],
                                                      rstd[:, t:t + 1], ALU.subtract, ALU.mult))
                    s.at(T_STEPS)
            batch_loop(dve, body)

        @block.tensor
        def _(pe):
            pe.wait_ge(g_loaded, 16)

            def spread_taps(b):
                pe.wait_ge(at_loaded, 16 * (b + 1))
                a = aT[:, :, :].rearrange("p a (n i) -> p (a n) i", i=TT)
                for u, (d, h) in enumerate(HHS):
                    pe.wait_ge(a_by_dve if u % 2 else a_by_act, (NU // 2) * b + u // 2)
                    for w in range(SIDE):
                        at = TT * d - SIDE * (h - R) - (w - R) + G0
                        v = 1 + EDGE.index(w) if w in EDGE else 0
                        o = (w % SLOT) * 2 * BT
                        last = nc.tensor.matmul(pS[u % 2][0:TT, w // SLOT, o:o + 2 * BT],
                                                G[:, v, at:at + TT], a[:, :, h * SIDE + w],
                                                start=True, stop=True)
                    last.then_inc(spread, 1)

            def attend(b, m):
                n, s = 4 * b + m, m % 2
                pe.wait_ge(t_step, n * T_STEPS + 1)
                for u in range(3):
                    if u < 2 and is_first(b) and m == 0:
                        pass
                    elif u == 2:
                        pe.wait_ge(t_step, n * T_STEPS + 2)
                    else:
                        pe.wait_ge(t_step, (n - 1) * T_STEPS + 3 + u)
                    for t in (2 * u, 2 * u + 1):
                        terms = [(d, a, x) for d in (-1, 0, 1) if 0 <= t + d < NT
                                 for a, x in ((0, 0), (0, 1), (1, 0))]
                        for k, (d, a, x) in enumerate(terms):
                            last = nc.tensor.matmul(pO[0:TT, (3 * m + u) % 2, (t % 2) * C:(t % 2 + 1) * C],
                                                    A[:, d + 1, a * BT + m * NT + t, :], X[:, s, t + d, x, :],
                                                    start=(k == 0), stop=(k == len(terms) - 1))
                    last.then_inc(o_ready, 1)

            def body(b):
                spread_taps(b)
                pe.wait_ge(a_by_act, (NU // 2) * (b + 1))
                pe.wait_ge(a_by_dve, (NU // 2) * (b + 1))
                for m in range(4):
                    attend(b, m)
            batch_loop(pe, body)


EXPERTS, TOPK, FH = 8, 2, 512
FB = FH // P
CAPACITY = float(-(-N * 5 // (4 * EXPERTS)))
CT = 3
CN = CT * P
CHUNKS = SB // CN
JB = TOPK * FB
R_STEPS = 24
Z_VE = 3 * CT + 1
Z_ALL = 5 * CT + 1


def ffn_phase(nc, acc, t_d, tn_d, wr, br, ew1, eb1, ew2, eb2, gamma, beta, ident_d, out):
    with ExitStack() as ctx:
        def sb(name, shape, dt):
            return ctx.enter_context(nc.sbuf_tensor(name, shape, dt))

        def sem(name):
            return ctx.enter_context(nc.semaphore(name))

        ident = sb("ident3", [P, P], F32)
        wrs = sb("wrs", [P, CC, EXPERTS], F32)
        brs = sb("brs", [1, EXPERTS], F32)
        ones = sb("ones3", [P, P], F32)
        mean = sb("mean3", [P, CC * B], F32)
        r = sb("r", [B, 8, EXPERTS], F32)
        rc = sb("rc", [B, 8], F32)
        idx = sb("idx", [B, EXPERTS], U32)
        wv = sb("wv", [B, TOPK], F32)
        irow = sb("irow", [1, B * TOPK], U32)
        wrow = sb("wrow", [1, B * TOPK], F32)
        wbc = sb("wbc", [P, B * TOPK], F32)
        gam = sb("gam", [P, C], F32)
        bet = sb("bet", [P, C], F32)
        w1r = sb("w1r", [P, TOPK, CC, FH], F32)
        w2r = sb("w2r", [P, TOPK, FB, C], F32)
        b1r = sb("b1r", [P, TOPK, FB], F32)
        b2r = sb("b2r", [P, TOPK, C], F32)
        w1h = sb("w1h", [P, TOPK, CC, FH], F32R)
        w1l = sb("w1l", [P, TOPK, CC, FH], F32R)
        w2h = sb("w2h", [P, TOPK, FB, C], F32R)
        w2l = sb("w2l", [P, TOPK, FB, C], F32R)
        b1c = sb("b1c", [P, TOPK, FB], F32)
        b2c = sb("b2c", [P, 2, C], F32)
        tk = sb("tk", [P, 2, CT, C], F32)
        tnk = sb("tnk", [P, 2, CT, C], F32)
        tb = sb("tb", [P, 2, CT, C], F32)
        tnb = sb("tnb", [P, 2, CT, C], F32)
        xh = sb("xh", [P, 2, CC, CN], F32R)
        xl = sb("xl", [P, 2, CC, CN], F32R)
        gf = sb("gf", [P, 2, CN], F32)
        gh = sb("gh", [P, 2, JB, CN], F32R)
        gl = sb("gl", [P, 2, JB, CN], F32R)
        z = sb("z", [P, CT, C], F32)
        o = sb("o", [P, 2, CT, C], F32)
        spare = sb("spare3", [1, 1], F32)
        st = sb("st3", [P, CT, 6], F32)
        mv = sb("mv3", [P, CT, 2], F32)
        ve = sb("ve3", [P, CT], F32)
        rstd = sb("rstd3", [P, CT], F32)
        mhalf = sb("mhalf3", [P, CT], F32)
        pT = ctx.enter_context(nc.psum_tensor("pT", [P, CC, 512], F32))
        pH = ctx.enter_context(nc.psum_tensor("pH", [P, 4, 512], F32))
        pY = ctx.enter_context(nc.psum_tensor("pY", [P, 2, 512], F32))

        c_loaded = sem("c_loaded")
        c_set = sem("c_set")
        sums_ready = sem("sums_ready")
        r_pe = sem("r_pe")
        r_step = sem("r_step")
        r_exp = sem("r_exp")
        row_loaded = sem("row_loaded")
        w1_loaded = sem("w1_loaded")
        w2_loaded = sem("w2_loaded")
        whi_ready = sem("whi_ready")
        w_step = sem("w_step")
        w_bias = sem("w_bias")
        tk_loaded = [sem(f"tk_loaded{s}") for s in range(2)]
        tnk_loaded = [sem(f"tnk_loaded{s}") for s in range(2)]
        x_turned = sem("x_turned")
        xh_ready = sem("xh_ready")
        xl_ready = sem("xl_ready")
        h_ready = sem("h_ready")
        gelu_done = sem("gelu_done")
        g_step = sem("g_step")
        y_ready = sem("y_ready3")
        bias_added = sem("bias_added")
        z_step = sem("z_step")
        rstd_ready = sem("rstd_ready3")
        out_stored = [sem(f"out_stored{s}") for s in range(2)]

        def batch_loop(eng, body):
            body(0)
            with eng.Fori(1, B) as b:
                body(b)

        block = ctx.enter_context(nc.Block())

        @block.sync
        def _(sp):
            sp.dma_start(ident[:, :], ident_d).then_inc(c_loaded, 16)
            sp.dma_start(wrs[:, :, :], wr.rearrange("(c p) e -> p c e", p=P)).then_inc(c_loaded, 16)
            sp.dma_start(brs[:, :], br).then_inc(c_loaded, 16)
            sp.dma_start(gam[:, :], gamma.broadcast_to([P, C])).then_inc(c_loaded, 16)
            sp.dma_start(bet[:, :], beta.broadcast_to([P, C])).then_inc(c_loaded, 16)

            def load_chunk(b, m):
                n, s = CHUNKS * b + m, m % 2
                if not (is_first(b) and m < 2):
                    sp.wait_ge(x_turned, 2 * (n - 1))
                    sp.wait_ge(bias_added, 2 * (n - 1))
                rows = ds(n * CN, CN)
                sp.dma_start(tnk[:, s], tn_d[rows, :].rearrange("(t p) c -> p t c", p=P)).then_inc(tnk_loaded[s], 16)
                sp.dma_start(tk[:, s], t_d[rows, :].rearrange("(t p) c -> p t c", p=P)).then_inc(tk_loaded[s], 16)

            def store_chunk(b, m):
                n, s = CHUNKS * b + m, m % 2
                sp.wait_ge(z_step, (n + 1) * Z_ALL)
                sp.dma_start(out[ds(n * CN, CN), :].rearrange("(t p) c -> p t c", p=P),
                             o[:, s]).then_inc(out_stored[s], 16)

            def load_experts(b):
                if not is_first(b):
                    sp.wait_ge(w_step, 4 * b)
                for k in range(TOPK):
                    e = sp.value_load(irow[0:1, ds(TOPK * b + k, 1)], min_val=0, max_val=EXPERTS - 1)
                    sp.dma_start(w1r[:, k], ew1[ds(e, 1)].rearrange("e (c p) f -> p (e c) f", p=P)
                                 ).then_inc(w1_loaded, 16)
                    sp.dma_start(b1r[:, k], ew_b(eb1, e)).then_inc(w1_loaded, 16)
                    sp.dma_start(w2r[:, k], ew2[ds(e, 1)].rearrange("e (f p) c -> p (e f) c", p=P)
                                 ).then_inc(w2_loaded, 16)
                    sp.dma_start(b2r[:, k], eb2[ds(e, 1), :].broadcast_to([P, C])).then_inc(w2_loaded, 16)

            def ew_b(eb1, e):
                return eb1[ds(e, 1)].rearrange("e p f -> (e p) f")

            load_chunk(0, 0)
            load_chunk(0, 1)
            sp.wait_ge(r_step, R_STEPS)
            for b in range(B):
                sp.dma_start(irow[0:1, TOPK * b:TOPK * (b + 1)], idx[b:b + 1, 0:TOPK]).then_inc(row_loaded, 16)
                sp.dma_start(wrow[0:1, TOPK * b:TOPK * (b + 1)], wv[b:b + 1, :]).then_inc(row_loaded, 16)
            sp.wait_ge(row_loaded, 16 * 2 * B)

            def body(b):
                load_experts(b)
                for m in range(CHUNKS):
                    if m + 2 < CHUNKS:
                        load_chunk(b, m + 2)
                    elif not (isinstance(b, int) and b == B - 1):
                        load_chunk(b + 1, m + 2 - CHUNKS)
                    store_chunk(b, m)

            body(0)
            with sp.Fori(1, B - 1) as b:
                body(b)
            body(B - 1)
            for s in range(2):
                sp.wait_ge(out_stored[s], 16 * B * CHUNKS // 2)

        @block.gpsimd
        def _(pool):
            nc.gpsimd.memset(ones[:, :], 1.0).then_inc(c_set, 1)
            nc.gpsimd.memset(mhalf[:, :], -0.5).then_inc(c_set, 1)
            pool.wait_ge(c_set, 2)
            pool.wait_ge(c_loaded, 16 * 5)

            def add_bias(b, m):
                n, s = CHUNKS * b + m, m % 2
                if m == 0:
                    pool.wait_ge(w_step, 4 * (b + 1))
                pool.wait_ge(tnk_loaded[s], 16 * (CHUNKS // 2 * b + m // 2 + 1))
                pool.wait_ge(tk_loaded[s], 16 * (CHUNKS // 2 * b + m // 2 + 1))
                if not (is_first(b) and m < 2):
                    pool.wait_ge(z_step, (n - 1) * Z_ALL)
                nc.gpsimd.tensor_tensor(tnb[:, s], tnk[:, s], b2c[:, 1:2, :].broadcast_to([P, CT, C]),
                                        ALU.add).then_inc(bias_added, 1)
                nc.gpsimd.tensor_tensor(tb[:, s], tk[:, s], bet[:, None, :].broadcast_to([P, CT, C]),
                                        ALU.add).then_inc(bias_added, 1)

            def rsqrt(b, m):
                n = CHUNKS * b + m
                pool.wait_ge(z_step, n * Z_ALL + Z_VE)
                nc.gpsimd.tensor_tensor(rstd[:, :], ve[:, :], mhalf[:, :], ALU.pow).then_inc(rstd_ready, 1)

            def body(b):
                add_bias(b, 0)
                for m in range(CHUNKS):
                    if m + 1 < CHUNKS:
                        add_bias(b, m + 1)
                    rsqrt(b, m)
            batch_loop(pool, body)

        @block.scalar
        def _(act):
            for k in range(3):
                act.wait_ge(r_step, (3, 15, 21)[k])
                if k < 2:
                    nc.scalar.activation(r[:, 2 * k + 1, :], r[:, 2 * k, :], ACT.Exp).then_inc(r_exp, 1)
                else:
                    nc.scalar.activation(rc[:, 5:6], rc[:, 4:5], ACT.Exp).then_inc(r_exp, 1)

            def split_weights(b):
                act.wait_ge(w1_loaded, 64 * (b + 1))
                if not is_first(b):
                    act.wait_ge(y_ready, CT * CHUNKS * b)
                nc.scalar.copy(w1h[:, :, :, :], w1r[:, :, :, :]).then_inc(whi_ready, 1)
                act.wait_ge(w2_loaded, 64 * (b + 1))
                act.wait_ge(r_pe, 3)
                act.wait_ge(r_step, R_STEPS + 1)
                for k in range(TOPK):
                    nc.scalar.activation(w2h[:, k], w2r[:, k], ACT.Copy,
                                         scale=wbc[:, ds(TOPK * b + k, 1)]).then_inc(whi_ready, 1)

            def take_x(b, m):
                n, s = CHUNKS * b + m, m % 2
                act.wait_ge(x_turned, 2 * (n + 1))
                if not (is_first(b) and m < 2):
                    act.wait_ge(h_ready, JB * (n - 1))
                nc.scalar.copy(xh[:, s], pT[:, :, 0:CN]).then_inc(xh_ready, 1)

            def gelus(b, m):
                n = CHUNKS * b + m
                for j in range(JB):
                    act.wait_ge(h_ready, JB * n + j + 1)
                    if not (is_first(b) and m == 0 and j < 2):
                        act.wait_ge(g_step, 2 * (JB * n + j - 1))
                    nc.scalar.activation(gf[:, j % 2, :], pH[:, j % 4, 0:CN], ACT.Gelu,
                                         bias=b1c[:, j // FB, j % FB:j % FB + 1]).then_inc(gelu_done, 1)

            def body(b):
                split_weights(b)
                act.wait_ge(w_step, 4 * (b + 1))
                take_x(b, 0)
                for m in range(CHUNKS):
                    gelus(b, m)
                    if m + 1 < CHUNKS:
                        take_x(b, m + 1)
            batch_loop(act, body)

        @block.vector
        def _(dve):
            tt, stt = nc.vector.tensor_tensor, nc.vector.scalar_tensor_tensor
            s = Steps(dve, r_step, 0, R_STEPS)

            def do(ins):
                s.did(ins)
                s.settle()

            def softmax_shift(src, dst, col):
                do(nc.vector.tensor_reduce(rc[:, col:col + 1], src, AX.X, ALU.max))
                do(nc.vector.tensor_scalar(dst, src, rc[:, col:col + 1], None, ALU.subtract))

            def softmax_divide(src, dst, col):
                do(nc.vector.tensor_reduce(rc[:, col:col + 1], src, AX.X, ALU.add))
                do(nc.vector.reciprocal(rc[:, col:col + 1], rc[:, col:col + 1]))
                do(nc.vector.tensor_scalar(dst, src, rc[:, col:col + 1], None, ALU.mult))

            dve.wait_ge(sums_ready, 1)
            do(nc.vector.tensor_scalar(mean[:, :], pT[:, 0, 0:CC * B], 1.0 / SB, None, ALU.mult))
            dve.wait_ge(r_pe, 1)
            softmax_shift(pT[0:B, 1, 0:EXPERTS], r[:, 0, :], 0)
            dve.wait_ge(r_exp, 1)
            softmax_divide(r[:, 1, :], r[:, 4, :], 1)
            dve.wait_ge(r_pe, 2)
            do(nc.vector.tensor_scalar(r[:, 5, :], pT[0:B, 0, 64:64 + EXPERTS], float(SB), None, ALU.mult))
            do(nc.vector.reciprocal(r[:, 5, :], r[:, 5, :]))
            do(nc.vector.tensor_scalar(r[:, 5, :], r[:, 5, :], CAPACITY, 1.0, ALU.mult, ALU.min))
            do(tt(r[:, 6, :], r[:, 5, :], r[:, 4, :], ALU.mult))
            softmax_shift(r[:, 6, :], r[:, 2, :], 2)
            do(nc.vector.tensor_copy(rc[:, 6:7], rc[:, 2:3]))
            do(nc.vector.tensor_copy(rc[:, 7:8], rc[:, 2:3]))
            do(nc.vector.tensor_copy(rc[:, 7:8], rc[:, 2:3]))
            dve.wait_ge(r_exp, 2)
            softmax_divide(r[:, 3, :], r[:, 7, :], 3)
            do(nc.vector.max(r[:, 0, :], r[:, 7, :]))
            do(nc.vector.max_index(idx[:, :], r[:, 0, :], r[:, 7, :]))
            do(tt(rc[:, 4:5], r[:, 0, 1:2], r[:, 0, 0:1], ALU.subtract))
            dve.wait_ge(r_exp, 3)
            do(nc.vector.tensor_scalar(rc[:, 6:7], rc[:, 5:6], 1.0, None, ALU.add))
            do(nc.vector.reciprocal(wv[:, 0:1], rc[:, 6:7]))
            do(tt(wv[:, 1:2], rc[:, 5:6], wv[:, 0:1], ALU.mult))
            s.at(R_STEPS)
            dve.wait_ge(r_pe, 3)
            nc.vector.tensor_copy(wbc[:, :], pT[:, 1, 64:64 + TOPK * B]).then_inc(r_step, 1)
            dve.wait_ge(r_step, R_STEPS + 1)

            def split_weights(b):
                s = Steps(dve, w_step, b, 4)
                dve.wait_ge(whi_ready, 3 * b + 1)
                s.did(tt(w1l[:, :, :, :], w1r[:, :, :, :], w1h[:, :, :, :].bitcast(F32), ALU.subtract))
                nc.vector.tensor_copy(b1c[:, :, :], b1r[:, :, :]).then_inc(w_bias, 1)
                dve.wait_ge(whi_ready, 3 * b + 2)
                nc.vector.tensor_scalar(b2c[:, 0, :], b2r[:, 0, :], wbc[:, ds(TOPK * b, 1)], None,
                                        ALU.mult).then_inc(w_bias, 1)
                s.did(stt(w2l[:, 0], w2r[:, 0], wbc[:, ds(TOPK * b, 1)], w2h[:, 0].bitcast(F32),
                          ALU.mult, ALU.subtract))
                dve.wait_ge(w_bias, 2 * (b + 1))
                s.did(stt(b2c[:, 1, :], b2r[:, 1, :], wbc[:, ds(TOPK * b + 1, 1)], b2c[:, 0, :],
                          ALU.mult, ALU.add))
                dve.wait_ge(whi_ready, 3 * b + 3)
                s.did(stt(w2l[:, 1], w2r[:, 1], wbc[:, ds(TOPK * b + 1, 1)], w2h[:, 1].bitcast(F32),
                          ALU.mult, ALU.subtract))
                s.at(4)

            def take_x(b, m):
                n, sl = CHUNKS * b + m, m % 2
                dve.wait_ge(xh_ready, n + 1)
                tt(xl[:, sl], pT[:, :, 0:CN], xh[:, sl].bitcast(F32), ALU.subtract).then_inc(xl_ready, 1)

            def split_hidden(b, m):
                n, sl = CHUNKS * b + m, m % 2
                s = Steps(dve, g_step, n, 2 * JB)
                if not (is_first(b) and m < 2):
                    dve.wait_ge(y_ready, CT * (n - 1))
                for j in range(JB):
                    dve.wait_ge(gelu_done, JB * n + j + 1)
                    s.did(nc.vector.tensor_copy(gh[:, sl, j, :], gf[:, j % 2, :]))
                    s.settle()
                    s.did(tt(gl[:, sl, j, :], gf[:, j % 2, :], gh[:, sl, j, :].bitcast(F32), ALU.subtract))

            def finish(b, m):
                n, sl = CHUNKS * b + m, m % 2
                s = Steps(dve, z_step, n, Z_ALL)
                s.settle()
                dve.wait_ge(bias_added, 2 * (n + 1))
                for t in range(CT):
                    dve.wait_ge(y_ready, CT * n + t + 1)
                    s.did(tt(z[:, t, :], pY[:, (CT * m + t) % 2, 0:C], tnb[:, sl, t, :], ALU.add))
                s.settle()
                for t in range(CT):
                    s.did(nc.vector.bn_stats(st[:, t, :], z[:, t, :]))
                s.settle()
                carry(nc, spare[0:1, 0:1])
                for t in range(CT):
                    s.did(nc.vector.bn_aggr(mv[:, t, :], st[:, t, :]))
                s.settle()
                s.did(nc.vector.tensor_scalar(ve[:, :], mv[:, :, 1], 1e-5, None, ALU.add))
                s.at(Z_VE)
                for t in range(CT):
                    s.did(stt(z[:, t, :], z[:, t, :], mv[:, t, 0:1], gam[:, :], ALU.subtract, ALU.mult))
                s.settle()
                dve.wait_ge(rstd_ready, n + 1)
                if not (is_first(b) and m < 2):
                    dve.wait_ge(out_stored[sl], 16 * (CHUNKS // 2 * b + m // 2))
                for t in range(CT):
                    s.did(stt(o[:, sl, t, :], z[:, t, :], rstd[:, t:t + 1], tb[:, sl, t, :],
                              ALU.mult, ALU.add))
                s.at(Z_ALL)

            def body(b):
                split_weights(b)
                take_x(b, 0)
                split_hidden(b, 0)
                for m in range(CHUNKS):
                    if m + 1 < CHUNKS:
                        take_x(b, m + 1)
                        split_hidden(b, m + 1)
                    finish(b, m)
            batch_loop(dve, body)

        @block.tensor
        def _(pe):
            pe.wait_ge(c_set, 2)
            pe.wait_ge(c_loaded, 16 * 5)
            for c in range(CC):
                for b in range(B):
                    for t in range(NT):
                        last = nc.tensor.matmul(pT[:, 0, c * B + b:c * B + b + 1],
                                                acc[:, b, t, c * P:(c + 1) * P], ones[0:TT, 0:1],
                                                start=(t == 0), stop=(t == NT - 1))
            last.then_inc(sums_ready, 1)
            pe.wait_ge(r_step, 1)
            for c in range(CC):
                nc.tensor.matmul(pT[0:B, 1, 0:EXPERTS], mean[:, c * B:(c + 1) * B], wrs[:, c, :],
                                 start=(c == 0), stop=False)
            nc.tensor.matmul(pT[0:B, 1, 0:EXPERTS], ones[0:1, 0:B], brs[:, :],
                             start=False, stop=True).then_inc(r_pe, 1)
            pe.wait_ge(r_step, 6)
            nc.tensor.matmul(pT[0:B, 0, 64:64 + EXPERTS], ones[0:B, 0:B], r[:, 4, :],
                             start=True, stop=True).then_inc(r_pe, 1)
            pe.wait_ge(row_loaded, 16 * 2 * B)
            nc.tensor.matmul(pT[:, 1, 64:64 + TOPK * B], ones[0:1, :], wrow[:, :],
                             start=True, stop=True).then_inc(r_pe, 1)
            pe.wait_ge(r_step, R_STEPS + 1)

            def turn_x(b, m):
                n, s = CHUNKS * b + m, m % 2
                pe.wait_ge(tnk_loaded[s], 16 * (CHUNKS // 2 * b + m // 2 + 1))
                after(pe, xl_ready, n)
                for c in range(CC):
                    for t in range(CT):
                        last = nc.tensor.transpose(pT[:, c, t * P:(t + 1) * P],
                                                   tnk[:, s, t, c * P:(c + 1) * P], ident[:, :])
                    last.then_inc(x_turned, 1)

            def layer1(b, m):
                n, s = CHUNKS * b + m, m % 2
                pe.wait_ge(xl_ready, n + 1)
                for j in range(JB):
                    if not (is_first(b) and m == 0 and j < 4):
                        pe.wait_ge(gelu_done, JB * n + j - 3)
                    k, f = j // FB, j % FB
                    terms = [(c, w, x) for c in range(CC) for w, x in ((w1h, xh), (w1h, xl), (w1l, xh))]
                    for i, (c, w, x) in enumerate(terms):
                        last = nc.tensor.matmul(pH[:, j % 4, 0:CN], w[:, k, c, f * P:(f + 1) * P], x[:, s, c, :],
                                                start=(i == 0), stop=(i == len(terms) - 1))
                    last.then_inc(h_ready, 1)

            def layer2(b, m):
                n, s = CHUNKS * b + m, m % 2
                pe.wait_ge(g_step, 2 * JB * (n + 1))
                for t in range(CT):
                    if not (is_first(b) and m == 0 and t < 2):
                        pe.wait_ge(z_step, (n - 1) * Z_ALL + t + 2 if t < 2 else n * Z_ALL + 1)
                    terms = [(j, g, w) for j in range(JB) for g, w in ((gh, w2h), (gh, w2l), (gl, w2h))]
                    for i, (j, g, w) in enumerate(terms):
                        last = nc.tensor.matmul(pY[:, (CT * m + t) % 2, 0:C], g[:, s, j, t * P:(t + 1) * P],
                                                w[:, j // FB, j % FB, :],
                                                start=(i == 0), stop=(i == len(terms) - 1))
                    last.then_inc(y_ready, 1)

            def body(b):
                pe.wait_ge(w_step, 4 * (b + 1))
                turn_x(b, 0)
                layer1(b, 0)
                turn_x(b, 1)
                for m in range(CHUNKS):
                    if m + 1 < CHUNKS:
                        layer1(b, m + 1)
                    if m + 2 < CHUNKS:
                        turn_x(b, m + 2)
                    layer2(b, m)
            batch_loop(pe, body)


def program(nc, xt, w1p, b1, w2, b2, bn_gamma, bn_beta, bn_mean, bn_var, wr, br, ew1, eb1, ew2, eb2,
            gamma, beta, ident_d, spread_d, out):
    xn_d = nc.dram_tensor("xn_scratch", (N, C), F32, kind="Internal").ap()
    attn_d = nc.dram_tensor("attn_scratch", (TAPS, 2, N), F16, kind="Internal").ap()
    t_d = nc.dram_tensor("t_scratch", (N, C), F32, kind="Internal").ap()
    tn_d = nc.dram_tensor("tn_scratch", (N, C), F32, kind="Internal").ap()
    conv_phase(nc, xt, w1p, b1, w2, b2, bn_gamma, bn_beta, bn_mean, bn_var, ident_d, xn_d, attn_d)
    with nc.sbuf_tensor("acc", [TT, B, NT, C], F32) as acc:
        attend_phase(nc, xt, xn_d, attn_d, spread_d, t_d, tn_d, acc)
        ffn_phase(nc, acc, t_d, tn_d, wr, br, ew1, eb1, ew2, eb2, gamma, beta, ident_d, out)


def kernel(**inputs):
    import numpy as np
    import concourse.bacc as bacc
    from concourse.bass_utils import run_bass_kernel_spmd

    a = {k: np.asarray(v) for k, v in inputs.items()}

    def parity_order(x):
        return x.reshape(B, C, SIDE, 2, SIDE, 2).transpose(0, 3, 5, 2, 4, 1)

    w1 = a["L0_conv_w1"].reshape(CMID, CC, P, KS, KS)
    arrays = {
        "xt": parity_order(a["x"]).reshape(N, C),
        "w1p": w1.transpose(1, 3, 2, 4, 0).reshape(CC * KS, P, KS * CMID),
        "b1": a["L0_conv_b1"].reshape(CMID, 1),
        "w2": a["L0_conv_w2"].reshape(TAPS, CMID),
        "b2": a["L0_conv_b2"].reshape(TAPS, 1),
        "bn_gamma": a["L0_conv_bn_gamma"].reshape(TAPS, 1),
        "bn_beta": a["L0_conv_bn_beta"].reshape(TAPS, 1),
        "bn_mean": a["L0_conv_bn_mean"].reshape(TAPS, 1),
        "bn_var": a["L0_conv_bn_var"].reshape(TAPS, 1),
        "wr": a["L0_ffn_Wr"],
        "br": a["L0_ffn_br"].reshape(1, EXPERTS),
        "ew1": a["L0_ffn_W1"],
        "eb1": a["L0_ffn_b1"].reshape(EXPERTS, FB, P).transpose(0, 2, 1),
        "ew2": a["L0_ffn_W2"],
        "eb2": a["L0_ffn_b2"],
        "gamma": a["L0_ffn_gamma"].reshape(1, C),
        "beta": a["L0_ffn_beta"].reshape(1, C),
        "ident": np.eye(P, dtype=np.float32),
        "spread": spread_table(),
    }
    arrays = {k: np.ascontiguousarray(v) for k, v in arrays.items()}
    nc = bacc.Bacc("TRN2", target_bir_lowering=False, num_devices=1)
    args = [nc.dram_tensor(f"in_{k}", v.shape, mybir.dt.from_np(v.dtype), kind="ExternalInput").ap()
            for k, v in arrays.items()]
    out = nc.dram_tensor("out_0", (N, C), F32, kind="ExternalOutput").ap()
    program(nc, *args, out)
    r = run_bass_kernel_spmd(nc, [{f"in_{k}": v for k, v in arrays.items()}], core_ids=[0])
    y = np.asarray(r.results[0]["out_0"]).reshape(B, 2, 2, SIDE, SIDE, C)
    return np.ascontiguousarray(y.transpose(0, 5, 3, 1, 4, 2).reshape(B, C, HH, WW))
```

```python
from contextlib import ExitStack

import concourse.bass as bass
from concourse import mybir
from concourse.bass import ds

ALU = mybir.AluOpType
ACT = mybir.ActivationFunctionType
F32 = mybir.dt.float32
F32R = mybir.dt.float32r
F16 = mybir.dt.float16
U32 = mybir.dt.uint32
I32 = mybir.dt.int32
AX = mybir.AxisListType

P = 128
B, C, HH, WW = 4, 256, 48, 48
KS = 7
TAPS = KS * KS
SIDE = HH // 2
IMGS = B * 4
PIX = SIDE * SIDE
N = IMGS * PIX
SB = N // B
CC = C // P
CMID = 128
TR = 4
TT = TR * SIDE
NT = SIDE // TR
PAIRS = IMGS // 2

POINTS = [1.0, -1.0, 2.0, -2.0, -0.5, 0.0]
NP = len(POINTS) + 1
UNITS = 2 * NP - 1
QT = SIDE // 4
VT = QT + 1
CW = 32
HALF = 2 * SIDE * QT
ATT_SCALE = 1024.0
EPAD = 66

LN_VE = 2 * NT + 1
LN_STEPS = 2 * (LN_VE + NT)
V_STEPS = 12
V_READ, V_HEAD = 2, 5
W_SLOTS = 4
UV_STEPS, UP_STEPS = 7, 4
Y_STEPS = 14
SM_STEPS = 14
BN_STEPS = 5
SIG_STEPS = 4


def point_norm(k):
    if k == NP - 1:
        return 1.0
    d = 1.0
    for j, b in enumerate(POINTS):
        if j != k:
            d *= POINTS[k] - b
    return 1.0 / d


class Steps:

    def __init__(self, eng, sem, run, per, first=0):
        self.eng, self.sem, self.base, self.n = eng, sem, run * per, first

    def did(self, ins):
        self.n += 1
        ins.then_inc(self.sem, 1)

    def settle(self):
        after(self.eng, self.sem, self.base + self.n)

    def at(self, n):
        assert self.n == n, (self.n, n)


def after(eng, sem, value):
    if isinstance(value, int) and value <= 0:
        return
    eng.wait_ge(sem, value)


def carry(nc, spare):
    nc.vector.memset(spare, 0.0)


def is_first(q):
    return isinstance(q, int) and q == 0


def conv_phase(nc, xt, w1p, b1, w2, b2, bn_gamma, bn_beta, bn_mean, bn_var, ident_d, xn_d, attn_d):
    PIECES = CC * KS
    PADS = 4 + 2 + 3 + W_SLOTS
    with ExitStack() as ctx:
        def sb(name, shape, dt):
            return ctx.enter_context(nc.sbuf_tensor(name, shape, dt))

        def ps(name, shape):
            return ctx.enter_context(nc.psum_tensor(name, shape, F32))

        def sem(name):
            return ctx.enter_context(nc.semaphore(name))

        U = sb("U", [P, 2, UNITS, PIECES, CMID], F16)
        VR = SIDE + KS - 1
        V = sb("V", [P, 2, 2, NP, CC, 2, VR * VT], F16)
        ch = sb("ch", [P, 2, CC, SIDE, CW], F32)
        xa = sb("xa", [TT, 2, NT, C], F32)
        ydata = sb("ydata", [P, 4 * HALF], F32)
        k1 = sb("k1", [P, 4 * HALF], F32)
        WORK = SIDE * (CW + 28 + 14 + 14 + NP * VT)
        work = sb("work", [P, WORK], F32)
        msb = sb("msb", [P, 2, HALF], F32)
        sd = sb("sd", [P, 4, HALF], F32)
        E = sb("E", [TT, 2, NT * TAPS + EPAD - TAPS], F32)
        spare = sb("spare", [1, 1], F32)
        aTs = sb("aTs", [TAPS, 2, 2, PIX], F16)
        ident = sb("ident", [P, P], F32)
        st = sb("st", [TT, 2, NT, 6], F32)
        mv = sb("mv", [TT, 2, NT, 2], F32)
        ve = sb("ve", [TT, 2, NT], F32)
        rstd = sb("rstd", [TT, 2, NT], F32)
        mhalf = sb("mhalf", [TT, NT], F32)
        mx = sb("mx", [TT, 2, NT], F32)
        sm = sb("sm", [TT, 2, NT], F32)
        w2s = sb("w2s", [TAPS, CMID], F32)
        w2T = sb("w2T", [CMID, TAPS], F32)
        bnp = sb("bnp", [TAPS, 8], F32)
        brow = sb("brow", [1, NT, TAPS], F32)
        ones = sb("ones", [1, TT], F32)
        b1s = sb("b1s", [CMID, 1], F32)
        mxp = sb("mxp", [P, PIECES], F32)
        sg = sb("sg", [P, 6], F32)

        pM = ps("pM", [P, 4, 512])
        pX = ps("pX", [P, 2, 512])
        pL = ps("pL", [P, 512])
        pA = ps("pA", [P, 512])

        par_loaded = sem("par_loaded")
        pads_zeroed = sem("pads_zeroed")
        odd_zeroed = sem("odd_zeroed")
        w_seen = sem("w_seen")
        wmax_ready = sem("wmax_ready")
        wmax_all = sem("wmax_all")
        sig_step = sem("sig_step")
        uv_step = sem("uv_step")
        up_step = sem("up_step")
        t_free = sem("t_free")
        uhi_ready = sem("uhi_ready")
        bn_step = sem("bn_step")
        bn_rstd = sem("bn_rstd")
        w2_turned = sem("w2_turned")
        w2_ready = sem("w2_ready")
        ln_step = sem("ln_step")
        rstd_ready = sem("rstd_ready")
        xT_ready = sem("xT_ready")
        xT_used = sem("xT_used")
        v_step = sem("v_step")
        vhi_ready = sem("vhi_ready")
        vlo_ready = sem("vlo_ready")
        m_ready = sem("m_ready")
        m_copied = sem("m_copied")
        y_step = sem("y_step")
        k1_ready = sem("k1_ready")
        logits_ready = sem("logits_ready")
        sm_step = sem("sm_step")
        exp_ready = sem("exp_ready")
        aT_ready = sem("aT_ready")
        ahi_ready = sem("ahi_ready")
        alo_ready = sem("alo_ready")
        w_loaded = [sem(f"w_loaded{s}") for s in range(W_SLOTS)]
        x_loaded = [sem(f"x_loaded{i}") for i in range(2)]
        xn_stored = [sem(f"xn_stored{i}") for i in range(2)]
        at_stored = [sem(f"at_stored{i}") for i in range(2)]

        def pair_loop(eng, body):
            body(0, 0)
            with eng.Fori(0, PAIRS // 2 - 1) as j:
                body(2 * j + 1, 1)
                body(2 * j + 2, 0)
            body(PAIRS - 1, 1)

        def is_last(q):
            return isinstance(q, int) and q == PAIRS - 1

        wst = [V[:, 1, s // 2].rearrange("p k c i n -> p (k c i n)").bitcast(F32)[
            :, (s % 2) * 8 * CMID:(s % 2 + 1) * 8 * CMID] for s in range(W_SLOTS)]
        TU = UNITS - 3
        Tu = work[:, 0:2 * TU * CMID].rearrange("p (s u n) -> p s u n", s=2, n=CMID)
        Au = sd[:, :, :].rearrange("p k n -> p (k n)")[:, 0:8 * CMID].rearrange("p (k g n) -> p k g n", k=4, g=2)

        def taps_of(sl):
            return wst[sl].rearrange("p (g j n) -> p j g n", g=2, j=4)

        def piece_loop(eng, body):
            with eng.Fori(0, PIECES // W_SLOTS) as j:
                body(j * W_SLOTS, j, W_SLOTS)
            body(PIECES // W_SLOTS * W_SLOTS, PIECES // W_SLOTS, PIECES % W_SLOTS)

        def w_turns(sl):
            return PIECES // W_SLOTS + (sl < PIECES % W_SLOTS)

        def vtile(w):
            o = SIDE * (CW + 28 + 14 + 14)
            return w[:, o:o + NP * SIDE * VT].rearrange("p (k n) -> p k n", k=NP)

        def a_bank(i, h):
            return ((pA, pL), (pX[:, 0, :], pX[:, 1, :]))[i][h]

        block = ctx.enter_context(nc.Block())

        @block.sync
        def _(sp):
            sp.dma_start(w2s[:, :], w2).then_inc(par_loaded, 16)
            for k, v in enumerate((b2, bn_gamma, bn_beta, bn_mean, bn_var)):
                sp.dma_start(bnp[:, k:k + 1], v).then_inc(par_loaded, 16)
            sp.dma_start(b1s[:, :], b1).then_inc(par_loaded, 16)
            sp.dma_start(ident[:, :], ident_d).then_inc(par_loaded, 16)

            for i in range(2):
                sp.sem_inc(at_stored[i], 16)
            sp.sem_inc(t_free, 2)

            def load_x(q, i):
                if not is_first(q):
                    sp.wait_ge(xn_stored[i], 16 * q)
                    sp.wait_ge(xT_ready, 8 * q - 4 + 4 * i)
                src = xt[ds((2 * q + i) * PIX, PIX), :].rearrange("(t p) c -> p t c", p=TT)
                sp.dma_start(xa[:, i, :, :], src).then_inc(x_loaded[i], 16)

            def store_xn(q, i):
                sp.wait_ge(ln_step, (q + 1) * LN_STEPS - (1 - i) * NT)
                dst = xn_d[ds((2 * q + i) * PIX, PIX), :].rearrange("(t p) c -> p t c", p=TT)
                sp.dma_start(dst, xa[:, i, :, :]).then_inc(xn_stored[i], 16)

            def store_attn(q, i):
                sp.wait_ge(alo_ready, 4 * q + 2 * i + 2)
                sp.dma_start(attn_d[:, :, ds((2 * q + i) * PIX, PIX)],
                             aTs[:, i, :, :]).then_inc(at_stored[i], 16)

            load_x(0, 0)
            load_x(0, 1)

            def load_w(k, sl):
                sp.dma_start(wst[sl][:, 0:KS * CMID],
                             w1p[ds(k, 1), :, :].rearrange("a p n -> (a p) n")).then_inc(w_loaded[sl], 16)

            def load_sweep(used, value):
                for k in range(W_SLOTS):
                    load_w(k, k)

                def group(j, pieces):
                    for sl in range(pieces):
                        sp.wait_ge(used, W_SLOTS * j + sl + value)
                        load_w(W_SLOTS * j + sl, sl)
                with sp.Fori(1, PIECES // W_SLOTS) as j:
                    group(j, W_SLOTS)
                group(PIECES // W_SLOTS, PIECES % W_SLOTS)

            load_sweep(w_seen, 1 - W_SLOTS)
            sp.wait_ge(w_seen, PIECES)
            load_sweep(t_free, 3 - W_SLOTS)

            def body(q):
                if is_first(q):
                    for i in range(2):
                        store_xn(0, i)
                    for i in range(2):
                        load_x(1, i)
                if not is_last(q):
                    for i in range(2):
                        store_xn(q + 1, i)
                    if not (isinstance(q, int) and q >= PAIRS - 2):
                        for i in range(2):
                            load_x(q + 2, i)
                if not is_first(q):
                    for i in range(2):
                        store_attn(q - 1, i)

            body(0)
            with sp.Fori(1, PAIRS - 2) as q:
                body(q)
            body(PAIRS - 2)
            body(PAIRS - 1)
            for i in range(2):
                store_attn(PAIRS - 1, i)
            for i in range(2):
                sp.wait_ge(xn_stored[i], 16 * PAIRS)
                sp.wait_ge(at_stored[i], 16 * (PAIRS + 1))

        @block.gpsimd
        def _(pool):
            def zero_pads(par, zeroed):
                for part in range(2):
                    v = V[:, par, part].rearrange("p k c i n -> p (k c i) n")
                    nc.gpsimd.memset(v[:, :, 0:3 * VT], 0.0).then_inc(zeroed, 1)
                    nc.gpsimd.memset(v[:, :, (VR - 3) * VT:VR * VT], 0.0).then_inc(zeroed, 1)
            zero_pads(0, pads_zeroed)
            c = ch[:, :, :, :, :].rearrange("p i c r w -> p (i c r) w")
            nc.gpsimd.memset(c[:, :, 0:3], 0.0).then_inc(pads_zeroed, 1)
            nc.gpsimd.memset(c[:, :, 3 + SIDE:CW], 0.0).then_inc(pads_zeroed, 1)
            nc.gpsimd.memset(mhalf[:, :], -0.5).then_inc(pads_zeroed, 1)
            nc.gpsimd.memset(ones[:, :], 1.0).then_inc(pads_zeroed, 1)
            nc.gpsimd.memset(E[:, :, NT * TAPS:], 0.0).then_inc(pads_zeroed, 1)
            for sl in range(W_SLOTS):
                nc.gpsimd.memset(wst[sl][:, KS * CMID:(KS + 1) * CMID], 0.0).then_inc(pads_zeroed, 1)
            pool.wait_ge(pads_zeroed, PADS)
            pool.wait_ge(bn_step, 1)
            nc.gpsimd.tensor_tensor(bnp[:, 6:7], bnp[:, 5:6], mhalf[0:TAPS, 0:1], ALU.pow).then_inc(bn_rstd, 1)

            def rsqrt(q, i):
                pool.wait_ge(ln_step, q * LN_STEPS + (i + 1) * LN_VE)
                nc.gpsimd.tensor_tensor(rstd[:, i, :], ve[:, i, :], mhalf[:, :], ALU.pow).then_inc(rstd_ready, 1)

            rsqrt(0, 0)
            rsqrt(0, 1)
            pool.wait_ge(wmax_ready, 1)
            nc.gpsimd.partition_all_reduce(sg[:, 1:2], sg[:, 0:1], P,
                                           bass.bass_isa.ReduceOp.max).then_inc(wmax_all, 1)
            add, sub = ALU.add, ALU.subtract

            def points_one(first, j, pieces):
                for sl in range(pieces):
                    s = Steps(pool, up_step, first + sl, UP_STEPS)
                    g = taps_of(sl)
                    pool.wait_ge(w_loaded[sl], 16 * (j + w_turns(sl) + 1))
                    pool.wait_ge(t_free, first + sl + 1)
                    s.did(nc.gpsimd.tensor_tensor(Au[:, 0], g[:, 0], g[:, 2], add))
                    s.did(nc.gpsimd.tensor_tensor(Au[:, 1], g[:, 1], g[:, 3], add))
                    s.settle()
                    s.did(nc.gpsimd.tensor_tensor(Tu[:, sl % 2, 0:2], Au[:, 0], Au[:, 1], add))
                    s.did(nc.gpsimd.tensor_tensor(Tu[:, sl % 2, 2:4], Au[:, 0], Au[:, 1], sub))
                    s.settle()
            piece_loop(pool, points_one)
            pool.wait_ge(t_free, PIECES + 2)
            zero_pads(1, odd_zeroed)

            with pool.Fori(1, PAIRS) as q:
                rsqrt(q, 0)
                rsqrt(q, 1)

        @block.scalar
        def _(act):
            act.wait_ge(pads_zeroed, PADS)
            act.wait_ge(par_loaded, 16 * 8)
            act.wait_ge(w2_turned, 2)
            nc.scalar.copy(w2T[:, :], pL[:, 0:TAPS]).then_inc(w2_ready, 1)
            nc.scalar.copy(brow[:, :, :], pL[0:1, None, P:P + TAPS].broadcast_to([1, NT, TAPS])
                           ).then_inc(w2_ready, 1)

            def plain(q, i, c):
                for h in range(2):
                    act.wait_ge(xT_ready, 8 * q + 4 * i + 2 * c + h + 1)
                    if not is_first(q):
                        act.wait_ge(v_step, (4 * q - 4 + 2 * i + c) * V_STEPS + V_READ)
                    nc.scalar.copy(
                        ch[:, i, c, h * (SIDE // 2):(h + 1) * (SIDE // 2), 3:3 + SIDE],
                        pX[:, h, 0:3 * TT].rearrange("p (r w) -> p r w", w=SIDE)
                    ).then_inc(xT_used, 1)

            def v_high(q, par, i, c):
                act.wait_ge(v_step, (4 * q + 2 * i + c + 1) * V_STEPS)
                if not (isinstance(q, int) and q < 2):
                    act.wait_ge(m_ready, NP * (q - 1))
                nc.scalar.copy(V[:, par, 0, :, c, i, 3 * VT:(3 + SIDE) * VT], vtile(work)
                               ).then_inc(vhi_ready, 1)

            def copy_m(q, k):
                act.wait_ge(m_ready, NP * q + 2 * k + 1)
                if not is_first(q):
                    act.wait_ge(y_step, (q - 1) * Y_STEPS + 2 * k + 2)
                nc.scalar.activation(msb[:, k, :], pM[:, 2 * k, 0:HALF], ACT.Copy,
                                     scale=point_norm(2 * k)).then_inc(m_copied, 1)

            def relu(q):
                act.wait_ge(y_step, (q + 1) * Y_STEPS)
                after(act, logits_ready, 2 * q)
                for r in range(4):
                    ins = nc.scalar.activation(k1[:, :].rearrange("p (n r) -> p r n", r=4)[:, r, :],
                                               ydata[:, r * HALF:(r + 1) * HALF], ACT.Relu,
                                               bias=b1s[:, 0:1], scale=sg[:, 4:5])
                ins.then_inc(k1_ready, 1)

            def exp(q, i):
                act.wait_ge(sm_step, q * SM_STEPS + i * SM_STEPS // 2 + 3)
                nc.scalar.activation(E[:, i, 0:NT * TAPS], E[:, i, 0:NT * TAPS], ACT.Exp).then_inc(exp_ready, 1)

            def a_high(q):
                for i in range(2):
                    act.wait_ge(at_stored[i], 16 * (q + 1))
                    for h in range(2):
                        act.wait_ge(aT_ready, 4 * q + 2 * i + h + 1)
                        nc.scalar.copy(aTs[:, i, 0, h * 3 * TT:(h + 1) * 3 * TT],
                                       a_bank(i, h)[0:TAPS, 0:3 * TT]).then_inc(ahi_ready, 1)

            for i in range(2):
                for c in range(CC):
                    plain(0, i, c)
                    v_high(0, 0, i, c)

            act.wait_ge(sig_step, SIG_STEPS)

            def u_high(first, j, pieces):
                for sl in range(pieces):
                    k = first + sl
                    g, hi = taps_of(sl), U[:, 0, :, ds(k, 1), :].rearrange("p u a n -> p u (a n)")
                    act.wait_ge(up_step, (k + 1) * UP_STEPS)
                    act.wait_ge(uv_step, (k + 1) * UV_STEPS)
                    nc.scalar.activation(hi[:, 0:TU], Tu[:, sl % 2], ACT.Copy, scale=sg[:, 3:4])
                    nc.scalar.activation(hi[:, TU:TU + 2], g[:, 0], ACT.Copy, scale=sg[:, 3:4])
                    nc.scalar.activation(hi[:, TU + 2:], g[:, 3, 0:1], ACT.Copy,
                                         scale=sg[:, 3:4]).then_inc(uhi_ready, 1)
            piece_loop(act, u_high)
            act.wait_ge(odd_zeroed, 4)

            def body(q, par):
                copy_m(q, 0)
                if not is_last(q):
                    for c in range(CC):
                        plain(q + 1, 0, c)
                    for c in range(CC):
                        v_high(q + 1, 1 - par, 0, c)
                if not is_first(q):
                    exp(q - 1, 0)
                if not is_last(q):
                    plain(q + 1, 1, 0)
                    v_high(q + 1, 1 - par, 1, 0)
                copy_m(q, 1)
                if not is_last(q):
                    plain(q + 1, 1, 1)
                    v_high(q + 1, 1 - par, 1, 1)
                if not is_first(q):
                    exp(q - 1, 1)
                    a_high(q - 1)
                relu(q)

            pair_loop(act, body)
            for i in range(2):
                exp(PAIRS - 1, i)
            a_high(PAIRS - 1)

        @block.vector
        def _(dve):
            tt, stt = nc.vector.tensor_tensor, nc.vector.scalar_tensor_tensor
            Et = E[:, :, 0:NT * TAPS].rearrange("p i (t k) -> p i t k", k=TAPS)

            def ln(q):
                s = Steps(dve, ln_step, q, LN_STEPS)
                for i in range(2):
                    dve.wait_ge(x_loaded[i], 16 * (q + 1))
                    for t in range(NT):
                        s.did(nc.vector.bn_stats(st[:, i, t, :], xa[:, i, t, :]))
                    s.settle()
                    carry(nc, spare[0:1, 0:1])
                    for t in range(NT):
                        s.did(nc.vector.bn_aggr(mv[:, i, t, :], st[:, i, t, :]))
                    s.settle()
                    s.did(nc.vector.tensor_scalar(ve[:, i, :], mv[:, i, :, 1], 1e-6, None, ALU.add))
                for i in range(2):
                    dve.wait_ge(rstd_ready, 2 * q + i + 1)
                    for t in range(NT):
                        s.did(nc.vector.tensor_scalar(xa[:, i, t, :], xa[:, i, t, :], mv[:, i, t, 0:1],
                                                      rstd[:, i, t:t + 1], ALU.subtract, ALU.mult))
                s.at(LN_STEPS)

            o = 0
            E1 = work[:, 0:SIDE * CW].rearrange("p (r w) -> p r w", w=CW)
            o += SIDE * CW
            S = work[:, o:o + SIDE * 28].rearrange("p (r w) -> p r w", w=28)
            o += SIDE * 28
            Ux = work[:, o:o + SIDE * 14].rearrange("p (w r t) -> p w r t", r=SIDE, w=2)
            o += SIDE * 14
            Sd = work[:, o:o + SIDE * 14].rearrange("p (r t w) -> p r t w", r=SIDE, w=2)
            T = vtile(work).rearrange("p k (r t) -> p k r t", t=VT)
            S4 = S.rearrange("p r (t w) -> p r t w", w=4)
            E4 = E1.rearrange("p r (t w) -> p r t w", w=4)

            def v_head(q, i, c):
                s = Steps(dve, v_step, 4 * q + 2 * i + c, V_STEPS)
                D = ch[:, i, c, :, :]
                D2 = D.rearrange("p r (t w) -> p r t w", w=2)
                s.settle()
                dve.wait_ge(xT_used, 8 * q + 4 * i + 2 * c + 2)
                s.did(stt(E1[:, :, 0:30], D[:, :, 0:30], 0.5, D[:, :, 1:31], ALU.mult, ALU.add))
                s.did(stt(Sd.rearrange("p r t w -> p r (t w)"), D2[:, :, 0:14, 1], -4.0,
                          D2[:, :, 1:15, 1], ALU.mult, ALU.add))
                s.at(V_READ)
                s.settle()
                s.did(stt(S, E1[:, :, 0:28], -4.0, E1[:, :, 2:30], ALU.mult, ALU.add))
                s.did(tt(Ux[:, 0], E4[:, :, 0:VT, 3], E4[:, :, 0:VT, 1], ALU.subtract))
                s.did(tt(Ux[:, 1], E4[:, :, 1:VT + 1, 0], E4[:, :, 0:VT, 2], ALU.subtract))
                s.at(V_HEAD)

            def v_data(q, i, c):
                s = Steps(dve, v_step, 4 * q + 2 * i + c, V_STEPS, V_HEAD)
                s.settle()
                s.did(tt(T[:, 0], S4[:, :, :, 2], S4[:, :, :, 1], ALU.add))
                s.did(tt(T[:, 1], S4[:, :, :, 2], S4[:, :, :, 1], ALU.subtract))
                s.did(stt(T[:, 2], Ux[:, 0], 2.0, Ux[:, 1], ALU.mult, ALU.add))
                s.did(stt(T[:, 3], Ux[:, 0], -2.0, Ux[:, 1], ALU.mult, ALU.add))
                s.did(tt(T[:, 4], Sd[:, :, :, 1], Sd[:, :, :, 0], ALU.subtract))
                s.did(tt(T[:, 5], S4[:, :, :, 2], S4[:, :, :, 0], ALU.subtract))
                s.did(tt(T[:, 6], S4[:, :, :, 3], S4[:, :, :, 1], ALU.subtract))
                s.at(V_STEPS)

            def v_low(q, par, i, c):
                r = 4 * q + 2 * i + c
                dve.wait_ge(vhi_ready, r + 1)
                rows = slice(3 * VT, (3 + SIDE) * VT)
                tt(V[:, par, 1, :, c, i, rows], vtile(work), V[:, par, 0, :, c, i, rows],
                   ALU.subtract).then_inc(vlo_ready, 1)
                dve.wait_ge(vlo_ready, r + 1)

            y = [ydata[:, r * HALF:(r + 1) * HALF] for r in range(4)]

            def y_points(q, k):
                s = Steps(dve, y_step, q, Y_STEPS, 2 * k)
                dve.wait_ge(m_copied, 2 * q + k + 1)
                dve.wait_ge(m_ready, NP * q + 2 * k + 2)
                m = pM[:, 2 * k + 1, 0:HALF]
                norm = point_norm(2 * k + 1)
                s.did(stt(sd[:, 2 * k, :], m, norm, msb[:, k, :], ALU.mult, ALU.add))
                s.did(stt(sd[:, 2 * k + 1, :], m, -norm, msb[:, k, :], ALU.mult, ALU.add))

            def y_mid(q):
                s = Steps(dve, y_step, q, Y_STEPS, 4)
                s.settle()
                after(dve, k1_ready, q)
                s.did(tt(y[0], sd[:, 0, :], sd[:, 2, :], ALU.add))
                s.did(stt(y[1], sd[:, 3, :], 2.0, sd[:, 1, :], ALU.mult, ALU.add))
                s.did(stt(y[2], sd[:, 2, :], 4.0, sd[:, 0, :], ALU.mult, ALU.add))
                s.did(stt(y[3], sd[:, 3, :], 8.0, sd[:, 1, :], ALU.mult, ALU.add))
                s.settle()
                dve.wait_ge(m_ready, NP * q + 5)
                for r in range(4):
                    s.did(stt(y[r], pM[:, 0, 0:HALF], (-0.5) ** r * point_norm(4), y[r], ALU.mult, ALU.add))

            def y_end(q):
                s = Steps(dve, y_step, q, Y_STEPS, 12)
                s.settle()
                dve.wait_ge(m_ready, NP * q + 6)
                s.did(stt(y[0], pM[:, 1, 0:HALF], point_norm(5), y[0], ALU.mult, ALU.add))
                dve.wait_ge(m_ready, NP * q + 7)
                s.did(tt(y[3], pM[:, 2, 0:HALF], y[3], ALU.add))
                s.at(Y_STEPS)

            def shift_logits(q, i):
                s = Steps(dve, sm_step, q, SM_STEPS, i * SM_STEPS // 2)
                L = pL[0:TT, 0:NT * TAPS].rearrange("p (t k) -> p t k", t=NT)
                dve.wait_ge(logits_ready, 2 * q + i + 1)
                s.did(nc.vector.tensor_reduce(mx[:, i, :], L, AX.X, ALU.max))
                s.settle()
                s.did(nc.vector.tensor_scalar(mx[:, i, :], mx[:, i, :], 0.0, None, ALU.max))
                s.settle()
                s.did(stt(Et[:, i], L, 0.0, mx[:, i, :, None].broadcast_to([TT, NT, TAPS]),
                          ALU.max, ALU.subtract))

            def normalise(q, i):
                s = Steps(dve, sm_step, q, SM_STEPS, i * SM_STEPS // 2 + 3)
                dve.wait_ge(exp_ready, 2 * q + i + 1)
                s.did(nc.vector.tensor_reduce(sm[:, i, :], Et[:, i], AX.X, ALU.add))
                s.settle()
                s.did(nc.vector.reciprocal(sm[:, i, :], sm[:, i, :]))
                s.settle()
                s.did(nc.vector.tensor_scalar(sm[:, i, :], sm[:, i, :], ATT_SCALE, None, ALU.mult))
                s.settle()
                s.did(tt(Et[:, i], Et[:, i], sm[:, i, :, None].broadcast_to([TT, NT, TAPS]), ALU.mult))

            def a_low(q):
                for i in range(2):
                    for h in range(2):
                        dve.wait_ge(ahi_ready, 4 * q + 2 * i + h + 1)
                        cols = slice(h * 3 * TT, (h + 1) * 3 * TT)
                        tt(aTs[:, i, 1, cols], a_bank(i, h)[0:TAPS, 0:3 * TT], aTs[:, i, 0, cols],
                           ALU.subtract).then_inc(alo_ready, 1)

            dve.wait_ge(par_loaded, 16 * 8)
            s = Steps(dve, bn_step, 0, BN_STEPS)
            s.did(nc.vector.tensor_scalar(bnp[:, 5:6], bnp[:, 4:5], 1e-5, None, ALU.add))
            s.did(tt(bnp[:, 0:1], bnp[:, 0:1], bnp[:, 3:4], ALU.subtract))
            dve.wait_ge(bn_rstd, 1)
            s.did(tt(bnp[:, 7:8], bnp[:, 6:7], bnp[:, 1:2], ALU.mult))
            s.settle()
            s.did(nc.vector.tensor_scalar(w2s[:, :], w2s[:, :], bnp[:, 7:8], None, ALU.mult))
            s.did(stt(bnp[:, 0:1], bnp[:, 0:1], bnp[:, 7:8], bnp[:, 2:3], ALU.mult, ALU.add))
            s.at(BN_STEPS)

            ln(0)
            dve.wait_ge(pads_zeroed, PADS)
            for i in range(2):
                for c in range(CC):
                    v_head(0, i, c)
                    if i + c > 0:
                        v_low(0, 0, (2 * i + c - 1) // 2, (2 * i + c - 1) % 2)
                    v_data(0, i, c)
            v_low(0, 0, 1, 1)

            def magnitudes(first, j, pieces):
                for sl in range(pieces):
                    dve.wait_ge(w_loaded[sl], 16 * (j + 1))
                    nc.vector.tensor_reduce(mxp[:, ds(first + sl, 1)], wst[sl][:, 0:KS * CMID], AX.X, ALU.max,
                                            apply_absolute_value=True).then_inc(w_seen, 1)
            piece_loop(dve, magnitudes)
            dve.wait_ge(w_seen, PIECES)
            nc.vector.tensor_reduce(sg[:, 0:1], mxp[:, :], AX.X, ALU.max).then_inc(wmax_ready, 1)
            dve.wait_ge(wmax_all, 1)
            s = Steps(dve, sig_step, 0, SIG_STEPS)
            s.did(nc.vector.tensor_scalar(sg[:, 1:2], sg[:, 1:2], 2.0 ** -100, 2.0 ** 100, ALU.max, ALU.min))
            s.settle()
            s.did(nc.vector.tensor_scalar(sg[:, 2:3].bitcast(U32), sg[:, 1:2].bitcast(U32), 0x7F800000, None,
                                          ALU.bitwise_and))
            s.settle()
            s.did(nc.vector.tensor_scalar(sg[:, 4:5], sg[:, 2:3], 2.0 ** -10, None, ALU.mult))
            s.settle()
            s.did(nc.vector.reciprocal(sg[:, 3:4], sg[:, 4:5]))
            s.settle()
            s.at(SIG_STEPS)

            def u_points(k, j, sl):
                A2, A3, g = Au[:, 2], Au[:, 3], taps_of(sl)

                def pt(i):
                    return Tu[:, sl % 2, 2 * i:2 * i + 2]

                s = Steps(dve, uv_step, k, UV_STEPS)
                dve.wait_ge(w_loaded[sl], 16 * (j + w_turns(sl) + 1))
                dve.wait_ge(t_free, k + 1)
                s.did(stt(A2, g[:, 2], 4.0, g[:, 0], ALU.mult, ALU.add))
                s.did(stt(A3, g[:, 3], 4.0, g[:, 1], ALU.mult, ALU.add))
                s.did(stt(pt(4), g[:, 3], -0.5, g[:, 2], ALU.mult, ALU.add))
                s.settle()
                s.did(stt(pt(2), A3, 2.0, A2, ALU.mult, ALU.add))
                s.did(stt(pt(3), A3, -2.0, A2, ALU.mult, ALU.add))
                s.did(stt(pt(4), pt(4), -0.5, g[:, 1], ALU.mult, ALU.add))
                s.settle()
                s.did(stt(pt(4), pt(4), -0.5, g[:, 0], ALU.mult, ALU.add))
                s.at(UV_STEPS)
                s.settle()

            def u_low(k, sl):
                g = taps_of(sl)
                hi = U[:, 0, :, ds(k, 1), :].rearrange("p u a n -> p u (a n)")
                lo = U[:, 1, :, ds(k, 1), :].rearrange("p u a n -> p u (a n)")
                dve.wait_ge(uhi_ready, k + 1)
                stt(lo[:, TU:TU + 2], g[:, 0], sg[:, 3:4], hi[:, TU:TU + 2], ALU.mult, ALU.subtract)
                stt(lo[:, TU + 2:], g[:, 3, 0:1], sg[:, 3:4], hi[:, TU + 2:], ALU.mult, ALU.subtract)
                stt(lo[:, 0:TU], Tu[:, sl % 2], sg[:, 3:4], hi[:, 0:TU], ALU.mult,
                    ALU.subtract).then_inc(t_free, 1)

            def u_pieces(first, j, pieces):
                for sl in range(pieces):
                    u_points(first + sl, j, sl)
                    if sl > 0:
                        u_low(first + sl - 1, sl - 1)
                u_low(first + pieces - 1, pieces - 1)
            piece_loop(dve, u_pieces)
            dve.wait_ge(odd_zeroed, 4)

            def body(q, par):
                if not is_last(q):
                    ln(q + 1)
                    v_head(q + 1, 0, 0)
                    v_data(q + 1, 0, 0)
                    v_head(q + 1, 0, 1)
                    v_low(q + 1, 1 - par, 0, 0)
                    v_data(q + 1, 0, 1)
                if not is_first(q):
                    shift_logits(q - 1, 0)
                if not is_last(q):
                    v_low(q + 1, 1 - par, 0, 1)
                y_points(q, 0)
                if not is_last(q):
                    v_head(q + 1, 1, 0)
                    v_data(q + 1, 1, 0)
                if not is_first(q):
                    normalise(q - 1, 0)
                if not is_last(q):
                    v_low(q + 1, 1 - par, 1, 0)
                    v_head(q + 1, 1, 1)
                    v_data(q + 1, 1, 1)
                if not is_first(q):
                    shift_logits(q - 1, 1)
                if not is_last(q):
                    v_low(q + 1, 1 - par, 1, 1)
                if not is_first(q):
                    normalise(q - 1, 1)
                y_points(q, 1)
                y_mid(q)
                if not is_first(q):
                    a_low(q - 1)
                y_end(q)

            pair_loop(dve, body)
            q = PAIRS - 1
            for i in range(2):
                shift_logits(q, i)
                normalise(q, i)
            a_low(q)

        @block.tensor
        def _(pe):
            pe.wait_ge(par_loaded, 16 * 8)
            pe.wait_ge(bn_step, BN_STEPS)
            nc.tensor.transpose(pL[:, 0:TAPS], w2s[:, :], ident[0:TAPS, 0:TAPS]).then_inc(w2_turned, 1)
            nc.tensor.transpose(pL[0:1, P:P + TAPS], bnp[:, 0:1], ident[0:TAPS, 0:TAPS]).then_inc(w2_turned, 1)

            def turn_x(q, i, c):
                pe.wait_ge(ln_step, (q + 1) * LN_STEPS - (1 - i) * NT)
                for h in range(2):
                    if not (is_first(q) and i == 0 and c == 0):
                        pe.wait_ge(xT_used, 8 * q + 4 * i + 2 * c + h - 1)
                    for t in range(3):
                        last = nc.tensor.transpose(pX[:, h, t * TT:(t + 1) * TT],
                                                   xa[:, i, 3 * h + t, c * P:(c + 1) * P], ident[0:TT, 0:TT])
                    last.then_inc(xT_ready, 1)

            def conv(q, par, k):
                if k == 0:
                    pe.wait_ge(vlo_ready, 4 * (q + 1))
                if k < 3:
                    after(pe, y_step, q * Y_STEPS - (2, 1, 0)[k])
                elif k == 4:
                    pe.wait_ge(m_copied, 2 * q + 1)
                elif k == 5:
                    pe.wait_ge(y_step, q * Y_STEPS + 2)
                elif k == 6:
                    pe.wait_ge(m_copied, 2 * q + 2)
                work_list = [(g, ky, c, a, b) for g in range(2) if 2 * k + g < UNITS
                             for ky in range(KS) for c in range(CC) for a, b in ((0, 0), (0, 1), (1, 0))]
                for n, (g, ky, c, a, b) in enumerate(work_list):
                    v = V[:, par, b, k, c].rearrange("p i (r t) -> p i r t", t=VT)
                    last = nc.tensor.matmul(pM[:, k % 4, 0:HALF], U[:, a, 2 * k + g, c * KS + ky, :],
                                            v[:, :, ky:ky + SIDE, g:g + QT],
                                            start=(n == 0), stop=(n == len(work_list) - 1))
                last.then_inc(m_ready, 1)

            def logits(q, i):
                if i == 0:
                    pe.wait_ge(k1_ready, q + 1)
                if i == 1:
                    pe.wait_ge(sm_step, q * SM_STEPS + 3)
                L = pL[0:TT, 0:NT * TAPS]
                nc.tensor.matmul(L, ones[:, :], brow[:, :, :].rearrange("p t k -> p (t k)"),
                                 start=True, stop=False)
                for t in range(NT):
                    last = nc.tensor.matmul(L[:, t * TAPS:(t + 1) * TAPS],
                                            k1[:, (i * NT + t) * TT:(i * NT + t + 1) * TT], w2T[:, :],
                                            start=False, stop=(t == NT - 1))
                last.then_inc(logits_ready, 1)

            def turn_a(q, turned):
                for i in range(2):
                    pe.wait_ge(sm_step, q * SM_STEPS + (SM_STEPS // 2 + 3, SM_STEPS)[i])
                    if i == 1:
                        pe.wait_ge(xT_used, 8 * turned)
                    for h in range(2):
                        for t in range(3):
                            last = nc.tensor.transpose(a_bank(i, h)[0:EPAD, t * TT:(t + 1) * TT],
                                                       E[:, i, (3 * h + t) * TAPS:(3 * h + t) * TAPS + EPAD],
                                                       ident[0:TT, 0:TT])
                        last.then_inc(aT_ready, 1)

            for i in range(2):
                for c in range(CC):
                    turn_x(0, i, c)
            pe.wait_ge(w2_ready, 2)
            pe.wait_ge(t_free, PIECES + 2)

            def body(q, par):
                conv(q, par, 0)
                if not is_last(q):
                    turn_x(q + 1, 0, 0)
                if not is_first(q):
                    logits(q - 1, 0)
                if not is_last(q):
                    turn_x(q + 1, 0, 1)
                conv(q, par, 1)
                if not is_last(q):
                    turn_x(q + 1, 1, 0)
                conv(q, par, 2)
                if not is_last(q):
                    turn_x(q + 1, 1, 1)
                if not is_first(q):
                    logits(q - 1, 1)
                for k in range(3, NP - 1):
                    conv(q, par, k)
                if not is_first(q):
                    turn_a(q - 1, q + 1 if is_last(q) else q + 2)
                conv(q, par, NP - 1)
                if not is_first(q):
                    pe.wait_ge(alo_ready, 4 * q)

            pair_loop(pe, body)
            logits(PAIRS - 1, 0)
            logits(PAIRS - 1, 1)
            turn_a(PAIRS - 1, PAIRS)


BLK = 3
R = KS // 2
EDGE = [w for w in range(SIDE) if w < R or w >= SIDE - R]
G0 = TT + SIDE * (TR - 1 - R - 1) + (SIDE - 1 - R)
GW = G0 + SIDE * (R - 1) + R + TT + TT
HHS = [(d, h) for d in (-1, 0, 1) for h in range(TR) if (d, h) not in ((-1, TR - 1), (1, 0))]
BT = 4 * NT
SLOT = 8
T_STEPS = 4 + 3 * NT + 1


def spread_table():
    import numpy as np
    g = np.zeros((TAPS, len(EDGE) + 1, GW), np.float16)
    for v, w in enumerate([SIDE // 2] + EDGE):
        for ki in range(KS):
            for kj in range(KS):
                if 0 <= w + kj - R < SIDE:
                    g[ki * KS + kj, v, SIDE * ki + kj + G0] = 1
    return g


def attend_phase(nc, xt, xn_d, attn_d, spread_d, t_d, tn_d, acc):
    with ExitStack() as ctx:
        def sb(name, shape, dt):
            return ctx.enter_context(nc.sbuf_tensor(name, shape, dt))

        def sem(name):
            return ctx.enter_context(nc.semaphore(name))

        G = sb("G", list(spread_d.shape), F16)
        aT = sb("aT", [TAPS, 2, SB], F16)
        A = sb("A", [TT, BLK, 2 * BT, TT], F16)
        xr = sb("xr", [TT, 2, NT, C], F32)
        xn = sb("xn", [TT, 2, NT, C], F32)
        X = sb("X", [TT, 2, NT, 2, C], F16)
        ts_ = sb("ts", [TT, 2, NT, C], F32)
        tn = sb("tn", [TT, 2, NT, C], F32)
        spare = sb("spare2", [1, 1], F32)
        st = sb("st2", [TT, NT, 6], F32)
        mv = sb("mv2", [TT, NT, 2], F32)
        ve = sb("ve2", [TT, NT], F32)
        rstd = sb("rstd2", [TT, NT], F32)
        mhalf = sb("mhalf2", [TT, NT], F32)
        pS = [ctx.enter_context(nc.psum_tensor(f"pS{g}", [P, 3, 512], F32)) for g in range(2)]
        pO = ctx.enter_context(nc.psum_tensor("pO", [P, 2, 512], F32))

        g_loaded = sem("g_loaded")
        at_loaded = sem("at_loaded")
        xr_loaded = [sem(f"xr_loaded{s}") for s in range(2)]
        xn_loaded = [sem(f"xn_loaded{s}") for s in range(2)]
        a_zeroed = sem("a_zeroed")
        spread = sem("spread")
        a_by_act = sem("a_by_act")
        a_by_dve = sem("a_by_dve")
        xhi_ready = sem("xhi_ready")
        o_ready = sem("o_ready")
        t_step = sem("t_step")
        rstd_ready2 = sem("rstd_ready2")
        acc_step = sem("acc_step")
        t_stored = [sem(f"t_stored{s}") for s in range(2)]
        tn_stored = [sem(f"tn_stored{s}") for s in range(2)]
        NU = len(HHS)

        def batch_loop(eng, body):
            body(0)
            with eng.Fori(1, B) as b:
                body(b)

        block = ctx.enter_context(nc.Block())

        @block.sync
        def _(sp):
            sp.dma_start(G[:, :, :], spread_d).then_inc(g_loaded, 16)

            def load(b, m):
                n, s = 4 * b + m, m % 2
                if not (is_first(b) and m < 2):
                    sp.wait_ge(t_step, (n - 2) * T_STEPS + 4)
                rows = ds(n * PIX, PIX)
                sp.dma_start(xn[:, s], xn_d[rows, :].rearrange("(t p) c -> p t c", p=TT)).then_inc(xn_loaded[s], 16)
                sp.dma_start(xr[:, s], xt[rows, :].rearrange("(t p) c -> p t c", p=TT)).then_inc(xr_loaded[s], 16)

            def body(b):
                if not is_first(b):
                    sp.wait_ge(spread, NU * b)
                sp.dma_start(aT[:, :, :], attn_d[:, :, ds(b * SB, SB)]).then_inc(at_loaded, 16)
                for m in range(4):
                    load(b, m)
            batch_loop(sp, body)

        @block.gpsimd
        def _(pool):
            nc.gpsimd.memset(A[:, 0, :, (TR - 1) * SIDE:TR * SIDE], 0.0).then_inc(a_zeroed, 1)
            nc.gpsimd.memset(A[:, 2, :, 0:SIDE], 0.0).then_inc(a_zeroed, 1)
            nc.gpsimd.memset(mhalf[:, :], -0.5).then_inc(a_zeroed, 1)
            pool.wait_ge(a_zeroed, 3)

            def body(b):
                for m in range(4):
                    n, s = 4 * b + m, m % 2
                    pool.wait_ge(t_step, n * T_STEPS + 4 + 2 * NT + 1)
                    nc.gpsimd.tensor_tensor(rstd[:, :], ve[:, :], mhalf[:, :], ALU.pow).then_inc(rstd_ready2, 1)
                    after(pool, acc_step, n)
                    pool.wait_ge(t_step, (n + 1) * T_STEPS)
                    rows = ds(n * PIX, PIX)
                    pool.dma_start(t_d[rows, :].rearrange("(t p) c -> p t c", p=TT), ts_[:, s]).then_inc(t_stored[s], 16)
                    pool.dma_start(tn_d[rows, :].rearrange("(t p) c -> p t c", p=TT), tn[:, s]).then_inc(tn_stored[s], 16)
                    a = acc[:, ds(b, 1)].rearrange("p b t c -> p (b t) c")
                    if m == 0:
                        nc.gpsimd.tensor_copy(a, tn[:, s]).then_inc(acc_step, 1)
                    else:
                        nc.gpsimd.tensor_tensor(a, a, tn[:, s], ALU.add).then_inc(acc_step, 1)
            batch_loop(pool, body)
            for s in range(2):
                pool.wait_ge(t_stored[s], 16 * IMGS // 2)
                pool.wait_ge(tn_stored[s], 16 * IMGS // 2)

        def spread_out(eng, copy, b, parity, done):
            eng.wait_ge(a_zeroed, 3)
            for u in range(parity, NU, 2):
                d, h = HHS[u]
                eng.wait_ge(spread, NU * b + u + 1)
                if u == parity and not is_first(b):
                    eng.wait_ge(o_ready, 12 * b)
                dst = A[:, d + 1, :, h * SIDE:(h + 1) * SIDE].rearrange("p n (k w) -> p k n w", w=SLOT)
                src = pS[parity][0:TT, :, 0:SLOT * 2 * BT].rearrange("p k (w n) -> p k n w", w=SLOT)
                copy(dst, src).then_inc(done, 1)

        @block.scalar
        def _(act):
            def body(b):
                spread_out(act, nc.scalar.copy, b, 0, a_by_act)
                for m in range(4):
                    n, s = 4 * b + m, m % 2
                    act.wait_ge(xn_loaded[s], 16 * (2 * b + m // 2 + 1))
                    if not (is_first(b) and m < 2):
                        act.wait_ge(o_ready, 3 * (n - 1))
                    nc.scalar.copy(X[:, s, :, 0, :], xn[:, s]).then_inc(xhi_ready, 1)
            batch_loop(act, body)

        @block.vector
        def _(dve):
            def body(b):
                spread_out(dve, nc.vector.tensor_copy, b, 1, a_by_dve)
                for m in range(4):
                    n, sl = 4 * b + m, m % 2
                    s = Steps(dve, t_step, n, T_STEPS)
                    dve.wait_ge(xhi_ready, n + 1)
                    s.did(nc.vector.tensor_tensor(X[:, sl, :, 1, :], xn[:, sl], X[:, sl, :, 0, :], ALU.subtract))
                    dve.wait_ge(xr_loaded[sl], 16 * (2 * b + m // 2 + 1))
                    if not (is_first(b) and m < 2):
                        dve.wait_ge(t_stored[sl], 16 * (2 * b + m // 2))
                        dve.wait_ge(tn_stored[sl], 16 * (2 * b + m // 2))
                        dve.wait_ge(acc_step, n - 1)
                    for u in range(3):
                        dve.wait_ge(o_ready, 3 * n + u + 1)
                        s.did(nc.vector.scalar_tensor_tensor(
                            ts_[:, sl, 2 * u:2 * u + 2, :].rearrange("p t c -> p (t c)"),
                            pO[0:TT, (3 * m + u) % 2, :], 1.0 / ATT_SCALE,
                            xr[:, sl, 2 * u:2 * u + 2, :].rearrange("p t c -> p (t c)"), ALU.mult, ALU.add))
                    s.settle()
                    for t in range(NT):
                        s.did(nc.vector.bn_stats(st[:, t, :], ts_[:, sl, t, :]))
                    s.settle()
                    carry(nc, spare[0:1, 0:1])
                    for t in range(NT):
                        s.did(nc.vector.bn_aggr(mv[:, t, :], st[:, t, :]))
                    s.settle()
                    s.did(nc.vector.tensor_scalar(ve[:, :], mv[:, :, 1], 1e-5, None, ALU.add))
                    dve.wait_ge(rstd_ready2, n + 1)
                    for t in range(NT):
                        s.did(nc.vector.tensor_scalar(tn[:, sl, t, :], ts_[:, sl, t, :], mv[:, t, 0:1],
                                                      rstd[:, t:t + 1], ALU.subtract, ALU.mult))
                    s.at(T_STEPS)
            batch_loop(dve, body)

        @block.tensor
        def _(pe):
            pe.wait_ge(g_loaded, 16)

            def spread_taps(b):
                pe.wait_ge(at_loaded, 16 * (b + 1))
                a = aT[:, :, :].rearrange("p a (n i) -> p (a n) i", i=TT)
                for u, (d, h) in enumerate(HHS):
                    pe.wait_ge(a_by_dve if u % 2 else a_by_act, (NU // 2) * b + u // 2)
                    for w in range(SIDE):
                        at = TT * d - SIDE * (h - R) - (w - R) + G0
                        v = 1 + EDGE.index(w) if w in EDGE else 0
                        o = (w % SLOT) * 2 * BT
                        last = nc.tensor.matmul(pS[u % 2][0:TT, w // SLOT, o:o + 2 * BT],
                                                G[:, v, at:at + TT], a[:, :, h * SIDE + w],
                                                start=True, stop=True)
                    last.then_inc(spread, 1)

            def attend(b, m):
                n, s = 4 * b + m, m % 2
                pe.wait_ge(t_step, n * T_STEPS + 1)
                for u in range(3):
                    if u < 2 and is_first(b) and m == 0:
                        pass
                    elif u == 2:
                        pe.wait_ge(t_step, n * T_STEPS + 2)
                    else:
                        pe.wait_ge(t_step, (n - 1) * T_STEPS + 3 + u)
                    for t in (2 * u, 2 * u + 1):
                        terms = [(d, a, x) for d in (-1, 0, 1) if 0 <= t + d < NT
                                 for a, x in ((0, 0), (0, 1), (1, 0))]
                        for k, (d, a, x) in enumerate(terms):
                            last = nc.tensor.matmul(pO[0:TT, (3 * m + u) % 2, (t % 2) * C:(t % 2 + 1) * C],
                                                    A[:, d + 1, a * BT + m * NT + t, :], X[:, s, t + d, x, :],
                                                    start=(k == 0), stop=(k == len(terms) - 1))
                    last.then_inc(o_ready, 1)

            def body(b):
                spread_taps(b)
                pe.wait_ge(a_by_act, (NU // 2) * (b + 1))
                pe.wait_ge(a_by_dve, (NU // 2) * (b + 1))
                for m in range(4):
                    attend(b, m)
            batch_loop(pe, body)


EXPERTS, TOPK, FH = 8, 2, 512
FB = FH // P
CAPACITY = float(-(-N * 5 // (4 * EXPERTS)))
CT = 3
CN = CT * P
CHUNKS = SB // CN
JB = TOPK * FB
R_STEPS = 24
Z_VE = 3 * CT + 1
Z_ALL = 5 * CT + 1


def ffn_phase(nc, acc, t_d, tn_d, wr, br, ew1, eb1, ew2, eb2, gamma, beta, ident_d, out):
    with ExitStack() as ctx:
        def sb(name, shape, dt):
            return ctx.enter_context(nc.sbuf_tensor(name, shape, dt))

        def sem(name):
            return ctx.enter_context(nc.semaphore(name))

        ident = sb("ident3", [P, P], F32)
        wrs = sb("wrs", [P, CC, EXPERTS], F32)
        brs = sb("brs", [1, EXPERTS], F32)
        ones = sb("ones3", [P, P], F32)
        mean = sb("mean3", [P, CC * B], F32)
        r = sb("r", [B, 8, EXPERTS], F32)
        rc = sb("rc", [B, 8], F32)
        idx = sb("idx", [B, EXPERTS], U32)
        wv = sb("wv", [B, TOPK], F32)
        irow = sb("irow", [1, B * TOPK], U32)
        wrow = sb("wrow", [1, B * TOPK], F32)
        wbc = sb("wbc", [P, B * TOPK], F32)
        gam = sb("gam", [P, C], F32)
        bet = sb("bet", [P, C], F32)
        w1r = sb("w1r", [P, TOPK, CC, FH], F32)
        w2r = sb("w2r", [P, TOPK, FB, C], F32)
        b1r = sb("b1r", [P, TOPK, FB], F32)
        b2r = sb("b2r", [P, TOPK, C], F32)
        w1h = sb("w1h", [P, TOPK, CC, FH], F32R)
        w1l = sb("w1l", [P, TOPK, CC, FH], F32R)
        w2h = sb("w2h", [P, TOPK, FB, C], F32R)
        w2l = sb("w2l", [P, TOPK, FB, C], F32R)
        b1c = sb("b1c", [P, TOPK, FB], F32)
        b2c = sb("b2c", [P, 2, C], F32)
        tk = sb("tk", [P, 2, CT, C], F32)
        tnk = sb("tnk", [P, 2, CT, C], F32)
        tb = sb("tb", [P, 2, CT, C], F32)
        tnb = sb("tnb", [P, 2, CT, C], F32)
        xh = sb("xh", [P, 2, CC, CN], F32R)
        xl = sb("xl", [P, 2, CC, CN], F32R)
        gf = sb("gf", [P, 2, CN], F32)
        gh = sb("gh", [P, 2, JB, CN], F32R)
        gl = sb("gl", [P, 2, JB, CN], F32R)
        z = sb("z", [P, CT, C], F32)
        o = sb("o", [P, 2, CT, C], F32)
        spare = sb("spare3", [1, 1], F32)
        st = sb("st3", [P, CT, 6], F32)
        mv = sb("mv3", [P, CT, 2], F32)
        ve = sb("ve3", [P, CT], F32)
        rstd = sb("rstd3", [P, CT], F32)
        mhalf = sb("mhalf3", [P, CT], F32)
        pT = ctx.enter_context(nc.psum_tensor("pT", [P, CC, 512], F32))
        pH = ctx.enter_context(nc.psum_tensor("pH", [P, 4, 512], F32))
        pY = ctx.enter_context(nc.psum_tensor("pY", [P, 2, 512], F32))

        c_loaded = sem("c_loaded")
        c_set = sem("c_set")
        sums_ready = sem("sums_ready")
        r_pe = sem("r_pe")
        r_step = sem("r_step")
        r_exp = sem("r_exp")
        row_loaded = sem("row_loaded")
        w1_loaded = sem("w1_loaded")
        w2_loaded = sem("w2_loaded")
        w1hi_ready = sem("w1hi_ready")
        w2hi_ready = sem("w2hi_ready")
        w1_step = sem("w1_step")
        w2_step = sem("w2_step")
        bias_step = sem("bias_step")
        tk_loaded = [sem(f"tk_loaded{s}") for s in range(2)]
        tnk_loaded = [sem(f"tnk_loaded{s}") for s in range(2)]
        x_turned = sem("x_turned")
        xh_ready = sem("xh_ready")
        xl_ready = sem("xl_ready")
        h_ready = sem("h_ready")
        gelu_done = sem("gelu_done")
        g_step = sem("g_step")
        y_ready = sem("y_ready3")
        bias_added = sem("bias_added")
        z_step = sem("z_step")
        rstd_ready = sem("rstd_ready3")
        out_stored = [sem(f"out_stored{s}") for s in range(2)]

        def batch_loop(eng, body):
            body(0)
            with eng.Fori(1, B - 1) as b:
                body(b)
            body(B - 1)

        def later(b, m, by):
            if m + by < CHUNKS:
                return b, m + by
            return None if isinstance(b, int) and b == B - 1 else (b + 1, m + by - CHUNKS)

        block = ctx.enter_context(nc.Block())

        @block.sync
        def _(sp):
            sp.dma_start(ident[:, :], ident_d).then_inc(c_loaded, 16)
            sp.dma_start(wrs[:, :, :], wr.rearrange("(c p) e -> p c e", p=P)).then_inc(c_loaded, 16)
            sp.dma_start(brs[:, :], br).then_inc(c_loaded, 16)
            sp.dma_start(gam[:, :], gamma.broadcast_to([P, C])).then_inc(c_loaded, 16)
            sp.dma_start(bet[:, :], beta.broadcast_to([P, C])).then_inc(c_loaded, 16)

            def load_chunk(b, m):
                n, s = CHUNKS * b + m, m % 2
                if not (is_first(b) and m < 2):
                    sp.wait_ge(x_turned, 2 * (n - 1))
                    sp.wait_ge(bias_added, 2 * (n - 1))
                rows = ds(n * CN, CN)
                sp.dma_start(tnk[:, s], tn_d[rows, :].rearrange("(t p) c -> p t c", p=P)).then_inc(tnk_loaded[s], 16)
                sp.dma_start(tk[:, s], t_d[rows, :].rearrange("(t p) c -> p t c", p=P)).then_inc(tk_loaded[s], 16)

            def store_chunk(b, m):
                n, s = CHUNKS * b + m, m % 2
                sp.wait_ge(z_step, (n + 1) * Z_ALL)
                sp.dma_start(out[ds(n * CN, CN), :].rearrange("(t p) c -> p t c", p=P),
                             o[:, s]).then_inc(out_stored[s], 16)

            def load_experts(b):
                if not is_first(b):
                    sp.wait_ge(w2_step, 2 * b)
                for k in range(TOPK):
                    e = sp.value_load(irow[0:1, ds(TOPK * b + k, 1)], min_val=0, max_val=EXPERTS - 1)
                    sp.dma_start(w1r[:, k], ew1[ds(e, 1)].rearrange("e (c p) f -> p (e c) f", p=P)
                                 ).then_inc(w1_loaded, 16)
                    sp.dma_start(b1r[:, k], ew_b(eb1, e)).then_inc(w1_loaded, 16)
                    sp.dma_start(b2r[:, k], eb2[ds(e, 1), :].broadcast_to([P, C])).then_inc(w1_loaded, 16)
                    sp.dma_start(w2r[:, k], ew2[ds(e, 1)].rearrange("e (f p) c -> p (e f) c", p=P)
                                 ).then_inc(w2_loaded, 16)

            def ew_b(eb1, e):
                return eb1[ds(e, 1)].rearrange("e p f -> (e p) f")

            load_chunk(0, 0)
            load_chunk(0, 1)
            sp.wait_ge(r_step, R_STEPS)
            for b in range(B):
                sp.dma_start(irow[0:1, TOPK * b:TOPK * (b + 1)], idx[b:b + 1, 0:TOPK]).then_inc(row_loaded, 16)
                sp.dma_start(wrow[0:1, TOPK * b:TOPK * (b + 1)], wv[b:b + 1, :]).then_inc(row_loaded, 16)
            sp.wait_ge(row_loaded, 16 * 2 * B)

            load_experts(0)
            load_chunk(0, 2)

            def body(b):
                for m in range(CHUNKS):
                    if later(b, m, 3):
                        load_chunk(*later(b, m, 3))
                    if m == 1 and later(b, m, CHUNKS):
                        load_experts(b + 1)
                    store_chunk(b, m)
            batch_loop(sp, body)
            for s in range(2):
                sp.wait_ge(out_stored[s], 16 * B * CHUNKS // 2)

        @block.gpsimd
        def _(pool):
            nc.gpsimd.memset(ones[:, :], 1.0).then_inc(c_set, 1)
            nc.gpsimd.memset(mhalf[:, :], -0.5).then_inc(c_set, 1)
            pool.wait_ge(c_set, 2)
            pool.wait_ge(c_loaded, 16 * 5)

            def add_bias(b, m):
                n, s = CHUNKS * b + m, m % 2
                if m == 0:
                    pool.wait_ge(bias_step, 3 * (b + 1))
                pool.wait_ge(tnk_loaded[s], 16 * (CHUNKS // 2 * b + m // 2 + 1))
                pool.wait_ge(tk_loaded[s], 16 * (CHUNKS // 2 * b + m // 2 + 1))
                if not (is_first(b) and m < 2):
                    pool.wait_ge(z_step, (n - 1) * Z_ALL)
                nc.gpsimd.tensor_tensor(tnb[:, s], tnk[:, s], b2c[:, 1:2, :].broadcast_to([P, CT, C]),
                                        ALU.add).then_inc(bias_added, 1)
                nc.gpsimd.tensor_tensor(tb[:, s], tk[:, s], bet[:, None, :].broadcast_to([P, CT, C]),
                                        ALU.add).then_inc(bias_added, 1)

            def rsqrt(b, m):
                n = CHUNKS * b + m
                pool.wait_ge(z_step, n * Z_ALL + Z_VE)
                nc.gpsimd.tensor_tensor(rstd[:, :], ve[:, :], mhalf[:, :], ALU.pow).then_inc(rstd_ready, 1)

            add_bias(0, 0)

            def body(b):
                for m in range(CHUNKS):
                    if later(b, m, 1):
                        add_bias(*later(b, m, 1))
                    rsqrt(b, m)
            batch_loop(pool, body)

        @block.scalar
        def _(act):
            for k in range(3):
                act.wait_ge(r_step, (3, 15, 21)[k])
                if k < 2:
                    nc.scalar.activation(r[:, 2 * k + 1, :], r[:, 2 * k, :], ACT.Exp).then_inc(r_exp, 1)
                else:
                    nc.scalar.activation(rc[:, 5:6], rc[:, 4:5], ACT.Exp).then_inc(r_exp, 1)

            def split_w1(b):
                act.wait_ge(w1_loaded, 96 * (b + 1))
                if not is_first(b):
                    act.wait_ge(h_ready, JB * CHUNKS * b)
                nc.scalar.copy(w1h[:, :, :, :], w1r[:, :, :, :]).then_inc(w1hi_ready, 1)

            def split_w2(b):
                act.wait_ge(w2_loaded, 32 * (b + 1))
                if not is_first(b):
                    act.wait_ge(y_ready, CT * CHUNKS * b)
                for k in range(TOPK):
                    nc.scalar.activation(w2h[:, k], w2r[:, k], ACT.Copy,
                                         scale=wbc[:, ds(TOPK * b + k, 1)]).then_inc(w2hi_ready, 1)

            def take_x(b, m):
                n, s = CHUNKS * b + m, m % 2
                act.wait_ge(x_turned, 2 * (n + 1))
                if not (is_first(b) and m < 2):
                    act.wait_ge(h_ready, JB * (n - 1))
                nc.scalar.copy(xh[:, s], pT[:, :, 0:CN]).then_inc(xh_ready, 1)

            def gelus(b, m):
                n, s = CHUNKS * b + m, m % 2
                if not (is_first(b) and m < 2):
                    act.wait_ge(y_ready, CT * (n - 1))
                for j in range(JB):
                    act.wait_ge(h_ready, JB * n + j + 1)
                    if not (is_first(b) and m == 0 and j < 2):
                        act.wait_ge(g_step, JB * n + j - 1)
                    for dst in (gf[:, j % 2, :], gh[:, s, j, :]):
                        last = nc.scalar.activation(dst, pH[:, j % 4, 0:CN], ACT.Gelu,
                                                    bias=b1c[:, j // FB, j % FB:j % FB + 1])
                    last.then_inc(gelu_done, 1)

            split_w1(0)
            act.wait_ge(r_pe, 3)
            act.wait_ge(r_step, R_STEPS + 1)
            split_w2(0)
            act.wait_ge(bias_step, 3)
            take_x(0, 0)
            gelus(0, 0)
            take_x(0, 1)

            def body(b):
                for m in range(CHUNKS):
                    if m == 0 and not is_first(b):
                        split_w2(b)
                    if later(b, m, 1):
                        if m == CHUNKS - 1:
                            act.wait_ge(bias_step, 3 * (b + 2))
                        gelus(*later(b, m, 1))
                    if later(b, m, 2):
                        take_x(*later(b, m, 2))
                    if m == CHUNKS - 2 and later(b, m, 2):
                        split_w1(b + 1)
            batch_loop(act, body)

        @block.vector
        def _(dve):
            tt, stt = nc.vector.tensor_tensor, nc.vector.scalar_tensor_tensor
            s = Steps(dve, r_step, 0, R_STEPS)

            def do(ins):
                s.did(ins)
                s.settle()

            def softmax_shift(src, dst, col):
                do(nc.vector.tensor_reduce(rc[:, col:col + 1], src, AX.X, ALU.max))
                do(nc.vector.tensor_scalar(dst, src, rc[:, col:col + 1], None, ALU.subtract))

            def softmax_divide(src, dst, col):
                do(nc.vector.tensor_reduce(rc[:, col:col + 1], src, AX.X, ALU.add))
                do(nc.vector.reciprocal(rc[:, col:col + 1], rc[:, col:col + 1]))
                do(nc.vector.tensor_scalar(dst, src, rc[:, col:col + 1], None, ALU.mult))

            dve.wait_ge(sums_ready, 1)
            do(nc.vector.tensor_scalar(mean[:, :], pT[:, 0, 0:CC * B], 1.0 / SB, None, ALU.mult))
            dve.wait_ge(r_pe, 1)
            softmax_shift(pT[0:B, 1, 0:EXPERTS], r[:, 0, :], 0)
            dve.wait_ge(r_exp, 1)
            softmax_divide(r[:, 1, :], r[:, 4, :], 1)
            dve.wait_ge(r_pe, 2)
            do(nc.vector.tensor_scalar(r[:, 5, :], pT[0:B, 0, 64:64 + EXPERTS], float(SB), None, ALU.mult))
            do(nc.vector.reciprocal(r[:, 5, :], r[:, 5, :]))
            do(nc.vector.tensor_scalar(r[:, 5, :], r[:, 5, :], CAPACITY, 1.0, ALU.mult, ALU.min))
            do(tt(r[:, 6, :], r[:, 5, :], r[:, 4, :], ALU.mult))
            softmax_shift(r[:, 6, :], r[:, 2, :], 2)
            do(nc.vector.tensor_copy(rc[:, 6:7], rc[:, 2:3]))
            do(nc.vector.tensor_copy(rc[:, 7:8], rc[:, 2:3]))
            do(nc.vector.tensor_copy(rc[:, 7:8], rc[:, 2:3]))
            dve.wait_ge(r_exp, 2)
            softmax_divide(r[:, 3, :], r[:, 7, :], 3)
            do(nc.vector.max(r[:, 0, :], r[:, 7, :]))
            do(nc.vector.max_index(idx[:, :], r[:, 0, :], r[:, 7, :]))
            do(tt(rc[:, 4:5], r[:, 0, 1:2], r[:, 0, 0:1], ALU.subtract))
            dve.wait_ge(r_exp, 3)
            do(nc.vector.tensor_scalar(rc[:, 6:7], rc[:, 5:6], 1.0, None, ALU.add))
            do(nc.vector.reciprocal(wv[:, 0:1], rc[:, 6:7]))
            do(tt(wv[:, 1:2], rc[:, 5:6], wv[:, 0:1], ALU.mult))
            s.at(R_STEPS)
            dve.wait_ge(r_pe, 3)
            nc.vector.tensor_copy(wbc[:, :], pT[:, 1, 64:64 + TOPK * B]).then_inc(r_step, 1)
            dve.wait_ge(r_step, R_STEPS + 1)

            def split_w1(b):
                dve.wait_ge(w1hi_ready, b + 1)
                tt(w1l[:, :, :, :], w1r[:, :, :, :], w1h[:, :, :, :].bitcast(F32),
                   ALU.subtract).then_inc(w1_step, 1)
                s = Steps(dve, bias_step, b, 3)
                if not is_first(b):
                    dve.wait_ge(bias_added, 2 * CHUNKS * b)
                    dve.wait_ge(gelu_done, JB * CHUNKS * b)
                s.did(nc.vector.tensor_copy(b1c[:, :, :], b1r[:, :, :]))
                s.did(nc.vector.tensor_scalar(b2c[:, 0, :], b2r[:, 0, :], wbc[:, ds(TOPK * b, 1)], None,
                                              ALU.mult))
                s.settle()
                s.did(stt(b2c[:, 1, :], b2r[:, 1, :], wbc[:, ds(TOPK * b + 1, 1)], b2c[:, 0, :],
                          ALU.mult, ALU.add))

            def split_w2(b):
                for k in range(TOPK):
                    dve.wait_ge(w2hi_ready, 2 * b + k + 1)
                    stt(w2l[:, k], w2r[:, k], wbc[:, ds(TOPK * b + k, 1)], w2h[:, k].bitcast(F32),
                        ALU.mult, ALU.subtract).then_inc(w2_step, 1)

            def take_x(b, m):
                n, sl = CHUNKS * b + m, m % 2
                dve.wait_ge(xh_ready, n + 1)
                tt(xl[:, sl], pT[:, :, 0:CN], xh[:, sl].bitcast(F32), ALU.subtract).then_inc(xl_ready, 1)

            def split_hidden(b, m, blocks):
                n, sl = CHUNKS * b + m, m % 2
                for j in blocks:
                    dve.wait_ge(gelu_done, JB * n + j + 1)
                    tt(gl[:, sl, j, :], gf[:, j % 2, :], gh[:, sl, j, :].bitcast(F32),
                       ALU.subtract).then_inc(g_step, 1)

            def sum_up(b, m):
                n, sl = CHUNKS * b + m, m % 2
                s = Steps(dve, z_step, n, Z_ALL)
                s.settle()
                dve.wait_ge(bias_added, 2 * (n + 1))

                def add(t):
                    dve.wait_ge(y_ready, CT * n + t + 1)
                    s.did(tt(z[:, t, :], pY[:, (CT * m + t) % 2, 0:C], tnb[:, sl, t, :], ALU.add))

                def stats(t):
                    s.did(nc.vector.bn_stats(st[:, t, :], z[:, t, :]))

                add(0)
                for t in range(1, CT):
                    add(t)
                    s.settle()
                    stats(t - 1)
                stats(CT - 1)
                s.settle()
                carry(nc, spare[0:1, 0:1])
                for t in range(CT):
                    s.did(nc.vector.bn_aggr(mv[:, t, :], st[:, t, :]))
                s.settle()
                s.did(nc.vector.tensor_scalar(ve[:, :], mv[:, :, 1], 1e-5, None, ALU.add))
                s.at(Z_VE)

            def finish(b, m):
                n, sl = CHUNKS * b + m, m % 2
                s = Steps(dve, z_step, n, Z_ALL, Z_VE)
                for t in range(CT):
                    s.did(stt(z[:, t, :], z[:, t, :], mv[:, t, 0:1], gam[:, :], ALU.subtract, ALU.mult))
                s.settle()
                dve.wait_ge(rstd_ready, n + 1)
                if not (is_first(b) and m < 2):
                    dve.wait_ge(out_stored[sl], 16 * (CHUNKS // 2 * b + m // 2))
                for t in range(CT):
                    s.did(stt(o[:, sl, t, :], z[:, t, :], rstd[:, t:t + 1], tb[:, sl, t, :],
                              ALU.mult, ALU.add))
                s.at(Z_ALL)

            half = JB // 2
            split_w1(0)
            take_x(0, 0)
            split_hidden(0, 0, range(JB))
            take_x(0, 1)
            split_w2(0)

            def body(b):
                for m in range(CHUNKS):
                    if m == 0 and not is_first(b):
                        split_w2(b)
                    if later(b, m, 1):
                        split_hidden(*later(b, m, 1), range(half))
                    if m > 0:
                        finish(b, m - 1)
                    elif not is_first(b):
                        finish(b - 1, CHUNKS - 1)
                    if later(b, m, 1):
                        split_hidden(*later(b, m, 1), range(half, JB))
                    if later(b, m, 2):
                        take_x(*later(b, m, 2))
                    if m == CHUNKS - 2 and later(b, m, 2):
                        split_w1(b + 1)
                    sum_up(b, m)
            batch_loop(dve, body)
            finish(B - 1, CHUNKS - 1)

        @block.tensor
        def _(pe):
            pe.wait_ge(c_set, 2)
            pe.wait_ge(c_loaded, 16 * 5)
            for c in range(CC):
                for b in range(B):
                    for t in range(NT):
                        last = nc.tensor.matmul(pT[:, 0, c * B + b:c * B + b + 1],
                                                acc[:, b, t, c * P:(c + 1) * P], ones[0:TT, 0:1],
                                                start=(t == 0), stop=(t == NT - 1))
            last.then_inc(sums_ready, 1)
            pe.wait_ge(r_step, 1)
            for c in range(CC):
                nc.tensor.matmul(pT[0:B, 1, 0:EXPERTS], mean[:, c * B:(c + 1) * B], wrs[:, c, :],
                                 start=(c == 0), stop=False)
            nc.tensor.matmul(pT[0:B, 1, 0:EXPERTS], ones[0:1, 0:B], brs[:, :],
                             start=False, stop=True).then_inc(r_pe, 1)
            pe.wait_ge(r_step, 6)
            nc.tensor.matmul(pT[0:B, 0, 64:64 + EXPERTS], ones[0:B, 0:B], r[:, 4, :],
                             start=True, stop=True).then_inc(r_pe, 1)
            pe.wait_ge(row_loaded, 16 * 2 * B)
            nc.tensor.matmul(pT[:, 1, 64:64 + TOPK * B], ones[0:1, :], wrow[:, :],
                             start=True, stop=True).then_inc(r_pe, 1)
            pe.wait_ge(r_step, R_STEPS + 1)

            def turn_x(b, m):
                n, s = CHUNKS * b + m, m % 2
                pe.wait_ge(tnk_loaded[s], 16 * (CHUNKS // 2 * b + m // 2 + 1))
                after(pe, xl_ready, n)
                for c in range(CC):
                    for t in range(CT):
                        last = nc.tensor.transpose(pT[:, c, t * P:(t + 1) * P],
                                                   tnk[:, s, t, c * P:(c + 1) * P], ident[:, :])
                    last.then_inc(x_turned, 1)

            def layer1(b, m):
                n, s = CHUNKS * b + m, m % 2
                pe.wait_ge(xl_ready, n + 1)
                if m == 0:
                    pe.wait_ge(w1_step, b + 1)
                for j in range(JB):
                    if not (is_first(b) and m == 0 and j < 4):
                        pe.wait_ge(gelu_done, JB * n + j - 3)
                    k, f = j // FB, j % FB
                    terms = [(c, w, x) for c in range(CC) for w, x in ((w1h, xh), (w1h, xl), (w1l, xh))]
                    for i, (c, w, x) in enumerate(terms):
                        last = nc.tensor.matmul(pH[:, j % 4, 0:CN], w[:, k, c, f * P:(f + 1) * P], x[:, s, c, :],
                                                start=(i == 0), stop=(i == len(terms) - 1))
                    last.then_inc(h_ready, 1)

            def layer2(b, m):
                n, s = CHUNKS * b + m, m % 2
                pe.wait_ge(g_step, JB * (n + 1))
                if m == 0:
                    pe.wait_ge(w2_step, 2 * (b + 1))
                for t in range(CT):
                    if not (is_first(b) and m == 0 and t < 2):
                        pe.wait_ge(z_step, (n - 1) * Z_ALL + 2 * t + 2 if t < 2 else n * Z_ALL + 1)
                    terms = [(j, g, w) for j in range(JB) for g, w in ((gh, w2h), (gh, w2l), (gl, w2h))]
                    for i, (j, g, w) in enumerate(terms):
                        last = nc.tensor.matmul(pY[:, (CT * m + t) % 2, 0:C], g[:, s, j, t * P:(t + 1) * P],
                                                w[:, j // FB, j % FB, :],
                                                start=(i == 0), stop=(i == len(terms) - 1))
                    last.then_inc(y_ready, 1)

            turn_x(0, 0)
            layer1(0, 0)
            turn_x(0, 1)

            def body(b):
                for m in range(CHUNKS):
                    if later(b, m, 1):
                        layer1(*later(b, m, 1))
                    if later(b, m, 2):
                        turn_x(*later(b, m, 2))
                    layer2(b, m)
            batch_loop(pe, body)


def program(nc, xt, w1p, b1, w2, b2, bn_gamma, bn_beta, bn_mean, bn_var, wr, br, ew1, eb1, ew2, eb2,
            gamma, beta, ident_d, spread_d, out):
    xn_d = nc.dram_tensor("xn_scratch", (N, C), F32, kind="Internal").ap()
    attn_d = nc.dram_tensor("attn_scratch", (TAPS, 2, N), F16, kind="Internal").ap()
    t_d = nc.dram_tensor("t_scratch", (N, C), F32, kind="Internal").ap()
    tn_d = nc.dram_tensor("tn_scratch", (N, C), F32, kind="Internal").ap()
    conv_phase(nc, xt, w1p, b1, w2, b2, bn_gamma, bn_beta, bn_mean, bn_var, ident_d, xn_d, attn_d)
    with nc.sbuf_tensor("acc", [TT, B, NT, C], F32) as acc:
        attend_phase(nc, xt, xn_d, attn_d, spread_d, t_d, tn_d, acc)
        ffn_phase(nc, acc, t_d, tn_d, wr, br, ew1, eb1, ew2, eb2, gamma, beta, ident_d, out)


def kernel(**inputs):
    import numpy as np
    import concourse.bacc as bacc
    from concourse.bass_utils import run_bass_kernel_spmd

    a = {k: np.asarray(v) for k, v in inputs.items()}

    def parity_order(x):
        return x.reshape(B, C, SIDE, 2, SIDE, 2).transpose(0, 3, 5, 2, 4, 1)

    w1 = a["L0_conv_w1"].reshape(CMID, CC, P, KS, KS)
    arrays = {
        "xt": parity_order(a["x"]).reshape(N, C),
        "w1p": w1.transpose(1, 3, 2, 4, 0).reshape(CC * KS, P, KS * CMID),
        "b1": a["L0_conv_b1"].reshape(CMID, 1),
        "w2": a["L0_conv_w2"].reshape(TAPS, CMID),
        "b2": a["L0_conv_b2"].reshape(TAPS, 1),
        "bn_gamma": a["L0_conv_bn_gamma"].reshape(TAPS, 1),
        "bn_beta": a["L0_conv_bn_beta"].reshape(TAPS, 1),
        "bn_mean": a["L0_conv_bn_mean"].reshape(TAPS, 1),
        "bn_var": a["L0_conv_bn_var"].reshape(TAPS, 1),
        "wr": a["L0_ffn_Wr"],
        "br": a["L0_ffn_br"].reshape(1, EXPERTS),
        "ew1": a["L0_ffn_W1"],
        "eb1": a["L0_ffn_b1"].reshape(EXPERTS, FB, P).transpose(0, 2, 1),
        "ew2": a["L0_ffn_W2"],
        "eb2": a["L0_ffn_b2"],
        "gamma": a["L0_ffn_gamma"].reshape(1, C),
        "beta": a["L0_ffn_beta"].reshape(1, C),
        "ident": np.eye(P, dtype=np.float32),
        "spread": spread_table(),
    }
    arrays = {k: np.ascontiguousarray(v) for k, v in arrays.items()}
    nc = bacc.Bacc("TRN2", target_bir_lowering=False, num_devices=1)
    args = [nc.dram_tensor(f"in_{k}", v.shape, mybir.dt.from_np(v.dtype), kind="ExternalInput").ap()
            for k, v in arrays.items()]
    out = nc.dram_tensor("out_0", (N, C), F32, kind="ExternalOutput").ap()
    program(nc, *args, out)
    r = run_bass_kernel_spmd(nc, [{f"in_{k}": v for k, v in arrays.items()}], core_ids=[0])
    y = np.asarray(r.results[0]["out_0"]).reshape(B, 2, 2, SIDE, SIDE, C)
    return np.ascontiguousarray(y.transpose(0, 5, 3, 1, 4, 2).reshape(B, C, HH, WW))
```

```python
from contextlib import ExitStack

import concourse.bass as bass
from concourse import mybir
from concourse.bass import ds

ALU = mybir.AluOpType
ACT = mybir.ActivationFunctionType
F32 = mybir.dt.float32
F32R = mybir.dt.float32r
F16 = mybir.dt.float16
U32 = mybir.dt.uint32
AX = mybir.AxisListType

P = 128
B, C, HH, WW = 4, 256, 48, 48
KS = 7
ROWS = [3, 0, 1, 2, 4, 5, 6]
TAPS = KS * KS
SIDE = HH // 2
IMGS = B * 4
PIX = SIDE * SIDE
N = IMGS * PIX
SB = N // B
CC = C // P
CMID = 128
TR = 4
TT = TR * SIDE
NT = SIDE // TR
PAIRS = IMGS // 2

POINTS = [1.0, -1.0, 2.0, -2.0, -0.5, 0.0]
NP = len(POINTS) + 1
UNITS = 2 * NP - 1
QT = SIDE // 4
VT = QT + 1
CW = 32
HALF = 2 * SIDE * QT
ATT_SCALE = 1024.0
EPAD = 66

LN_STEPS = 2 * NT + 2
V_STEPS = 12
V_READ, V_HEAD = 2, 5
W_SLOTS = 4
UV_STEPS, UP_STEPS = 7, 4
Y_STEPS = 14
SM_STEPS = 14
BN_STEPS = 5
SIG_STEPS = 4


def point_norm(k):
    if k == NP - 1:
        return 1.0
    d = 1.0
    for j, b in enumerate(POINTS):
        if j != k:
            d *= POINTS[k] - b
    return 1.0 / d


class Steps:

    def __init__(self, eng, sem, run, per, first=0):
        self.eng, self.sem, self.base, self.n = eng, sem, run * per, first

    def did(self, ins):
        self.n += 1
        ins.then_inc(self.sem, 1)

    def settle(self):
        after(self.eng, self.sem, self.base + self.n)

    def at(self, n):
        assert self.n == n, (self.n, n)


def after(eng, sem, value):
    if isinstance(value, int) and value <= 0:
        return
    eng.wait_ge(sem, value)


def carry(nc, spare):
    nc.vector.memset(spare, 0.0)


def is_first(q):
    return isinstance(q, int) and q == 0


def batch_loop(eng, body):
    body(0)
    with eng.Fori(1, B - 1) as b:
        body(b)
    body(B - 1)


def later(b, m, by, per):
    if m + by < per:
        return b, m + by
    return None if isinstance(b, int) and b == B - 1 else (b + 1, m + by - per)


def conv_phase(nc, xt, w1p, b1, w2, b2, bn_gamma, bn_beta, bn_mean, bn_var, ident_d, xn_d, attn_d):
    PIECES = CC * KS
    PADS = 2 + 3 + W_SLOTS
    with ExitStack() as ctx:
        def sb(name, shape, dt):
            return ctx.enter_context(nc.sbuf_tensor(name, shape, dt))

        def ps(name, shape):
            return ctx.enter_context(nc.psum_tensor(name, shape, F32))

        def sem(name):
            return ctx.enter_context(nc.semaphore(name))

        U = sb("U", [P, 2, UNITS, PIECES, CMID], F16)
        V = sb("V", [P, 2, 2, NP, CC, 2, SIDE * VT], F16)
        ch = sb("ch", [P, 2, CC, SIDE, CW], F32)
        xa = sb("xa", [TT, 2, NT, C], F32)
        ydata = sb("ydata", [P, 4 * HALF], F32)
        k1 = sb("k1", [P, 4 * HALF], F32)
        WORK = SIDE * (CW + 4 * VT + 4 * VT + NP * VT)
        work = sb("work", [P, WORK], F32)
        msb = sb("msb", [P, 2, HALF], F32)
        sd = sb("sd", [P, 4, HALF], F32)
        E = sb("E", [TT, 2, NT * TAPS + EPAD - TAPS], F32)
        spare = sb("spare", [1, 1], F32)
        aTs = sb("aTs", [TAPS, 2, 2, PIX], F16)
        ident = sb("ident", [P, P], F32)
        st = sb("st", [TT, 2, NT, 6], F32)
        mv = sb("mv", [TT, 2, NT, 2], F32)
        ve = sb("ve", [TT, 2, NT], F32)
        nmean = sb("nmean1", [TT, 2, NT], F32)
        shift = sb("shift1", [TT, 2, NT], F32)
        rstd = sb("rstd", [TT, 2, NT], F32)
        mhalf = sb("mhalf", [TT, NT], F32)
        mx = sb("mx", [TT, 2, NT], F32)
        sm = sb("sm", [TT, 2, NT], F32)
        w2s = sb("w2s", [TAPS, CMID], F32)
        w2T = sb("w2T", [CMID, TAPS], F32)
        bnp = sb("bnp", [TAPS, 8], F32)
        brow = sb("brow", [1, NT, TAPS], F32)
        ones = sb("ones", [1, TT], F32)
        b1s = sb("b1s", [CMID, 1], F32)
        mxp = sb("mxp", [P, PIECES], F32)
        sg = sb("sg", [P, 6], F32)

        pM = ps("pM", [P, 4, 512])
        pX = ps("pX", [P, 2, 512])
        pL = ps("pL", [P, 512])
        pA = ps("pA", [P, 512])

        par_loaded = sem("par_loaded")
        pads_zeroed = sem("pads_zeroed")
        w_seen = sem("w_seen")
        wmax_ready = sem("wmax_ready")
        wmax_all = sem("wmax_all")
        sig_step = sem("sig_step")
        uv_step = sem("uv_step")
        up_step = sem("up_step")
        t_free = sem("t_free")
        uhi_ready = sem("uhi_ready")
        bn_step = sem("bn_step")
        bn_rstd = sem("bn_rstd")
        w2_turned = sem("w2_turned")
        w2_ready = sem("w2_ready")
        ln_step = sem("ln_step")
        rstd_step = sem("rstd_step1")
        xn_ready = sem("xn_ready")
        xT_ready = sem("xT_ready")
        xT_used = sem("xT_used")
        v_step = sem("v_step")
        vhi_ready = sem("vhi_ready")
        vlo_ready = sem("vlo_ready")
        m_ready = sem("m_ready")
        m_copied = sem("m_copied")
        y_step = sem("y_step")
        k1_ready = sem("k1_ready")
        logits_ready = sem("logits_ready")
        sm_step = sem("sm_step")
        exp_ready = sem("exp_ready")
        aT_ready = sem("aT_ready")
        ahi_ready = sem("ahi_ready")
        alo_ready = sem("alo_ready")
        w_loaded = [sem(f"w_loaded{s}") for s in range(W_SLOTS)]
        x_loaded = [sem(f"x_loaded{i}") for i in range(2)]
        xn_stored = [sem(f"xn_stored{i}") for i in range(2)]
        at_stored = [sem(f"at_stored{i}") for i in range(2)]

        def pair_loop(eng, body):
            body(0, 0)
            body(1, 1)
            with eng.Fori(1, PAIRS // 2 - 1) as j:
                body(2 * j, 0)
                body(2 * j + 1, 1)
            body(PAIRS - 2, 0)
            body(PAIRS - 1, 1)

        def chunk(q, n):
            return (n % 2, n // 2) if isinstance(q, int) and q < 2 else (n // 2, n % 2)

        def is_last(q):
            return isinstance(q, int) and q == PAIRS - 1

        wst = [V[:, 1, s // 2].rearrange("p k c i n -> p (k c i n)").bitcast(F32)[
            :, (s % 2) * 8 * CMID:(s % 2 + 1) * 8 * CMID] for s in range(W_SLOTS)]
        TU = UNITS - 3
        Tu = work[:, 0:2 * TU * CMID].rearrange("p (s u n) -> p s u n", s=2, n=CMID)
        Au = sd[:, :, :].rearrange("p k n -> p (k n)")[:, 0:8 * CMID].rearrange("p (k g n) -> p k g n", k=4, g=2)

        def taps_of(sl):
            return wst[sl].rearrange("p (g j n) -> p j g n", g=2, j=4)

        def piece_loop(eng, body):
            with eng.Fori(0, PIECES // W_SLOTS) as j:
                body(j * W_SLOTS, j, W_SLOTS)
            body(PIECES // W_SLOTS * W_SLOTS, PIECES // W_SLOTS, PIECES % W_SLOTS)

        def w_turns(sl):
            return PIECES // W_SLOTS + (sl < PIECES % W_SLOTS)

        def vtile(w):
            o = SIDE * (CW + 28 + 14 + 14)
            return w[:, o:o + NP * SIDE * VT].rearrange("p (k n) -> p k n", k=NP)

        def m_bank(q, k):
            if is_first(q) and k >= 4:
                return (pX[:, 0, :], pX[:, 1, :], pL)[k - 4]
            return pM[:, k % 4, :]

        def a_bank(i, h):
            return ((pA, pL), (pX[:, 0, :], pX[:, 1, :]))[i][h]

        block = ctx.enter_context(nc.Block())

        @block.sync
        def _(sp):
            for i in range(2):
                sp.sem_inc(at_stored[i], 16)
            sp.sem_inc(t_free, 2)

            def load_x(q, i):
                if not is_first(q):
                    sp.wait_ge(xn_stored[i], 16 * q)
                    sp.wait_ge(xT_ready, 8 * q - 2 + 2 * i)
                src = xt[ds((2 * q + i) * PIX, PIX), :].rearrange("(t p) c -> p t c", p=TT)
                sp.dma_start(xa[:, i, :, :], src).then_inc(x_loaded[i], 16)

            def store_xn(q, i):
                sp.wait_ge(xn_ready, 2 * q + i + 1)
                dst = xn_d[ds((2 * q + i) * PIX, PIX), :].rearrange("(t p) c -> p t c", p=TT)
                sp.dma_start(dst, xa[:, i, :, :]).then_inc(xn_stored[i], 16)

            def store_attn(q, i):
                sp.wait_ge(alo_ready, 4 * q + 2 * i + 2)
                sp.dma_start(attn_d[:, :, ds((2 * q + i) * PIX, PIX)],
                             aTs[:, i, :, :]).then_inc(at_stored[i], 16)

            load_x(0, 0)
            load_x(0, 1)
            sp.dma_start(w2s[:, :], w2).then_inc(par_loaded, 16)
            for k, v in enumerate((b2, bn_gamma, bn_beta, bn_mean, bn_var)):
                sp.dma_start(bnp[:, k:k + 1], v).then_inc(par_loaded, 16)
            sp.dma_start(b1s[:, :], b1).then_inc(par_loaded, 16)
            sp.dma_start(ident[:, :], ident_d).then_inc(par_loaded, 16)

            def load_w(k, sl):
                sp.dma_start(wst[sl][:, 0:KS * CMID],
                             w1p[ds(k, 1), :, :].rearrange("a p n -> (a p) n")).then_inc(w_loaded[sl], 16)

            def load_sweep(used, value):
                for k in range(W_SLOTS):
                    load_w(k, k)

                def group(j, pieces):
                    for sl in range(pieces):
                        sp.wait_ge(used, W_SLOTS * j + sl + value)
                        load_w(W_SLOTS * j + sl, sl)
                with sp.Fori(1, PIECES // W_SLOTS) as j:
                    group(j, W_SLOTS)
                group(PIECES // W_SLOTS, PIECES % W_SLOTS)

            load_sweep(w_seen, 1 - W_SLOTS)
            for i in range(2):
                store_xn(0, i)
            for i in range(2):
                load_x(1, i)
            sp.wait_ge(w_seen, PIECES)
            load_sweep(t_free, 3 - W_SLOTS)

            def body(q):
                if not is_last(q):
                    for i in range(2):
                        store_xn(q + 1, i)
                    if not (isinstance(q, int) and q >= PAIRS - 2):
                        for i in range(2):
                            load_x(q + 2, i)
                if not is_first(q):
                    for i in range(2):
                        store_attn(q - 1, i)

            body(0)
            with sp.Fori(1, PAIRS - 2) as q:
                body(q)
            body(PAIRS - 2)
            body(PAIRS - 1)
            for i in range(2):
                store_attn(PAIRS - 1, i)
            for i in range(2):
                sp.wait_ge(xn_stored[i], 16 * PAIRS)
                sp.wait_ge(at_stored[i], 16 * (PAIRS + 1))

        @block.gpsimd
        def _(pool):
            c = ch[:, :, :, :, :].rearrange("p i c r w -> p (i c r) w")
            nc.gpsimd.memset(c[:, :, 0:3], 0.0).then_inc(pads_zeroed, 1)
            nc.gpsimd.memset(c[:, :, 3 + SIDE:CW], 0.0).then_inc(pads_zeroed, 1)
            nc.gpsimd.memset(mhalf[:, :], -0.5).then_inc(pads_zeroed, 1)
            nc.gpsimd.memset(ones[:, :], 1.0).then_inc(pads_zeroed, 1)
            nc.gpsimd.memset(E[:, :, NT * TAPS:], 0.0).then_inc(pads_zeroed, 1)
            for sl in range(W_SLOTS):
                nc.gpsimd.memset(wst[sl][:, KS * CMID:(KS + 1) * CMID], 0.0).then_inc(pads_zeroed, 1)
            pool.wait_ge(pads_zeroed, PADS)
            def rsqrt(q, i):
                if not is_first(q):
                    pool.wait_ge(xn_ready, 2 * q + i - 1)
                pool.wait_ge(ln_step, (2 * q + i + 1) * LN_STEPS)
                nc.gpsimd.tensor_tensor(rstd[:, i, :], ve[:, i, :], mhalf[:, :], ALU.pow).then_inc(rstd_step, 1)
                pool.wait_ge(rstd_step, 2 * (2 * q + i) + 1)
                nc.gpsimd.tensor_tensor(shift[:, i, :], nmean[:, i, :], rstd[:, i, :],
                                        ALU.mult).then_inc(rstd_step, 1)

            def v_low(q, par, n):
                i, c = chunk(q, n)
                pool.wait_ge(vhi_ready, 4 * q + n + 1)
                nc.gpsimd.tensor_tensor(V[:, par, 1, :, c, i, :], vtile(work), V[:, par, 0, :, c, i, :],
                                        ALU.subtract).then_inc(vlo_ready, 1)

            rsqrt(0, 0)
            rsqrt(0, 1)
            pool.wait_ge(bn_step, 1)
            nc.gpsimd.tensor_tensor(bnp[:, 6:7], bnp[:, 5:6], mhalf[0:TAPS, 0:1], ALU.pow).then_inc(bn_rstd, 1)
            for n in range(3):
                v_low(0, 0, n)
            pool.wait_ge(wmax_ready, 1)
            nc.gpsimd.partition_all_reduce(sg[:, 1:2], sg[:, 0:1], P,
                                           bass.bass_isa.ReduceOp.max).then_inc(wmax_all, 1)
            v_low(0, 0, 3)
            add, sub = ALU.add, ALU.subtract

            def points_one(first, j, pieces):
                for sl in range(pieces):
                    s = Steps(pool, up_step, first + sl, UP_STEPS)
                    g = taps_of(sl)
                    pool.wait_ge(w_loaded[sl], 16 * (j + w_turns(sl) + 1))
                    pool.wait_ge(t_free, first + sl + 1)
                    s.did(nc.gpsimd.tensor_tensor(Au[:, 0], g[:, 0], g[:, 2], add))
                    s.did(nc.gpsimd.tensor_tensor(Au[:, 1], g[:, 1], g[:, 3], add))
                    s.settle()
                    s.did(nc.gpsimd.tensor_tensor(Tu[:, sl % 2, 0:2], Au[:, 0], Au[:, 1], add))
                    s.did(nc.gpsimd.tensor_tensor(Tu[:, sl % 2, 2:4], Au[:, 0], Au[:, 1], sub))
                    s.settle()
            pool.wait_ge(v_step, 4 * V_STEPS)
            pool.wait_ge(vlo_ready, 4)
            piece_loop(pool, points_one)

            rsqrt(1, 0)
            rsqrt(1, 1)
            for n in range(4):
                v_low(1, 1, n)
            with pool.Fori(2, PAIRS) as q:
                rsqrt(q, 0)
                rsqrt(q, 1)

        @block.scalar
        def _(act):
            act.wait_ge(pads_zeroed, PADS)

            def normalise_x(q, i):
                act.wait_ge(rstd_step, 2 * (2 * q + i + 1))
                for t in range(NT):
                    last = nc.scalar.activation(xa[:, i, t, :], xa[:, i, t, :], ACT.Identity,
                                                bias=shift[:, i, t:t + 1], scale=rstd[:, i, t:t + 1])
                last.then_inc(xn_ready, 1)

            def plain(q, n):
                i, c = chunk(q, n)
                for h in range(2):
                    act.wait_ge(xT_ready, 8 * q + 2 * n + h + 1)
                    if not is_first(q):
                        before = [k for k in range(4) if chunk(q - 1, k) == (i, c)][0]
                        act.wait_ge(v_step, (4 * q - 4 + before) * V_STEPS + V_READ)
                    nc.scalar.copy(
                        ch[:, i, c, h * (SIDE // 2):(h + 1) * (SIDE // 2), 3:3 + SIDE],
                        pX[:, h, 0:3 * TT].rearrange("p (r w) -> p r w", w=SIDE)
                    ).then_inc(xT_used, 1)

            def v_high(q, par, n):
                i, c = chunk(q, n)
                act.wait_ge(v_step, (4 * q + n + 1) * V_STEPS)
                if not (isinstance(q, int) and q < 2):
                    act.wait_ge(m_ready, NP * (q - 1))
                nc.scalar.copy(V[:, par, 0, :, c, i, :], vtile(work)
                               ).then_inc(vhi_ready, 1)

            def copy_m(q, k):
                act.wait_ge(m_ready, NP * q + 2 * k + 1)
                if not is_first(q):
                    act.wait_ge(y_step, (q - 1) * Y_STEPS + 2 * k + 2)
                nc.scalar.activation(msb[:, k, :], pM[:, 2 * k, 0:HALF], ACT.Copy,
                                     scale=point_norm(2 * k)).then_inc(m_copied, 1)

            def relu(q):
                act.wait_ge(y_step, (q + 1) * Y_STEPS)
                after(act, logits_ready, 2 * q)
                for r in range(4):
                    ins = nc.scalar.activation(k1[:, :].rearrange("p (n r) -> p r n", r=4)[:, r, :],
                                               ydata[:, r * HALF:(r + 1) * HALF], ACT.Relu,
                                               bias=b1s[:, 0:1], scale=sg[:, 4:5])
                ins.then_inc(k1_ready, 1)

            def exp(q, i):
                act.wait_ge(sm_step, q * SM_STEPS + i * SM_STEPS // 2 + 3)
                nc.scalar.activation(E[:, i, 0:NT * TAPS], E[:, i, 0:NT * TAPS], ACT.Exp).then_inc(exp_ready, 1)

            def a_high(q):
                for i in range(2):
                    act.wait_ge(at_stored[i], 16 * (q + 1))
                    for h in range(2):
                        act.wait_ge(aT_ready, 4 * q + 2 * i + h + 1)
                        nc.scalar.copy(aTs[:, i, 0, h * 3 * TT:(h + 1) * 3 * TT],
                                       a_bank(i, h)[0:TAPS, 0:3 * TT]).then_inc(ahi_ready, 1)

            def prepare(q, par):
                plain(q, 0)
                for n in range(4):
                    if n + 1 < 4:
                        plain(q, n + 1)
                    v_high(q, par, n)

            normalise_x(0, 0)
            normalise_x(0, 1)
            act.wait_ge(par_loaded, 16 * 8)
            act.wait_ge(w2_turned, 2)
            nc.scalar.copy(w2T[:, :], pL[:, 0:TAPS]).then_inc(w2_ready, 1)
            nc.scalar.copy(brow[:, :, :], pL[0:1, None, P:P + TAPS].broadcast_to([1, NT, TAPS])
                           ).then_inc(w2_ready, 1)
            prepare(0, 0)
            act.wait_ge(sig_step, SIG_STEPS)

            def u_high(first, j, pieces):
                for sl in range(pieces):
                    k = first + sl
                    g, hi = taps_of(sl), U[:, 0, :, ds(k, 1), :].rearrange("p u a n -> p u (a n)")
                    act.wait_ge(up_step, (k + 1) * UP_STEPS)
                    act.wait_ge(uv_step, (k + 1) * UV_STEPS)
                    nc.scalar.activation(hi[:, 0:TU], Tu[:, sl % 2], ACT.Copy, scale=sg[:, 3:4])
                    nc.scalar.activation(hi[:, TU:TU + 2], g[:, 0], ACT.Copy, scale=sg[:, 3:4])
                    nc.scalar.activation(hi[:, TU + 2:], g[:, 3, 0:1], ACT.Copy,
                                         scale=sg[:, 3:4]).then_inc(uhi_ready, 1)
            piece_loop(act, u_high)

            def body(q, par):
                if is_first(q):
                    normalise_x(1, 0)
                    copy_m(0, 0)
                    copy_m(0, 1)
                    normalise_x(1, 1)
                    prepare(1, 1)
                    relu(0)
                    return
                if not is_last(q):
                    normalise_x(q + 1, 0)
                    normalise_x(q + 1, 1)
                copy_m(q, 0)
                if not is_last(q):
                    for n in range(2):
                        plain(q + 1, n)
                    for n in range(2):
                        v_high(q + 1, 1 - par, n)
                exp(q - 1, 0)
                if not is_last(q):
                    plain(q + 1, 2)
                    v_high(q + 1, 1 - par, 2)
                copy_m(q, 1)
                if not is_last(q):
                    plain(q + 1, 3)
                    v_high(q + 1, 1 - par, 3)
                exp(q - 1, 1)
                a_high(q - 1)
                relu(q)

            pair_loop(act, body)
            for i in range(2):
                exp(PAIRS - 1, i)
            a_high(PAIRS - 1)

        @block.vector
        def _(dve):
            tt, stt = nc.vector.tensor_tensor, nc.vector.scalar_tensor_tensor
            Et = E[:, :, 0:NT * TAPS].rearrange("p i (t k) -> p i t k", k=TAPS)

            def ln(q):
                for i in range(2):
                    s = Steps(dve, ln_step, 2 * q + i, LN_STEPS)
                    dve.wait_ge(x_loaded[i], 16 * (q + 1))
                    for t in range(NT):
                        s.did(nc.vector.bn_stats(st[:, i, t, :], xa[:, i, t, :]))
                    s.settle()
                    carry(nc, spare[0:1, 0:1])
                    for t in range(NT):
                        s.did(nc.vector.bn_aggr(mv[:, i, t, :], st[:, i, t, :]))
                    s.settle()
                    after(dve, rstd_step, 4 * q - 2 + 2 * i if not is_first(q) else 0)
                    s.did(nc.vector.tensor_scalar(ve[:, i, :], mv[:, i, :, 1], 1e-6, None, ALU.add))
                    s.did(nc.vector.tensor_scalar(nmean[:, i, :], mv[:, i, :, 0], -1.0, None, ALU.mult))
                    s.at(LN_STEPS)

            o = 0
            E1 = work[:, 0:SIDE * CW].rearrange("p (r w) -> p r w", w=CW)
            o += SIDE * CW
            S = work[:, o:o + SIDE * 28].rearrange("p (r w) -> p r w", w=28)
            o += SIDE * 28
            Ux = work[:, o:o + SIDE * 14].rearrange("p (w r t) -> p w r t", r=SIDE, w=2)
            o += SIDE * 14
            Sd = work[:, o:o + SIDE * 14].rearrange("p (r t w) -> p r t w", r=SIDE, w=2)
            T = vtile(work).rearrange("p k (r t) -> p k r t", t=VT)
            S4 = S.rearrange("p r (t w) -> p r t w", w=4)
            E4 = E1.rearrange("p r (t w) -> p r t w", w=4)

            def v_head(q, n):
                i, c = chunk(q, n)
                s = Steps(dve, v_step, 4 * q + n, V_STEPS)
                D = ch[:, i, c, :, :]
                D2 = D.rearrange("p r (t w) -> p r t w", w=2)
                s.settle()
                dve.wait_ge(xT_used, 8 * q + 2 * n + 2)
                s.did(stt(E1[:, :, 0:30], D[:, :, 0:30], 0.5, D[:, :, 1:31], ALU.mult, ALU.add))
                s.did(stt(Sd.rearrange("p r t w -> p r (t w)"), D2[:, :, 0:14, 1], -4.0,
                          D2[:, :, 1:15, 1], ALU.mult, ALU.add))
                s.at(V_READ)
                s.settle()
                s.did(stt(S, E1[:, :, 0:28], -4.0, E1[:, :, 2:30], ALU.mult, ALU.add))
                s.did(tt(Ux[:, 0], E4[:, :, 0:VT, 3], E4[:, :, 0:VT, 1], ALU.subtract))
                s.did(tt(Ux[:, 1], E4[:, :, 1:VT + 1, 0], E4[:, :, 0:VT, 2], ALU.subtract))
                s.at(V_HEAD)

            def v_data(q, n):
                s = Steps(dve, v_step, 4 * q + n, V_STEPS, V_HEAD)
                s.settle()
                s.did(tt(T[:, 0], S4[:, :, :, 2], S4[:, :, :, 1], ALU.add))
                s.did(tt(T[:, 1], S4[:, :, :, 2], S4[:, :, :, 1], ALU.subtract))
                s.did(stt(T[:, 2], Ux[:, 0], 2.0, Ux[:, 1], ALU.mult, ALU.add))
                s.did(stt(T[:, 3], Ux[:, 0], -2.0, Ux[:, 1], ALU.mult, ALU.add))
                s.did(tt(T[:, 4], Sd[:, :, :, 1], Sd[:, :, :, 0], ALU.subtract))
                s.did(tt(T[:, 5], S4[:, :, :, 2], S4[:, :, :, 0], ALU.subtract))
                s.did(tt(T[:, 6], S4[:, :, :, 3], S4[:, :, :, 1], ALU.subtract))
                s.at(V_STEPS)

            def v_low(q, par, n):
                i, c = chunk(q, n)
                r = 4 * q + n
                dve.wait_ge(vhi_ready, r + 1)
                tt(V[:, par, 1, :, c, i, :], vtile(work), V[:, par, 0, :, c, i, :],
                   ALU.subtract).then_inc(vlo_ready, 1)
                dve.wait_ge(vlo_ready, r + 1)

            y = [ydata[:, r * HALF:(r + 1) * HALF] for r in range(4)]

            def y_points(q, k):
                s = Steps(dve, y_step, q, Y_STEPS, 2 * k)
                dve.wait_ge(m_copied, 2 * q + k + 1)
                dve.wait_ge(m_ready, NP * q + 2 * k + 2)
                m = pM[:, 2 * k + 1, 0:HALF]
                norm = point_norm(2 * k + 1)
                s.did(stt(sd[:, 2 * k, :], m, norm, msb[:, k, :], ALU.mult, ALU.add))
                s.did(stt(sd[:, 2 * k + 1, :], m, -norm, msb[:, k, :], ALU.mult, ALU.add))

            def y_mid(q):
                s = Steps(dve, y_step, q, Y_STEPS, 4)
                s.settle()
                after(dve, k1_ready, q)
                s.did(tt(y[0], sd[:, 0, :], sd[:, 2, :], ALU.add))
                s.did(stt(y[1], sd[:, 3, :], 2.0, sd[:, 1, :], ALU.mult, ALU.add))
                s.did(stt(y[2], sd[:, 2, :], 4.0, sd[:, 0, :], ALU.mult, ALU.add))
                s.did(stt(y[3], sd[:, 3, :], 8.0, sd[:, 1, :], ALU.mult, ALU.add))
                s.settle()
                dve.wait_ge(m_ready, NP * q + 5)
                for r in range(4):
                    s.did(stt(y[r], m_bank(q, 4)[:, 0:HALF], (-0.5) ** r * point_norm(4), y[r], ALU.mult, ALU.add))

            def y_end(q):
                s = Steps(dve, y_step, q, Y_STEPS, 12)
                s.settle()
                dve.wait_ge(m_ready, NP * q + 6)
                s.did(stt(y[0], m_bank(q, 5)[:, 0:HALF], point_norm(5), y[0], ALU.mult, ALU.add))
                dve.wait_ge(m_ready, NP * q + 7)
                s.did(tt(y[3], m_bank(q, 6)[:, 0:HALF], y[3], ALU.add))
                s.at(Y_STEPS)

            def shift_logits(q, i):
                s = Steps(dve, sm_step, q, SM_STEPS, i * SM_STEPS // 2)
                L = pL[0:TT, 0:NT * TAPS].rearrange("p (t k) -> p t k", t=NT)
                dve.wait_ge(logits_ready, 2 * q + i + 1)
                s.did(nc.vector.tensor_reduce(mx[:, i, :], L, AX.X, ALU.max))
                s.settle()
                s.did(nc.vector.tensor_scalar(mx[:, i, :], mx[:, i, :], 0.0, None, ALU.max))
                s.settle()
                s.did(stt(Et[:, i], L, 0.0, mx[:, i, :, None].broadcast_to([TT, NT, TAPS]),
                          ALU.max, ALU.subtract))

            def normalise(q, i):
                s = Steps(dve, sm_step, q, SM_STEPS, i * SM_STEPS // 2 + 3)
                dve.wait_ge(exp_ready, 2 * q + i + 1)
                s.did(nc.vector.tensor_reduce(sm[:, i, :], Et[:, i], AX.X, ALU.add))
                s.settle()
                s.did(nc.vector.reciprocal(sm[:, i, :], sm[:, i, :]))
                s.settle()
                s.did(nc.vector.tensor_scalar(sm[:, i, :], sm[:, i, :], ATT_SCALE, None, ALU.mult))
                s.settle()
                s.did(tt(Et[:, i], Et[:, i], sm[:, i, :, None].broadcast_to([TT, NT, TAPS]), ALU.mult))

            def a_low(q):
                for i in range(2):
                    for h in range(2):
                        dve.wait_ge(ahi_ready, 4 * q + 2 * i + h + 1)
                        cols = slice(h * 3 * TT, (h + 1) * 3 * TT)
                        tt(aTs[:, i, 1, cols], a_bank(i, h)[0:TAPS, 0:3 * TT], aTs[:, i, 0, cols],
                           ALU.subtract).then_inc(alo_ready, 1)

            def prepare(q, between=lambda n: None):
                for n in range(4):
                    v_head(q, n)
                    after(dve, vlo_ready, 4 * q + n)
                    v_data(q, n)
                    between(n)

            def magnitudes(turn):
                for k in range(turn * W_SLOTS, min((turn + 1) * W_SLOTS, PIECES)):
                    dve.wait_ge(w_loaded[k % W_SLOTS], 16 * (turn + 1))
                    nc.vector.tensor_reduce(mxp[:, k:k + 1], wst[k % W_SLOTS][:, 0:KS * CMID], AX.X, ALU.max,
                                            apply_absolute_value=True).then_inc(w_seen, 1)
                if turn == PIECES // W_SLOTS:
                    dve.wait_ge(w_seen, PIECES)
                    nc.vector.tensor_reduce(sg[:, 0:1], mxp[:, :], AX.X, ALU.max).then_inc(wmax_ready, 1)

            ln(0)
            dve.wait_ge(par_loaded, 16 * 8)
            s = Steps(dve, bn_step, 0, BN_STEPS)
            s.did(nc.vector.tensor_scalar(bnp[:, 5:6], bnp[:, 4:5], 1e-5, None, ALU.add))
            s.did(tt(bnp[:, 0:1], bnp[:, 0:1], bnp[:, 3:4], ALU.subtract))
            dve.wait_ge(bn_rstd, 1)
            s.did(tt(bnp[:, 7:8], bnp[:, 6:7], bnp[:, 1:2], ALU.mult))
            s.settle()
            s.did(nc.vector.tensor_scalar(w2s[:, :], w2s[:, :], bnp[:, 7:8], None, ALU.mult))
            s.did(stt(bnp[:, 0:1], bnp[:, 0:1], bnp[:, 7:8], bnp[:, 2:3], ALU.mult, ALU.add))
            s.at(BN_STEPS)

            magnitudes(0)
            dve.wait_ge(pads_zeroed, PADS)
            prepare(0, lambda n: magnitudes(n + 1) if n < PIECES // W_SLOTS else None)
            dve.wait_ge(wmax_all, 1)
            s = Steps(dve, sig_step, 0, SIG_STEPS)
            s.did(nc.vector.tensor_scalar(sg[:, 1:2], sg[:, 1:2], 2.0 ** -100, 2.0 ** 100, ALU.max, ALU.min))
            s.settle()
            s.did(nc.vector.tensor_scalar(sg[:, 2:3].bitcast(U32), sg[:, 1:2].bitcast(U32), 0x7F800000, None,
                                          ALU.bitwise_and))
            s.settle()
            s.did(nc.vector.tensor_scalar(sg[:, 4:5], sg[:, 2:3], 2.0 ** -10, None, ALU.mult))
            s.settle()
            s.did(nc.vector.reciprocal(sg[:, 3:4], sg[:, 4:5]))
            s.settle()
            s.at(SIG_STEPS)

            def u_points(k, j, sl):
                A2, A3, g = Au[:, 2], Au[:, 3], taps_of(sl)

                def pt(i):
                    return Tu[:, sl % 2, 2 * i:2 * i + 2]

                s = Steps(dve, uv_step, k, UV_STEPS)
                dve.wait_ge(w_loaded[sl], 16 * (j + w_turns(sl) + 1))
                dve.wait_ge(t_free, k + 1)
                s.did(stt(A2, g[:, 2], 4.0, g[:, 0], ALU.mult, ALU.add))
                s.did(stt(A3, g[:, 3], 4.0, g[:, 1], ALU.mult, ALU.add))
                s.did(stt(pt(4), g[:, 3], -0.5, g[:, 2], ALU.mult, ALU.add))
                s.settle()
                s.did(stt(pt(2), A3, 2.0, A2, ALU.mult, ALU.add))
                s.did(stt(pt(3), A3, -2.0, A2, ALU.mult, ALU.add))
                s.did(stt(pt(4), pt(4), -0.5, g[:, 1], ALU.mult, ALU.add))
                s.settle()
                s.did(stt(pt(4), pt(4), -0.5, g[:, 0], ALU.mult, ALU.add))
                s.at(UV_STEPS)
                s.settle()

            def u_low(k, sl):
                g = taps_of(sl)
                hi = U[:, 0, :, ds(k, 1), :].rearrange("p u a n -> p u (a n)")
                lo = U[:, 1, :, ds(k, 1), :].rearrange("p u a n -> p u (a n)")
                dve.wait_ge(uhi_ready, k + 1)
                stt(lo[:, TU:TU + 2], g[:, 0], sg[:, 3:4], hi[:, TU:TU + 2], ALU.mult, ALU.subtract)
                stt(lo[:, TU + 2:], g[:, 3, 0:1], sg[:, 3:4], hi[:, TU + 2:], ALU.mult, ALU.subtract)
                stt(lo[:, 0:TU], Tu[:, sl % 2], sg[:, 3:4], hi[:, 0:TU], ALU.mult,
                    ALU.subtract).then_inc(t_free, 1)

            def u_pieces(first, j, pieces):
                for sl in range(pieces):
                    u_points(first + sl, j, sl)
                    if sl > 0:
                        u_low(first + sl - 1, sl - 1)
                u_low(first + pieces - 1, pieces - 1)
            dve.wait_ge(vlo_ready, 4)
            piece_loop(dve, u_pieces)

            def body(q, par):
                if is_first(q):
                    ln(1)
                    y_points(0, 0)
                    y_points(0, 1)
                    y_mid(0)
                    y_end(0)
                    prepare(1)
                    return
                if not is_last(q):
                    ln(q + 1)
                    v_head(q + 1, 0)
                    v_data(q + 1, 0)
                    v_head(q + 1, 1)
                    v_low(q + 1, 1 - par, 0)
                    v_data(q + 1, 1)
                shift_logits(q - 1, 0)
                if not is_last(q):
                    v_low(q + 1, 1 - par, 1)
                y_points(q, 0)
                if not is_last(q):
                    v_head(q + 1, 2)
                    v_data(q + 1, 2)
                normalise(q - 1, 0)
                if not is_last(q):
                    v_low(q + 1, 1 - par, 2)
                    v_head(q + 1, 3)
                    v_data(q + 1, 3)
                shift_logits(q - 1, 1)
                if not is_last(q):
                    v_low(q + 1, 1 - par, 3)
                normalise(q - 1, 1)
                y_points(q, 1)
                y_mid(q)
                a_low(q - 1)
                y_end(q)

            pair_loop(dve, body)
            q = PAIRS - 1
            for i in range(2):
                shift_logits(q, i)
                normalise(q, i)
            a_low(q)

        @block.tensor
        def _(pe):
            pe.wait_ge(par_loaded, 16 * 8)
            pe.wait_ge(bn_step, BN_STEPS)
            nc.tensor.transpose(pL[:, 0:TAPS], w2s[:, :], ident[0:TAPS, 0:TAPS]).then_inc(w2_turned, 1)
            nc.tensor.transpose(pL[0:1, P:P + TAPS], bnp[:, 0:1], ident[0:TAPS, 0:TAPS]).then_inc(w2_turned, 1)

            def turn_x(q, n):
                i, c = chunk(q, n)
                pe.wait_ge(xn_ready, 2 * q + i + 1)
                for h in range(2):
                    if not (is_first(q) and n == 0):
                        pe.wait_ge(xT_used, 8 * q + 2 * n + h - 1)
                    for t in range(3):
                        last = nc.tensor.transpose(pX[:, h, t * TT:(t + 1) * TT],
                                                   xa[:, i, 3 * h + t, c * P:(c + 1) * P], ident[0:TT, 0:TT])
                    last.then_inc(xT_ready, 1)

            def product(bank, par, k, g, piece, a, b, start, stop):
                c, d = piece // KS, ROWS[piece % KS] - KS // 2
                first, end = max(0, -d), min(SIDE, SIDE - d)
                v = V[:, par, b, k, c].rearrange("p i (r t) -> p i r t", t=VT)
                out = bank[:, 0:HALF].rearrange("p (i n) -> p i n", i=2)
                return nc.tensor.matmul(out[:, :, first * QT:end * QT], U[:, a, 2 * k + g, piece, :],
                                        v[:, :, first + d:end + d, g:g + QT], start=start, stop=stop)

            def terms(k, pieces):
                return [(g, piece, a, b) for piece in pieces for g in range(2) if 2 * k + g < UNITS
                        for a, b in ((0, 0), (0, 1), (1, 0))]

            def conv_half(q, par):
                pe.wait_ge(vlo_ready, 4 * q + 2)
                for k in range(4):
                    for n, term in enumerate(terms(k, range(KS))):
                        product(pM[:, k, :], par, k, *term, n == 0, False)

            def conv(q, par, k):
                if k == 0:
                    pe.wait_ge(vlo_ready, 4 * (q + 1))
                if k < 3:
                    after(pe, y_step, q * Y_STEPS - (2, 1, 0)[k])
                elif k == 4:
                    pe.wait_ge(m_copied, 2 * q + 1)
                elif k == 5:
                    pe.wait_ge(y_step, q * Y_STEPS + 2)
                elif k == 6:
                    pe.wait_ge(m_copied, 2 * q + 2)
                half_done = isinstance(q, int) and q == 1 and k < 4
                work_list = terms(k, range(KS if half_done else 0, PIECES))
                for n, term in enumerate(work_list):
                    last = product(pM[:, k % 4, :], par, k, *term, n == 0 and not half_done,
                                   n == len(work_list) - 1)
                last.then_inc(m_ready, 1)

            def logits(q, i):
                if i == 0:
                    pe.wait_ge(k1_ready, q + 1)
                if i == 1:
                    pe.wait_ge(sm_step, q * SM_STEPS + 3)
                L = pL[0:TT, 0:NT * TAPS]
                nc.tensor.matmul(L, ones[:, :], brow[:, :, :].rearrange("p t k -> p (t k)"),
                                 start=True, stop=False)
                for t in range(NT):
                    last = nc.tensor.matmul(L[:, t * TAPS:(t + 1) * TAPS],
                                            k1[:, (i * NT + t) * TT:(i * NT + t + 1) * TT], w2T[:, :],
                                            start=False, stop=(t == NT - 1))
                last.then_inc(logits_ready, 1)

            def turn_a(q, turned):
                for i in range(2):
                    pe.wait_ge(sm_step, q * SM_STEPS + (SM_STEPS // 2 + 3, SM_STEPS)[i])
                    if i == 1:
                        pe.wait_ge(xT_used, 8 * turned)
                    for h in range(2):
                        for t in range(3):
                            last = nc.tensor.transpose(a_bank(i, h)[0:EPAD, t * TT:(t + 1) * TT],
                                                       E[:, i, (3 * h + t) * TAPS:(3 * h + t) * TAPS + EPAD],
                                                       ident[0:TT, 0:TT])
                        last.then_inc(aT_ready, 1)

            for n in range(4):
                turn_x(0, n)
            pe.wait_ge(w2_ready, 2)

            def conv_pieces():
                pe.wait_ge(vlo_ready, 4)
                pe.wait_ge(xT_used, 8)
                for piece in range(PIECES):
                    pe.wait_ge(t_free, piece + 3)
                    for k in range(NP):
                        work_list = terms(k, [piece])
                        for n, term in enumerate(work_list):
                            last = product(m_bank(0, k), 0, k, *term, piece == 0 and n == 0,
                                           piece == PIECES - 1 and n == len(work_list) - 1)
                        if piece == PIECES - 1:
                            last.then_inc(m_ready, 1)

            def body(q, par):
                if is_first(q):
                    conv_pieces()
                    pe.wait_ge(y_step, Y_STEPS)
                    for n in range(4):
                        turn_x(1, n)
                    return
                if isinstance(q, int) and q == 1:
                    conv_half(q, par)
                conv(q, par, 0)
                if not is_last(q):
                    turn_x(q + 1, 0)
                logits(q - 1, 0)
                if not is_last(q):
                    turn_x(q + 1, 1)
                conv(q, par, 1)
                if not is_last(q):
                    turn_x(q + 1, 2)
                conv(q, par, 2)
                if not is_last(q):
                    turn_x(q + 1, 3)
                logits(q - 1, 1)
                for k in range(3, NP - 1):
                    conv(q, par, k)
                turn_a(q - 1, q + 1 if is_last(q) else q + 2)
                conv(q, par, NP - 1)
                pe.wait_ge(alo_ready, 4 * q)

            pair_loop(pe, body)
            logits(PAIRS - 1, 0)
            logits(PAIRS - 1, 1)
            turn_a(PAIRS - 1, PAIRS)


BLK = 3
R = KS // 2
EDGE = [w for w in range(SIDE) if w < R or w >= SIDE - R]
G0 = TT + SIDE * (TR - 1 - R - 1) + (SIDE - 1 - R)
GW = G0 + SIDE * (R - 1) + R + TT + TT
HHS = [(d, h) for d in (-1, 0, 1) for h in range(TR) if (d, h) not in ((-1, TR - 1), (1, 0))]
BI = IMGS // B
GROUPS = 2
GI = IMGS // GROUPS
BT = GI * NT
SLOT = 4
SBANKS = OBANKS = 4
SPREAD_BANKS = SIDE // SLOT
T_SUMS = 3
T_STEPS = T_SUMS + 2 * NT + 2


def spread_table():
    import numpy as np
    g = np.zeros((TAPS, len(EDGE) + 1, GW), np.float16)
    for v, w in enumerate([SIDE // 2] + EDGE):
        for ki in range(KS):
            for kj in range(KS):
                if 0 <= w + kj - R < SIDE:
                    g[ki * KS + kj, v, SIDE * ki + kj + G0] = 1
    return g


def attend_phase(nc, xt, xn_d, attn_d, spread_d, t_d, tn_d, mean, const_loads):
    with ExitStack() as ctx:
        def sb(name, shape, dt):
            return ctx.enter_context(nc.sbuf_tensor(name, shape, dt))

        def sem(name):
            return ctx.enter_context(nc.semaphore(name))

        G = sb("G", list(spread_d.shape), F16)
        aT = sb("aT", [TAPS, 2, GI * PIX], F16)
        A = sb("A", [TT, BLK, 2 * BT, TT], F16)
        xr = sb("xr", [TT, 2, NT, C], F32)
        xn = sb("xn", [TT, 2, NT, C], F32)
        X = sb("X", [TT, 2, NT, 2, C], F16)
        ts_ = sb("ts", [TT, 2, NT, C], F32)
        tn = sb("tn", [TT, 2, NT, C], F32)
        acc = sb("acc", [TT, B, NT, C], F32)
        ones = sb("ones2", [TT, 1], F32)
        st = sb("st2", [TT, NT, 6], F32)
        mv = sb("mv2", [TT, NT, 2], F32)
        ve = sb("ve2", [TT, NT], F32)
        rstd = sb("rstd2", [TT, 2, NT], F32)
        nmean = sb("nmean", [TT, NT], F32)
        shift = sb("shift", [TT, 2, NT], F32)
        mhalf = sb("mhalf2", [TT, NT], F32)
        pS = ctx.enter_context(nc.psum_tensor("pS", [P, SBANKS, 512], F32))
        pO = ctx.enter_context(nc.psum_tensor("pO", [P, OBANKS, 512], F32))

        g_loaded = sem("g_loaded")
        c_loaded = sem("c_loaded")
        at_loaded = sem("at_loaded")
        xr_loaded = [sem(f"xr_loaded{s}") for s in range(2)]
        xn_loaded = [sem(f"xn_loaded{s}") for s in range(2)]
        a_zeroed = sem("a_zeroed")
        spread = sem("spread")
        a_by_act = sem("a_by_act")
        a_by_dve = sem("a_by_dve")
        xhi_ready = sem("xhi_ready")
        xlo_ready = sem("xlo_ready")
        o_ready = sem("o_ready")
        t_step = sem("t_step")
        rstd_step = sem("rstd_step")
        tn_ready = sem("tn_ready")
        acc_step = sem("acc_step")
        sums_ready = sem("sums_ready")
        mean_ready = sem("mean_ready")
        t_stored = [sem(f"t_stored{s}") for s in range(2)]
        tn_stored = [sem(f"tn_stored{s}") for s in range(2)]
        ITEMS = [(d, h, g) for d, h in HHS for g in range(SPREAD_BANKS)]
        NU = len(ITEMS)
        SUM_COLS = SLOT * 2 * BT
        LATE = 2
        SUMS = B + LATE

        def summed(n):
            return (BI - 1) * (n // BI) + max(n % BI, 1)


        block = ctx.enter_context(nc.Block())

        @block.sync
        def _(sp):
            def load_xn(n):
                if n >= 2:
                    sp.wait_ge(xlo_ready, n - 1)
                src = xn_d[n * PIX:(n + 1) * PIX, :].rearrange("(t p) c -> p t c", p=TT)
                sp.dma_start(xn[:, n % 2], src).then_inc(xn_loaded[n % 2], 16)

            def load_x(n):
                if n >= 2:
                    sp.wait_ge(t_step, (n - 2) * T_STEPS + T_SUMS)
                src = xt[n * PIX:(n + 1) * PIX, :].rearrange("(t p) c -> p t c", p=TT)
                sp.dma_start(xr[:, n % 2], src).then_inc(xr_loaded[n % 2], 16)

            def load_attn(g):
                if g > 0:
                    sp.wait_ge(spread, NU * g)
                sp.dma_start(aT[:, :, :], attn_d[:, :, g * GI * PIX:(g + 1) * GI * PIX]).then_inc(at_loaded, 16)

            load_attn(0)
            for load in (load_xn, load_x):
                for n in range(2):
                    load(n)
            for dst, src in const_loads:
                sp.dma_start(dst, src).then_inc(c_loaded, 16)
            for n in range(IMGS):
                if n % GI == 0 and n // GI + 1 < GROUPS:
                    load_attn(n // GI + 1)
                if n + 2 < IMGS:
                    load_xn(n + 2)
                    load_x(n + 2)
            sp.wait_ge(c_loaded, 16 * len(const_loads))
            for s in range(2):
                sp.wait_ge(t_stored[s], 16 * IMGS // 2)
                sp.wait_ge(tn_stored[s], 16 * IMGS // 2)

        @block.gpsimd
        def _(pool):
            nc.gpsimd.memset(A[:, 0, :, (TR - 1) * SIDE:TR * SIDE], 0.0).then_inc(a_zeroed, 1)
            nc.gpsimd.memset(A[:, 2, :, 0:SIDE], 0.0).then_inc(a_zeroed, 1)
            nc.gpsimd.memset(mhalf[:, :], -0.5).then_inc(a_zeroed, 1)
            nc.gpsimd.memset(ones[:, :], 1.0).then_inc(a_zeroed, 1)
            pool.wait_ge(a_zeroed, 4)

            def scale(n):
                if n >= 2:
                    pool.wait_ge(tn_ready, n - 1)
                pool.wait_ge(t_step, (n + 1) * T_STEPS)
                nc.gpsimd.tensor_tensor(rstd[:, n % 2], ve[:, :], mhalf[:, :], ALU.pow).then_inc(rstd_step, 1)
                pool.wait_ge(rstd_step, 2 * n + 1)
                nc.gpsimd.tensor_tensor(shift[:, n % 2], nmean[:, :], rstd[:, n % 2],
                                        ALU.mult).then_inc(rstd_step, 1)

            def accumulate(n):
                after(pool, acc_step, summed(n) - 1)
                pool.wait_ge(tn_ready, n + 1)
                a = acc[:, n // BI]
                first = tn[:, (n - 1) % 2] if n % BI == 1 else a
                nc.gpsimd.tensor_tensor(a, first, tn[:, n % 2], ALU.add).then_inc(acc_step, 1)

            for n in range(IMGS):
                scale(n)
                if n % BI != 1 and 0 < n <= IMGS - LATE:
                    accumulate(n - 1)

        def spread_out(eng, copy, g, parity, done, between):
            if g == 0:
                eng.wait_ge(a_zeroed, 4)
            else:
                eng.wait_ge(o_ready, 3 * GI * g)
            for u in range(parity, NU, 2):
                if g == 0 and u // 2 == NU // 4:
                    between(0)
                d, h, k = ITEMS[u]
                eng.wait_ge(spread, NU * g + u + 1)
                at = h * SIDE + k * SLOT
                copy(A[:, d + 1, :, at:at + SLOT],
                     pS[0:TT, u % SBANKS, 0:SLOT * 2 * BT].rearrange("p (w n) -> p n w", w=SLOT)).then_inc(done, 1)

        @block.scalar
        def _(act):
            act.dma_start(G[:, :, :], spread_d).then_inc(g_loaded, 16)

            def x_high(n):
                act.wait_ge(xn_loaded[n % 2], 16 * (n // 2 + 1))
                if n >= 2:
                    act.wait_ge(o_ready, 3 * (n - 1))
                nc.scalar.copy(X[:, n % 2, :, 0, :], xn[:, n % 2]).then_inc(xhi_ready, 1)

            def normalise(n):
                act.wait_ge(rstd_step, 2 * (n + 1))
                if n >= 2:
                    act.wait_ge(tn_stored[n % 2], 16 * (n // 2))
                    act.wait_ge(acc_step, summed(n - 2))
                for t in range(NT):
                    last = nc.scalar.activation(tn[:, n % 2, t, :], ts_[:, n % 2, t, :], ACT.Identity,
                                                bias=shift[:, n % 2, t:t + 1],
                                                scale=rstd[:, n % 2, t:t + 1])
                last.then_inc(tn_ready, 1)

            def store(n):
                rows = slice(n * PIX, (n + 1) * PIX)
                act.dma_start(t_d[rows, :].rearrange("(t p) c -> p t c", p=TT),
                              ts_[:, n % 2]).then_inc(t_stored[n % 2], 16)
                act.wait_ge(tn_ready, n + 1)
                act.dma_start(tn_d[rows, :].rearrange("(t p) c -> p t c", p=TT),
                              tn[:, n % 2]).then_inc(tn_stored[n % 2], 16)

            for n in range(IMGS):
                if n % GI == 0:
                    spread_out(act, nc.scalar.copy, n // GI, 0, a_by_act, x_high)
                    x_high(n + 1)
                if (n + 1) % GI > 0 and n + 2 < IMGS:
                    x_high(n + 2)
                if n > 0:
                    normalise(n - 1)
                    store(n - 1)
            normalise(IMGS - 1)
            store(IMGS - 1)

        @block.vector
        def _(dve):
            def x_low(n):
                dve.wait_ge(xhi_ready, n + 1)
                nc.vector.tensor_tensor(X[:, n % 2, :, 1, :], xn[:, n % 2], X[:, n % 2, :, 0, :],
                                        ALU.subtract).then_inc(xlo_ready, 1)

            def sums(n):
                s = Steps(dve, t_step, n, T_STEPS)
                dve.wait_ge(xr_loaded[n % 2], 16 * (n // 2 + 1))
                if n >= 2:
                    dve.wait_ge(t_stored[n % 2], 16 * (n // 2))
                    dve.wait_ge(tn_ready, n - 1)
                for u in range(3):
                    dve.wait_ge(o_ready, 3 * n + u + 1)
                    s.did(nc.vector.scalar_tensor_tensor(
                        ts_[:, n % 2, 2 * u:2 * u + 2, :].rearrange("p t c -> p (t c)"),
                        pO[0:TT, (3 * n + u) % OBANKS, :], 1.0 / ATT_SCALE,
                        xr[:, n % 2, 2 * u:2 * u + 2, :].rearrange("p t c -> p (t c)"), ALU.mult, ALU.add))
                s.at(T_SUMS)

            def statistics(n):
                s = Steps(dve, t_step, n, T_STEPS, T_SUMS)
                s.settle()
                for t in range(NT):
                    s.did(nc.vector.bn_stats(st[:, t, :], ts_[:, n % 2, t, :]))
                s.settle()
                for t in range(NT):
                    s.did(nc.vector.bn_aggr(mv[:, t, :], st[:, t, :]))
                s.settle()
                after(dve, rstd_step, 2 * n)
                s.did(nc.vector.tensor_scalar(ve[:, :], mv[:, :, 1], 1e-5, None, ALU.add))
                s.did(nc.vector.tensor_scalar(nmean[:, :], mv[:, :, 0], -1.0, None, ALU.mult))
                s.at(T_STEPS)

            for n in range(IMGS):
                if n % GI == 0:
                    spread_out(dve, nc.vector.tensor_copy, n // GI, 1, a_by_dve, x_low)
                    if n > 0:
                        statistics(n - 1)
                    x_low(n + 1)
                sums(n)
                if (n + 1) % GI > 0:
                    statistics(n)
                    if n + 2 < IMGS:
                        x_low(n + 2)
            statistics(IMGS - 1)
            dve.wait_ge(sums_ready, 1)
            total = pS[:, 0, SUM_COLS:SUM_COLS + CC * SUMS].rearrange("p (c e) -> p c e", c=CC)
            means = mean[:, :].rearrange("p (c e) -> p c e", c=CC)
            nc.vector.tensor_scalar(means, total[:, :, 0:B], 1.0 / SB, None, ALU.mult).then_inc(mean_ready, 1)
            for e in range(LATE):
                dve.wait_ge(mean_ready, e + 1)
                nc.vector.scalar_tensor_tensor(means[:, :, B - 1:B], total[:, :, B + e:B + e + 1], 1.0 / SB,
                                               means[:, :, B - 1:B], ALU.mult, ALU.add).then_inc(mean_ready, 1)
            dve.wait_ge(mean_ready, LATE + 1)

        @block.tensor
        def _(pe):
            pe.wait_ge(g_loaded, 16)

            def spread_taps(g):
                pe.wait_ge(at_loaded, 16 * (g + 1))
                a = aT[:, :, :].rearrange("p a (n i) -> p (a n) i", i=TT)
                for u, (d, h, k) in enumerate(ITEMS):
                    after(pe, a_by_dve if u % 2 else a_by_act, (NU * g + u - SBANKS) // 2 + 1)
                    for w in range(k * SLOT, (k + 1) * SLOT):
                        at = TT * d - SIDE * (h - R) - (w - R) + G0
                        v = 1 + EDGE.index(w) if w in EDGE else 0
                        o = (w % SLOT) * 2 * BT
                        last = nc.tensor.matmul(pS[0:TT, u % SBANKS, o:o + 2 * BT],
                                                G[:, v, at:at + TT], a[:, :, h * SIDE + w],
                                                start=True, stop=True)
                    last.then_inc(spread, 1)
                pe.wait_ge(a_by_act, (NU // 2) * (g + 1))
                pe.wait_ge(a_by_dve, (NU // 2) * (g + 1))

            def attend(n):
                pe.wait_ge(xlo_ready, n + 1)
                for u in range(3):
                    e = 3 * n + u - OBANKS
                    if e >= 0:
                        pe.wait_ge(t_step, e // 3 * T_STEPS + e % 3 + 1)
                    for t in (2 * u, 2 * u + 1):
                        terms = [(d, a, x) for d in (-1, 0, 1) if 0 <= t + d < NT
                                 for a, x in ((0, 0), (0, 1), (1, 0))]
                        for k, (d, a, x) in enumerate(terms):
                            last = nc.tensor.matmul(
                                pO[0:TT, (3 * n + u) % OBANKS, (t % 2) * C:(t % 2 + 1) * C],
                                A[:, d + 1, a * BT + (n % GI) * NT + t, :], X[:, n % 2, t + d, x, :],
                                start=(k == 0), stop=(k == len(terms) - 1))
                    last.then_inc(o_ready, 1)

            def sum_tokens(e, c):
                at = SUM_COLS + c * SUMS + e
                for t in range(NT):
                    tokens = acc[:, e, t] if e < B else tn[:, (IMGS - LATE + e - B) % 2, t]
                    last = nc.tensor.matmul(pS[:, 0, at:at + 1], tokens[:, c * P:(c + 1) * P],
                                            ones[:, :], start=(t == 0), stop=(t == NT - 1))
                return last

            for n in range(IMGS):
                if n % GI == 0:
                    spread_taps(n // GI)
                attend(n)
                if n > BI and n % BI >= BI - CC:
                    pe.wait_ge(acc_step, summed(n // BI * BI - 1))
                    sum_tokens(n // BI - 1, n % BI - (BI - CC))
            pe.wait_ge(acc_step, summed(IMGS - LATE - 1))
            for c in range(CC):
                sum_tokens(B - 1, c)
            for e in range(LATE):
                pe.wait_ge(tn_ready, IMGS - LATE + e + 1)
                for c in range(CC):
                    last = sum_tokens(B + e, c)
            last.then_inc(sums_ready, 1)


EXPERTS, TOPK, FH = 8, 2, 512
FB = FH // P
CAPACITY = float(-(-N * 5 // (4 * EXPERTS)))
CT = 3
CN = CT * P
CHUNKS = SB // CN
JB = TOPK * FB
R_STEPS = 21
Z_VE = 3 * CT + 1
Z_ALL = 5 * CT + 1


def ffn_phase(nc, mean, consts, t_d, tn_d, ew1, eb1, ew2, eb2, out):
    ident, wrs, brs, gam, bet = consts
    with ExitStack() as ctx:
        def sb(name, shape, dt):
            return ctx.enter_context(nc.sbuf_tensor(name, shape, dt))

        def sem(name):
            return ctx.enter_context(nc.semaphore(name))

        ones = sb("ones3", [P, P], F32)
        r = sb("r", [B, 8, EXPERTS], F32)
        rc = sb("rc", [B, 8], F32)
        idx = sb("idx", [B, EXPERTS], U32)
        wv = sb("wv", [B, TOPK], F32)
        irow = sb("irow", [1, B * TOPK], U32)
        wdiag = sb("wdiag", [B, B, TOPK], F32)
        wbc = sb("wbc", [P, B * TOPK], F32)
        w1r = sb("w1r", [P, TOPK, CC, FH], F32)
        w2r = sb("w2r", [P, TOPK, FB, C], F32)
        b1r = sb("b1r", [P, TOPK, FB], F32)
        b2r = sb("b2r", [P, TOPK, C], F32)
        w1h = sb("w1h", [P, TOPK, CC, FH], F32R)
        w1l = sb("w1l", [P, TOPK, CC, FH], F32R)
        w2h = sb("w2h", [P, TOPK, FB, C], F32R)
        w2l = sb("w2l", [P, TOPK, FB, C], F32R)
        b1c = sb("b1c", [P, TOPK, FB], F32)
        b2c = sb("b2c", [P, 2, C], F32)
        tk = sb("tk", [P, 2, CT, C], F32)
        tnk = sb("tnk", [P, 2, CT, C], F32)
        tb = sb("tb", [P, 2, CT, C], F32)
        tnb = sb("tnb", [P, 2, CT, C], F32)
        xh = sb("xh", [P, 2, CC, CN], F32R)
        xl = sb("xl", [P, 2, CC, CN], F32R)
        gf = sb("gf", [P, 2, CN], F32)
        gh = sb("gh", [P, 2, JB, CN], F32R)
        gl = sb("gl", [P, 2, JB, CN], F32R)
        z = sb("z", [P, CT, C], F32)
        o = sb("o", [P, 2, CT, C], F32)
        spare = sb("spare3", [1, 1], F32)
        st = sb("st3", [P, CT, 6], F32)
        mv = sb("mv3", [P, CT, 2], F32)
        ve = sb("ve3", [P, CT], F32)
        rstd = sb("rstd3", [P, CT], F32)
        mhalf = sb("mhalf3", [P, CT], F32)
        pT = ctx.enter_context(nc.psum_tensor("pT", [P, CC, 512], F32))
        pH = ctx.enter_context(nc.psum_tensor("pH", [P, 4, 512], F32))
        pY = ctx.enter_context(nc.psum_tensor("pY", [P, 2, 512], F32))

        c_set = sem("c_set")
        r_pe = sem("r_pe")
        r_step = sem("r_step")
        r_exp = sem("r_exp")
        row_loaded = sem("row_loaded")
        w1_loaded = [sem(f"w1_loaded{k}") for k in range(TOPK)]
        b_loaded = sem("b_loaded")
        w2_loaded = sem("w2_loaded")
        w1hi_ready = sem("w1hi_ready")
        w2hi_ready = sem("w2hi_ready")
        w1_step = sem("w1_step")
        w2_step = sem("w2_step")
        bias_step = sem("bias_step")
        tk_loaded = [sem(f"tk_loaded{s}") for s in range(2)]
        tnk_loaded = [sem(f"tnk_loaded{s}") for s in range(2)]
        x_turned = sem("x_turned")
        xh_ready = sem("xh_ready")
        xl_ready = sem("xl_ready")
        h_ready = sem("h_ready")
        gelu_done = sem("gelu_done")
        g_step = sem("g_step")
        y_ready = sem("y_ready3")
        bias_added = sem("bias_added")
        z_step = sem("z_step")
        rstd_ready = sem("rstd_ready3")
        out_stored = [sem(f"out_stored{s}") for s in range(2)]

        block = ctx.enter_context(nc.Block())

        @block.sync
        def _(sp):
            def load_chunk(b, m):
                n, s = CHUNKS * b + m, m % 2
                if not (is_first(b) and m < 2):
                    sp.wait_ge(x_turned, 2 * (n - 1))
                    sp.wait_ge(bias_added, 2 * (n - 1))
                rows = ds(n * CN, CN)
                sp.dma_start(tnk[:, s], tn_d[rows, :].rearrange("(t p) c -> p t c", p=P)).then_inc(tnk_loaded[s], 16)
                sp.dma_start(tk[:, s], t_d[rows, :].rearrange("(t p) c -> p t c", p=P)).then_inc(tk_loaded[s], 16)

            def store_chunk(b, m):
                n, s = CHUNKS * b + m, m % 2
                sp.wait_ge(z_step, (n + 1) * Z_ALL)
                sp.dma_start(out[ds(n * CN, CN), :].rearrange("(t p) c -> p t c", p=P),
                             o[:, s]).then_inc(out_stored[s], 16)

            def load_experts(b):
                if not is_first(b):
                    sp.wait_ge(row_loaded, 16 * (B - 1))
                    sp.wait_ge(w2_step, 2 * b)
                chosen = [sp.value_load(idx[0:1, k:k + 1] if is_first(b) else irow[0:1, ds(TOPK * b + k, 1)],
                                        min_val=0, max_val=EXPERTS - 1) for k in range(TOPK)]
                for k, e in enumerate(chosen):
                    sp.dma_start(w1r[:, k], ew1[ds(e, 1)].rearrange("e (c p) f -> p (e c) f", p=P)
                                 ).then_inc(w1_loaded[k], 16)
                for k, e in enumerate(chosen):
                    sp.dma_start(b1r[:, k], ew_b(eb1, e)).then_inc(b_loaded, 16)
                    sp.dma_start(b2r[:, k], eb2[ds(e, 1), :].broadcast_to([P, C])).then_inc(b_loaded, 16)
                for k, e in enumerate(chosen):
                    sp.dma_start(w2r[:, k], ew2[ds(e, 1)].rearrange("e (f p) c -> p (e f) c", p=P)
                                 ).then_inc(w2_loaded, 16)

            def ew_b(eb1, e):
                return eb1[ds(e, 1)].rearrange("e p f -> (e p) f")

            load_chunk(0, 0)
            load_chunk(0, 1)
            sp.wait_ge(r_step, 16)
            load_experts(0)
            for b in range(1, B):
                sp.dma_start(irow[0:1, TOPK * b:TOPK * (b + 1)], idx[b:b + 1, 0:TOPK]).then_inc(row_loaded, 16)
            load_chunk(0, 2)

            def body(b):
                for m in range(CHUNKS):
                    if later(b, m, 3, CHUNKS):
                        load_chunk(*later(b, m, 3, CHUNKS))
                    if m == 1 and later(b, m, CHUNKS, CHUNKS):
                        load_experts(b + 1)
                    store_chunk(b, m)
            batch_loop(sp, body)
            for s in range(2):
                sp.wait_ge(out_stored[s], 16 * B * CHUNKS // 2)

        @block.gpsimd
        def _(pool):
            nc.gpsimd.memset(ones[:, :], 1.0).then_inc(c_set, 1)
            nc.gpsimd.memset(mhalf[:, :], -0.5).then_inc(c_set, 1)
            pool.wait_ge(c_set, 2)

            def add_bias(b, m):
                n, s = CHUNKS * b + m, m % 2
                if m == 0:
                    pool.wait_ge(bias_step, 3 * (b + 1))
                pool.wait_ge(tnk_loaded[s], 16 * (CHUNKS // 2 * b + m // 2 + 1))
                pool.wait_ge(tk_loaded[s], 16 * (CHUNKS // 2 * b + m // 2 + 1))
                if not (is_first(b) and m < 2):
                    pool.wait_ge(z_step, (n - 1) * Z_ALL)
                nc.gpsimd.tensor_tensor(tnb[:, s], tnk[:, s], b2c[:, 1:2, :].broadcast_to([P, CT, C]),
                                        ALU.add).then_inc(bias_added, 1)
                nc.gpsimd.tensor_tensor(tb[:, s], tk[:, s], bet[:, None, :].broadcast_to([P, CT, C]),
                                        ALU.add).then_inc(bias_added, 1)

            def rsqrt(b, m):
                n = CHUNKS * b + m
                pool.wait_ge(z_step, n * Z_ALL + Z_VE)
                nc.gpsimd.tensor_tensor(rstd[:, :], ve[:, :], mhalf[:, :], ALU.pow).then_inc(rstd_ready, 1)

            add_bias(0, 0)

            def body(b):
                for m in range(CHUNKS):
                    if later(b, m, 1, CHUNKS):
                        add_bias(*later(b, m, 1, CHUNKS))
                    rsqrt(b, m)
            batch_loop(pool, body)

        @block.scalar
        def _(act):
            for k in range(3):
                act.wait_ge(r_step, (2, 11, 17)[k])
                if k < 2:
                    nc.scalar.activation(r[:, 2 * k + 1, :], r[:, 2 * k, :], ACT.Exp).then_inc(r_exp, 1)
                else:
                    nc.scalar.activation(rc[:, 5:6], rc[:, 4:5], ACT.Exp).then_inc(r_exp, 1)

            def split_w1(b):
                if not is_first(b):
                    act.wait_ge(h_ready, JB * CHUNKS * b)
                for k in range(TOPK):
                    act.wait_ge(w1_loaded[k], 16 * (b + 1))
                    nc.scalar.copy(w1h[:, k], w1r[:, k]).then_inc(w1hi_ready, 1)

            def split_w2(b):
                act.wait_ge(w2_loaded, 32 * (b + 1))
                if not is_first(b):
                    act.wait_ge(y_ready, CT * CHUNKS * b)
                for k in range(TOPK):
                    nc.scalar.activation(w2h[:, k], w2r[:, k], ACT.Copy,
                                         scale=wbc[:, ds(TOPK * b + k, 1)]).then_inc(w2hi_ready, 1)

            def take_x(b, m):
                n, s = CHUNKS * b + m, m % 2
                act.wait_ge(x_turned, 2 * (n + 1))
                if not (is_first(b) and m < 2):
                    act.wait_ge(h_ready, JB * (n - 1))
                nc.scalar.copy(xh[:, s], pT[:, :, 0:CN]).then_inc(xh_ready, 1)

            def gelus(b, m):
                n, s = CHUNKS * b + m, m % 2
                if not (is_first(b) and m < 2):
                    act.wait_ge(y_ready, CT * (n - 1))
                for j in range(JB):
                    act.wait_ge(h_ready, JB * n + j + 1)
                    if not (is_first(b) and m == 0 and j < 2):
                        act.wait_ge(g_step, JB * n + j - 1)
                    for dst in (gf[:, j % 2, :], gh[:, s, j, :]):
                        last = nc.scalar.activation(dst, pH[:, j % 4, 0:CN], ACT.Gelu,
                                                    bias=b1c[:, j // FB, j % FB:j % FB + 1])
                    last.then_inc(gelu_done, 1)

            take_x(0, 0)
            split_w1(0)
            act.wait_ge(bias_step, 3)
            gelus(0, 0)
            take_x(0, 1)
            act.wait_ge(r_step, R_STEPS + 1)
            split_w2(0)

            def body(b):
                for m in range(CHUNKS):
                    if m == 0 and not is_first(b):
                        split_w2(b)
                    if later(b, m, 1, CHUNKS):
                        if m == CHUNKS - 1:
                            act.wait_ge(bias_step, 3 * (b + 2))
                        gelus(*later(b, m, 1, CHUNKS))
                    if later(b, m, 2, CHUNKS):
                        take_x(*later(b, m, 2, CHUNKS))
                    if m == CHUNKS - 2 and later(b, m, 2, CHUNKS):
                        split_w1(b + 1)
            batch_loop(act, body)

        @block.vector
        def _(dve):
            tt, stt = nc.vector.tensor_tensor, nc.vector.scalar_tensor_tensor
            s = Steps(dve, r_step, 0, R_STEPS)

            def do(ins):
                s.did(ins)
                s.settle()

            def softmax_shift(src, dst, col):
                do(nc.vector.tensor_reduce(rc[:, col:col + 1], src, AX.X, ALU.max))
                do(nc.vector.tensor_scalar(dst, src, rc[:, col:col + 1], None, ALU.subtract))

            def softmax_divide(src, dst, col):
                do(nc.vector.tensor_reduce(rc[:, col:col + 1], src, AX.X, ALU.add))
                do(nc.vector.reciprocal(rc[:, col:col + 1], rc[:, col:col + 1]))
                do(nc.vector.tensor_scalar(dst, src, rc[:, col:col + 1], None, ALU.mult))

            dve.wait_ge(r_pe, 1)
            softmax_shift(pT[0:B, 1, 0:EXPERTS], r[:, 0, :], 0)
            dve.wait_ge(r_exp, 1)
            softmax_divide(r[:, 1, :], r[:, 4, :], 1)
            dve.wait_ge(r_pe, 2)
            do(nc.vector.tensor_scalar(r[:, 5, :], pT[0:B, 0, 64:64 + EXPERTS], float(SB), None, ALU.mult))
            do(nc.vector.reciprocal(r[:, 5, :], r[:, 5, :]))
            do(nc.vector.tensor_scalar(r[:, 5, :], r[:, 5, :], CAPACITY, 1.0, ALU.mult, ALU.min))
            do(tt(r[:, 6, :], r[:, 5, :], r[:, 4, :], ALU.mult))
            softmax_shift(r[:, 6, :], r[:, 2, :], 2)
            dve.wait_ge(r_exp, 2)
            softmax_divide(r[:, 3, :], r[:, 7, :], 3)
            do(nc.vector.max(r[:, 0, :], r[:, 7, :]))
            do(nc.vector.max_index(idx[:, :], r[:, 0, :], r[:, 7, :]))
            do(tt(rc[:, 4:5], r[:, 0, 1:2], r[:, 0, 0:1], ALU.subtract))
            dve.wait_ge(r_exp, 3)
            do(nc.vector.tensor_scalar(rc[:, 6:7], rc[:, 5:6], 1.0, None, ALU.add))
            do(nc.vector.reciprocal(wv[:, 0:1], rc[:, 6:7]))
            do(tt(wv[:, 1:2], rc[:, 5:6], wv[:, 0:1], ALU.mult))
            do(tt(wdiag[:, :, :], ident[0:B, 0:B, None].broadcast_to([B, B, TOPK]),
                  wv[:, None, :].broadcast_to([B, B, TOPK]), ALU.mult))
            s.at(R_STEPS)
            dve.wait_ge(r_pe, 3)
            nc.vector.tensor_copy(wbc[:, :], pT[:, 1, 64:64 + TOPK * B]).then_inc(r_step, 1)
            dve.wait_ge(r_step, R_STEPS + 1)

            def split_w1(b):
                for k in range(TOPK):
                    dve.wait_ge(w1hi_ready, TOPK * b + k + 1)
                    tt(w1l[:, k], w1r[:, k], w1h[:, k].bitcast(F32), ALU.subtract).then_inc(w1_step, 1)
                s = Steps(dve, bias_step, b, 3)
                dve.wait_ge(b_loaded, 64 * (b + 1))
                if not is_first(b):
                    dve.wait_ge(bias_added, 2 * CHUNKS * b)
                    dve.wait_ge(gelu_done, JB * CHUNKS * b)
                s.did(nc.vector.tensor_copy(b1c[:, :, :], b1r[:, :, :]))
                s.did(nc.vector.tensor_scalar(b2c[:, 0, :], b2r[:, 0, :], wbc[:, ds(TOPK * b, 1)], None,
                                              ALU.mult))
                s.settle()
                s.did(stt(b2c[:, 1, :], b2r[:, 1, :], wbc[:, ds(TOPK * b + 1, 1)], b2c[:, 0, :],
                          ALU.mult, ALU.add))

            def split_w2(b):
                for k in range(TOPK):
                    dve.wait_ge(w2hi_ready, 2 * b + k + 1)
                    stt(w2l[:, k], w2r[:, k], wbc[:, ds(TOPK * b + k, 1)], w2h[:, k].bitcast(F32),
                        ALU.mult, ALU.subtract).then_inc(w2_step, 1)

            def take_x(b, m):
                n, sl = CHUNKS * b + m, m % 2
                dve.wait_ge(xh_ready, n + 1)
                tt(xl[:, sl], pT[:, :, 0:CN], xh[:, sl].bitcast(F32), ALU.subtract).then_inc(xl_ready, 1)

            def split_hidden(b, m, blocks):
                n, sl = CHUNKS * b + m, m % 2
                for j in blocks:
                    dve.wait_ge(gelu_done, JB * n + j + 1)
                    tt(gl[:, sl, j, :], gf[:, j % 2, :], gh[:, sl, j, :].bitcast(F32),
                       ALU.subtract).then_inc(g_step, 1)

            def sum_up(b, m):
                n, sl = CHUNKS * b + m, m % 2
                s = Steps(dve, z_step, n, Z_ALL)
                s.settle()
                dve.wait_ge(bias_added, 2 * (n + 1))

                def add(t):
                    dve.wait_ge(y_ready, CT * n + t + 1)
                    s.did(tt(z[:, t, :], pY[:, (CT * m + t) % 2, 0:C], tnb[:, sl, t, :], ALU.add))

                def stats(t):
                    s.did(nc.vector.bn_stats(st[:, t, :], z[:, t, :]))

                add(0)
                for t in range(1, CT):
                    add(t)
                    s.settle()
                    stats(t - 1)
                stats(CT - 1)
                s.settle()
                carry(nc, spare[0:1, 0:1])
                for t in range(CT):
                    s.did(nc.vector.bn_aggr(mv[:, t, :], st[:, t, :]))
                s.settle()
                s.did(nc.vector.tensor_scalar(ve[:, :], mv[:, :, 1], 1e-5, None, ALU.add))
                s.at(Z_VE)

            def finish(b, m):
                n, sl = CHUNKS * b + m, m % 2
                s = Steps(dve, z_step, n, Z_ALL, Z_VE)
                for t in range(CT):
                    s.did(stt(z[:, t, :], z[:, t, :], mv[:, t, 0:1], gam[:, :], ALU.subtract, ALU.mult))
                s.settle()
                dve.wait_ge(rstd_ready, n + 1)
                if not (is_first(b) and m < 2):
                    dve.wait_ge(out_stored[sl], 16 * (CHUNKS // 2 * b + m // 2))
                for t in range(CT):
                    s.did(stt(o[:, sl, t, :], z[:, t, :], rstd[:, t:t + 1], tb[:, sl, t, :],
                              ALU.mult, ALU.add))
                s.at(Z_ALL)

            half = JB // 2
            take_x(0, 0)
            split_w1(0)
            split_hidden(0, 0, range(JB))
            take_x(0, 1)
            split_w2(0)

            def body(b):
                for m in range(CHUNKS):
                    if m == 0 and not is_first(b):
                        split_w2(b)
                    if later(b, m, 1, CHUNKS):
                        split_hidden(*later(b, m, 1, CHUNKS), range(half))
                    if m > 0:
                        finish(b, m - 1)
                    elif not is_first(b):
                        finish(b - 1, CHUNKS - 1)
                    if later(b, m, 1, CHUNKS):
                        split_hidden(*later(b, m, 1, CHUNKS), range(half, JB))
                    if later(b, m, 2, CHUNKS):
                        take_x(*later(b, m, 2, CHUNKS))
                    if m == CHUNKS - 2 and later(b, m, 2, CHUNKS):
                        split_w1(b + 1)
                    sum_up(b, m)
            batch_loop(dve, body)
            finish(B - 1, CHUNKS - 1)

        @block.tensor
        def _(pe):
            pe.wait_ge(c_set, 2)
            for c in range(CC):
                nc.tensor.matmul(pT[0:B, 1, 0:EXPERTS], mean[:, c * B:(c + 1) * B], wrs[:, c, :],
                                 start=(c == 0), stop=False)
            nc.tensor.matmul(pT[0:B, 1, 0:EXPERTS], ones[0:1, 0:B], brs[:, :],
                             start=False, stop=True).then_inc(r_pe, 1)
            pe.wait_ge(r_step, 5)
            nc.tensor.matmul(pT[0:B, 0, 64:64 + EXPERTS], ones[0:B, 0:B], r[:, 4, :],
                             start=True, stop=True).then_inc(r_pe, 1)
            pe.wait_ge(r_step, R_STEPS)
            nc.tensor.matmul(pT[:, 1, 64:64 + TOPK * B], ones[0:B, :],
                             wdiag[:, :, :].rearrange("p b k -> p (b k)"),
                             start=True, stop=True).then_inc(r_pe, 1)
            pe.wait_ge(r_step, R_STEPS + 1)

            def turn_x(b, m):
                n, s = CHUNKS * b + m, m % 2
                pe.wait_ge(tnk_loaded[s], 16 * (CHUNKS // 2 * b + m // 2 + 1))
                after(pe, xl_ready, n)
                for c in range(CC):
                    for t in range(CT):
                        last = nc.tensor.transpose(pT[:, c, t * P:(t + 1) * P],
                                                   tnk[:, s, t, c * P:(c + 1) * P], ident[:, :])
                    last.then_inc(x_turned, 1)

            def layer1(b, m):
                n, s = CHUNKS * b + m, m % 2
                pe.wait_ge(xl_ready, n + 1)
                for j in range(JB):
                    if m == 0 and j % FB == 0:
                        pe.wait_ge(w1_step, TOPK * b + j // FB + 1)
                    if not (is_first(b) and m == 0 and j < 4):
                        pe.wait_ge(gelu_done, JB * n + j - 3)
                    k, f = j // FB, j % FB
                    terms = [(c, w, x) for c in range(CC) for w, x in ((w1h, xh), (w1h, xl), (w1l, xh))]
                    for i, (c, w, x) in enumerate(terms):
                        last = nc.tensor.matmul(pH[:, j % 4, 0:CN], w[:, k, c, f * P:(f + 1) * P], x[:, s, c, :],
                                                start=(i == 0), stop=(i == len(terms) - 1))
                    last.then_inc(h_ready, 1)

            def layer2(b, m):
                n, s = CHUNKS * b + m, m % 2
                pe.wait_ge(g_step, JB * (n + 1))
                if m == 0:
                    pe.wait_ge(w2_step, 2 * (b + 1))
                for t in range(CT):
                    if not (is_first(b) and m == 0 and t < 2):
                        pe.wait_ge(z_step, (n - 1) * Z_ALL + 2 * t + 2 if t < 2 else n * Z_ALL + 1)
                    terms = [(j, g, w) for j in range(JB) for g, w in ((gh, w2h), (gh, w2l), (gl, w2h))]
                    for i, (j, g, w) in enumerate(terms):
                        last = nc.tensor.matmul(pY[:, (CT * m + t) % 2, 0:C], g[:, s, j, t * P:(t + 1) * P],
                                                w[:, j // FB, j % FB, :],
                                                start=(i == 0), stop=(i == len(terms) - 1))
                    last.then_inc(y_ready, 1)

            turn_x(0, 0)
            layer1(0, 0)
            turn_x(0, 1)

            def body(b):
                for m in range(CHUNKS):
                    if later(b, m, 1, CHUNKS):
                        layer1(*later(b, m, 1, CHUNKS))
                    if later(b, m, 2, CHUNKS):
                        turn_x(*later(b, m, 2, CHUNKS))
                    layer2(b, m)
            batch_loop(pe, body)


def program(nc, xt, w1p, b1, w2, b2, bn_gamma, bn_beta, bn_mean, bn_var, wr, br, ew1, eb1, ew2, eb2,
            gamma, beta, ident_d, spread_d, out):
    xn_d = nc.dram_tensor("xn_scratch", (N, C), F32, kind="Internal").ap()
    attn_d = nc.dram_tensor("attn_scratch", (TAPS, 2, N), F16, kind="Internal").ap()
    t_d = nc.dram_tensor("t_scratch", (N, C), F32, kind="Internal").ap()
    tn_d = nc.dram_tensor("tn_scratch", (N, C), F32, kind="Internal").ap()
    conv_phase(nc, xt, w1p, b1, w2, b2, bn_gamma, bn_beta, bn_mean, bn_var, ident_d, xn_d, attn_d)
    with ExitStack() as ctx:
        def sb(name, shape):
            return ctx.enter_context(nc.sbuf_tensor(name, shape, F32))

        mean = sb("mean", [P, CC * B])
        consts = ident, wrs, brs, gam, bet = (sb("ident3", [P, P]), sb("wrs", [P, CC, EXPERTS]),
                                              sb("brs", [1, EXPERTS]), sb("gam", [P, C]), sb("bet", [P, C]))
        const_loads = [(ident[:, :], ident_d), (wrs[:, :, :], wr.rearrange("(c p) e -> p c e", p=P)),
                       (brs[:, :], br), (gam[:, :], gamma.broadcast_to([P, C])),
                       (bet[:, :], beta.broadcast_to([P, C]))]
        attend_phase(nc, xt, xn_d, attn_d, spread_d, t_d, tn_d, mean, const_loads)
        ffn_phase(nc, mean, consts, t_d, tn_d, ew1, eb1, ew2, eb2, out)


def kernel(**inputs):
    import numpy as np
    import concourse.bacc as bacc
    from concourse.bass_utils import run_bass_kernel_spmd

    a = {k: np.asarray(v) for k, v in inputs.items()}

    def parity_order(x):
        return x.reshape(B, C, SIDE, 2, SIDE, 2).transpose(0, 3, 5, 2, 4, 1)

    w1 = a["L0_conv_w1"].reshape(CMID, CC, P, KS, KS)
    arrays = {
        "xt": parity_order(a["x"]).reshape(N, C),
        "w1p": w1.transpose(1, 3, 2, 4, 0)[:, ROWS].reshape(CC * KS, P, KS * CMID),
        "b1": a["L0_conv_b1"].reshape(CMID, 1),
        "w2": a["L0_conv_w2"].reshape(TAPS, CMID),
        "b2": a["L0_conv_b2"].reshape(TAPS, 1),
        "bn_gamma": a["L0_conv_bn_gamma"].reshape(TAPS, 1),
        "bn_beta": a["L0_conv_bn_beta"].reshape(TAPS, 1),
        "bn_mean": a["L0_conv_bn_mean"].reshape(TAPS, 1),
        "bn_var": a["L0_conv_bn_var"].reshape(TAPS, 1),
        "wr": a["L0_ffn_Wr"],
        "br": a["L0_ffn_br"].reshape(1, EXPERTS),
        "ew1": a["L0_ffn_W1"],
        "eb1": a["L0_ffn_b1"].reshape(EXPERTS, FB, P).transpose(0, 2, 1),
        "ew2": a["L0_ffn_W2"],
        "eb2": a["L0_ffn_b2"],
        "gamma": a["L0_ffn_gamma"].reshape(1, C),
        "beta": a["L0_ffn_beta"].reshape(1, C),
        "ident": np.eye(P, dtype=np.float32),
        "spread": spread_table(),
    }
    arrays = {k: np.ascontiguousarray(v) for k, v in arrays.items()}
    nc = bacc.Bacc("TRN2", target_bir_lowering=False, num_devices=1)
    args = [nc.dram_tensor(f"in_{k}", v.shape, mybir.dt.from_np(v.dtype), kind="ExternalInput").ap()
            for k, v in arrays.items()]
    out = nc.dram_tensor("out_0", (N, C), F32, kind="ExternalOutput").ap()
    program(nc, *args, out)
    r = run_bass_kernel_spmd(nc, [{f"in_{k}": v for k, v in arrays.items()}], core_ids=[0])
    y = np.asarray(r.results[0]["out_0"]).reshape(B, 2, 2, SIDE, SIDE, C)
    return np.ascontiguousarray(y.transpose(0, 5, 3, 1, 4, 2).reshape(B, C, HH, WW))
```
